# Optimizing a Trainium2 kernel written in Bass

```python
import numpy as np
import jax
import jax.numpy as jnp

def _softmax(x, axis=-1):
    return jax.nn.softmax(x, axis=axis)

def _gelu(x):
    return jax.nn.gelu(x, approximate=True)

def _silu(x):
    return jax.nn.silu(x)

def _sigmoid(x):
    return jax.nn.sigmoid(x)

def _layernorm(x, axis=-1, eps=1e-05):
    m = jnp.mean(x, axis=axis, keepdims=True)
    v = jnp.var(x, axis=axis, keepdims=True)
    return (x - m) / jnp.sqrt(v + eps)

def _scatter_add(tgt, idx, src, axis=0):
    return tgt.at[idx].add(src)

def _segment_sum(src, seg, n):
    return jax.ops.segment_sum(src, seg, n)
kernel_name = 'mk_sandwich_d2_jaxref_r8_bc4d65'

def setup_inputs(seed: int=0):
    np.random.seed(seed)
    _w = jnp.asarray

    def _L0_attn_setup():
        import jax, jax.numpy as jnp
        import numpy as np
        B, S, HID = (2, 512, 512)
        H, HKV, D = (32, 8, 128)
        G = H // HKV
        EPS = 1e-06

        def _reference_tuple_inner(hidden_states, Wq, bq, Wk, bk, Wv, bv, Wo, M, z):
            b, s, _ = hidden_states.shape
            q = (hidden_states @ Wq.T + bq).reshape(b, s, H, D)
            k = (hidden_states @ Wk.T + bk).reshape(b, s, HKV, D)
            v = (hidden_states @ Wv.T + bv).reshape(b, s, HKV, D)
            sig_q = jax.nn.elu(q) + 1.0
            sig_k = jax.nn.elu(k) + 1.0
            q_sel = sig_q[:, :, ::G, :]
            num = jnp.einsum('bshd,hde->bshe', q_sel, M)
            den = jnp.einsum('bshd,hd->bsh', q_sel, z)[..., None] + EPS
            retrieved = num / den
            out_heads = jnp.repeat(retrieved, G, axis=2)
            output = out_heads.reshape(b, s, H * D) @ Wo.T
            M_new = M + jnp.einsum('bshd,bshe->hde', sig_k, v)
            z_new = z + sig_k.sum(axis=(0, 1))
            return (output, M_new, z_new)
        key = jax.random.key(seed)
        ks = jax.random.split(key, 10)
        s = 0.02
        return {'hidden_states': jax.random.normal(ks[0], (B, S, HID), jnp.float32), 'Wq': jax.random.normal(ks[1], (H * D, HID), jnp.float32) * s, 'bq': jnp.zeros((H * D,), jnp.float32), 'Wk': jax.random.normal(ks[2], (HKV * D, HID), jnp.float32) * s, 'bk': jnp.zeros((HKV * D,), jnp.float32), 'Wv': jax.random.normal(ks[3], (HKV * D, HID), jnp.float32) * s, 'bv': jnp.zeros((HKV * D,), jnp.float32), 'Wo': jax.random.normal(ks[4], (HID, H * D), jnp.float32) * s, 'M': jax.random.normal(ks[5], (HKV, D, D), jnp.float32), 'z': jax.random.uniform(ks[6], (HKV, D), jnp.float32) * 100.0 + 1.0}
    _L0_attn_in = _L0_attn_setup()

    def _L0_ffn_setup():
        import jax, jax.numpy as jnp
        import numpy as np
        H, FF = (512, 1792)
        B, S = (4, 256)
        key = jax.random.key(seed)
        ks = jax.random.split(key, 7)
        x = jax.random.normal(ks[0], (B, S, H), dtype=jnp.float32)
        gate_t = jax.random.randint(ks[1], (FF, H), -1, 2, dtype=jnp.int32)
        up_t = jax.random.randint(ks[2], (FF, H), -1, 2, dtype=jnp.int32)
        down_t = jax.random.randint(ks[3], (H, FF), -1, 2, dtype=jnp.int32)
        gate_s = jax.random.uniform(ks[4], (FF,), jnp.float32, 0.01, 0.1)
        up_s = jax.random.uniform(ks[5], (FF,), jnp.float32, 0.01, 0.1)
        down_s = jax.random.uniform(ks[6], (H,), jnp.float32, 0.01, 0.1)
        return {'x': x, 'gate_t': gate_t, 'up_t': up_t, 'down_t': down_t, 'gate_s': gate_s, 'up_s': up_s, 'down_s': down_s}
    _L0_ffn_in = _L0_ffn_setup()

    def _L1_attn_setup():
        import jax, jax.numpy as jnp
        import numpy as np
        HIDDEN = 512
        HEAD_DIM = 128
        N_Q_HEADS = 32
        N_KV_HEADS = 8
        SLIDING_WINDOW = 128
        ROPE_THETA = 10000.0
        BATCH, SEQ = (1, 256)

        def _rope(t, pos):
            d = t.shape[-1]
            half = d // 2
            inv_freq = ROPE_THETA ** (-jnp.arange(half, dtype=jnp.float32) / half)
            ang = pos[:, None].astype(jnp.float32) * inv_freq[None, :]
            cos = jnp.cos(ang)[None, :, None, :]
            sin = jnp.sin(ang)[None, :, None, :]
            t1, t2 = (t[..., :half], t[..., half:])
            return jnp.concatenate([t1 * cos - t2 * sin, t1 * sin + t2 * cos], axis=-1)
        key = jax.random.key(seed)
        ks = jax.random.split(key, 5)
        w_scale = HIDDEN ** (-0.5)
        return {'x': jax.random.normal(ks[0], (BATCH, SEQ, HIDDEN), jnp.float32), 'wq': jax.random.normal(ks[1], (HIDDEN, N_Q_HEADS * HEAD_DIM), jnp.float32) * w_scale, 'wk': jax.random.normal(ks[2], (HIDDEN, N_KV_HEADS * HEAD_DIM), jnp.float32) * w_scale, 'wv': jax.random.normal(ks[3], (HIDDEN, N_KV_HEADS * HEAD_DIM), jnp.float32) * w_scale, 'wo': jax.random.normal(ks[4], (N_Q_HEADS * HEAD_DIM, HIDDEN), jnp.float32) * w_scale}
    _L1_attn_in = _L1_attn_setup()

    def _L1_ffn_setup():
        import jax, jax.numpy as jnp
        import numpy as np

        def _dequant(weight_q, scale, zp):
            N, K = weight_q.shape
            num_groups = scale.shape[1]
            gs = K // num_groups
            q = weight_q.astype(jnp.float32).reshape(N, num_groups, gs)
            w = (q - zp[:, :, None]) * scale[:, :, None]
            return w.reshape(N, K)
        key = jax.random.key(seed)
        k1, k2, k3, k4, k5 = jax.random.split(key, 5)
        B, S, K, N, G = (4, 256, 512, 512, 64)
        x = jax.random.normal(k1, (B, S, K), dtype=jnp.float32)
        weight_q = jax.random.randint(k2, (N, K), 0, 4, dtype=jnp.int32)
        scale = jax.random.uniform(k3, (N, K // G), dtype=jnp.float32) * 0.05 + 0.01
        zp = jax.random.uniform(k4, (N, K // G), dtype=jnp.float32) * 3.0
        bias = jax.random.normal(k5, (N,), dtype=jnp.float32)
        return {'x': x, 'weight_q': weight_q, 'scale': scale, 'zp': zp, 'bias': bias}
    _L1_ffn_in = _L1_ffn_setup()
    _d = {'L0_attn_hidden_states': _L0_attn_in['hidden_states'], 'L0_attn_Wq': _L0_attn_in['Wq'], 'L0_attn_bq': _L0_attn_in['bq'], 'L0_attn_Wk': _L0_attn_in['Wk'], 'L0_attn_bk': _L0_attn_in['bk'], 'L0_attn_Wv': _L0_attn_in['Wv'], 'L0_attn_bv': _L0_attn_in['bv'], 'L0_attn_Wo': _L0_attn_in['Wo'], 'L0_attn_M': _L0_attn_in['M'], 'L0_attn_z': _L0_attn_in['z'], 'L0_ffn_gate_t': _L0_ffn_in['gate_t'], 'L0_ffn_up_t': _L0_ffn_in['up_t'], 'L0_ffn_down_t': _L0_ffn_in['down_t'], 'L0_ffn_gate_s': _L0_ffn_in['gate_s'], 'L0_ffn_up_s': _L0_ffn_in['up_s'], 'L0_ffn_down_s': _L0_ffn_in['down_s'], 'L1_attn_wq': _L1_attn_in['wq'], 'L1_attn_wk': _L1_attn_in['wk'], 'L1_attn_wv': _L1_attn_in['wv'], 'L1_attn_wo': _L1_attn_in['wo'], 'L1_ffn_weight_q': _L1_ffn_in['weight_q'], 'L1_ffn_scale': _L1_ffn_in['scale'], 'L1_ffn_zp': _L1_ffn_in['zp'], 'L1_ffn_bias': _L1_ffn_in['bias']}
    _x0 = _d['L0_attn_hidden_states']
    _d['L0_attn_hidden_states'] = jax.random.normal(jax.random.fold_in(jax.random.key(seed), 1), (4, 256, 512), dtype=_x0.dtype)
    del _x0
    return _d

def reference(L0_attn_hidden_states, L0_attn_Wq, L0_attn_bq, L0_attn_Wk, L0_attn_bk, L0_attn_Wv, L0_attn_bv, L0_attn_Wo, L0_attn_M, L0_attn_z, L0_ffn_gate_t, L0_ffn_up_t, L0_ffn_down_t, L0_ffn_gate_s, L0_ffn_up_s, L0_ffn_down_s, L1_attn_wq, L1_attn_wk, L1_attn_wv, L1_attn_wo, L1_ffn_weight_q, L1_ffn_scale, L1_ffn_zp, L1_ffn_bias):

    def _L0_attn_ref(hidden_states, Wq, bq, Wk, bk, Wv, bv, Wo, M, z):
        import jax, jax.numpy as jnp
        import numpy as np
        B, S, HID = (2, 512, 512)
        H, HKV, D = (32, 8, 128)
        G = H // HKV
        EPS = 1e-06

        def _reference_tuple_inner(hidden_states, Wq, bq, Wk, bk, Wv, bv, Wo, M, z):
            b, s, _ = hidden_states.shape
            q = (hidden_states @ Wq.T + bq).reshape(b, s, H, D)
            k = (hidden_states @ Wk.T + bk).reshape(b, s, HKV, D)
            v = (hidden_states @ Wv.T + bv).reshape(b, s, HKV, D)
            sig_q = jax.nn.elu(q) + 1.0
            sig_k = jax.nn.elu(k) + 1.0
            q_sel = sig_q[:, :, ::G, :]
            num = jnp.einsum('bshd,hde->bshe', q_sel, M)
            den = jnp.einsum('bshd,hd->bsh', q_sel, z)[..., None] + EPS
            retrieved = num / den
            out_heads = jnp.repeat(retrieved, G, axis=2)
            output = out_heads.reshape(b, s, H * D) @ Wo.T
            M_new = M + jnp.einsum('bshd,bshe->hde', sig_k, v)
            z_new = z + sig_k.sum(axis=(0, 1))
            return (output, M_new, z_new)
        return _reference_tuple_inner(hidden_states, Wq, bq, Wk, bk, Wv, bv, Wo, M, z)[0]

    def _L0_ffn_ref(x, gate_t, up_t, down_t, gate_s, up_s, down_s):
        import jax, jax.numpy as jnp
        import numpy as np
        H, FF = (512, 1792)
        B, S = (4, 256)
        Bb, Ss, Hh = x.shape
        x_flat = x.reshape(Bb * Ss, Hh)
        gate_w = gate_t.astype(jnp.float32) * gate_s[:, None]
        up_w = up_t.astype(jnp.float32) * up_s[:, None]
        down_w = down_t.astype(jnp.float32) * down_s[:, None]
        gate_out = x_flat @ gate_w.T
        up_out = x_flat @ up_w.T
        hidden = jax.nn.silu(gate_out) * up_out
        out_flat = hidden @ down_w.T
        return out_flat.reshape(Bb, Ss, -1)

    def _L1_attn_ref(x, wq, wk, wv, wo):
        import jax, jax.numpy as jnp
        import numpy as np
        HIDDEN = 512
        HEAD_DIM = 128
        N_Q_HEADS = 32
        N_KV_HEADS = 8
        SLIDING_WINDOW = 128
        ROPE_THETA = 10000.0
        BATCH, SEQ = (1, 256)

        def _rope(t, pos):
            d = t.shape[-1]
            half = d // 2
            inv_freq = ROPE_THETA ** (-jnp.arange(half, dtype=jnp.float32) / half)
            ang = pos[:, None].astype(jnp.float32) * inv_freq[None, :]
            cos = jnp.cos(ang)[None, :, None, :]
            sin = jnp.sin(ang)[None, :, None, :]
            t1, t2 = (t[..., :half], t[..., half:])
            return jnp.concatenate([t1 * cos - t2 * sin, t1 * sin + t2 * cos], axis=-1)
        B, S, _ = x.shape
        G = N_Q_HEADS // N_KV_HEADS
        sm_scale = HEAD_DIM ** (-0.5)
        q = (x @ wq).reshape(B, S, N_Q_HEADS, HEAD_DIM)
        k = (x @ wk).reshape(B, S, N_KV_HEADS, HEAD_DIM)
        v = (x @ wv).reshape(B, S, N_KV_HEADS, HEAD_DIM)
        pos = jnp.arange(S)
        q = _rope(q, pos)
        k = _rope(k, pos)
        qg = q.reshape(B, S, N_KV_HEADS, G, HEAD_DIM)
        scores = jnp.einsum('bqhgd,bshd->bhgqs', qg, k) * sm_scale
        i = pos[:, None]
        j = pos[None, :]
        allowed = (j <= i) & (j > i - SLIDING_WINDOW)
        neg = jnp.finfo(scores.dtype).min
        scores = jnp.where(allowed[None, None, None], scores, neg)
        attn = jax.nn.softmax(scores, axis=-1)
        out = jnp.einsum('bhgqs,bshd->bqhgd', attn, v).reshape(B, S, N_Q_HEADS * HEAD_DIM)
        return out @ wo

    def _L1_ffn_ref(x, weight_q, scale, zp, bias):
        import jax, jax.numpy as jnp
        import numpy as np

        def _dequant(weight_q, scale, zp):
            N, K = weight_q.shape
            num_groups = scale.shape[1]
            gs = K // num_groups
            q = weight_q.astype(jnp.float32).reshape(N, num_groups, gs)
            w = (q - zp[:, :, None]) * scale[:, :, None]
            return w.reshape(N, K)
        w = _dequant(weight_q, scale, zp)
        out = jnp.einsum('bsk,nk->bsn', x, w)
        return out + bias
    x = L0_attn_hidden_states
    x = x + _layernorm(_L0_attn_ref(_layernorm(x, axis=-1), L0_attn_Wq, L0_attn_bq, L0_attn_Wk, L0_attn_bk, L0_attn_Wv, L0_attn_bv, L0_attn_Wo, L0_attn_M, L0_attn_z), axis=-1)
    x = x + _layernorm(_L0_ffn_ref(_layernorm(x, axis=-1), L0_ffn_gate_t, L0_ffn_up_t, L0_ffn_down_t, L0_ffn_gate_s, L0_ffn_up_s, L0_ffn_down_s), axis=-1)
    x = x + _layernorm(_L1_attn_ref(_layernorm(x, axis=-1), L1_attn_wq, L1_attn_wk, L1_attn_wv, L1_attn_wo), axis=-1)
    x = x + _layernorm(_L1_ffn_ref(_layernorm(x, axis=-1), L1_ffn_weight_q, L1_ffn_scale, L1_ffn_zp, L1_ffn_bias), axis=-1)
    return x

_drawn_inputs = setup_inputs


def setup_inputs(seed=0):
    import zlib

    import numpy as np

    out = dict(_drawn_inputs(seed))
    spreads = {'L0_attn_bq': (0.0, 0.1), 'L0_attn_bk': (0.0, 0.1), 'L0_attn_bv': (0.0, 0.1)}
    factors = {}
    for name, (base, spread) in spreads.items():
        noise = np.random.default_rng([zlib.crc32(name.encode()), seed]).standard_normal(out[name].shape)
        drawn = base * np.exp(spread * noise) if base else spread * noise
        out[name] = jnp.asarray(drawn.astype(out[name].dtype))
    for name, factor in factors.items():
        out[name] = (out[name] * factor).astype(out[name].dtype)
    return out
```

```python
from contextlib import ExitStack

import concourse.bass as bass
from concourse import mybir

F32 = mybir.dt.float32
F32R = mybir.dt.float32r
I32 = mybir.dt.int32
ALU = mybir.AluOpType
ACT = mybir.ActivationFunctionType

P = 128
T = 1024
TILES = T // P
HALF = T // 2
HID = 512
KT = HID // P
D = 128
KV = 8
G = 4
FF = 1792
FT = FF // P
SCALE = float(D) ** -0.5
LN_EPS = 1e-5
DEN_EPS = 1e-6
LOWEST = -3.4028234663852886e38

A_W = KT * D + D
F_W = 2 * KT * P + HID
QKV_W = KT * (G + 2) * D
WO_W = G * HID
DEN_STEP = 48


def build(nc, x_in, a_w, a_wo, a_z, a_bq, f_w, f_scale, down_s, l_qkv, l_wo, d_q, d_zp, d_scale, d_bias,
          rope, mask, ident_in, out):
    with ExitStack() as ctx:
        def sem(name):
            return ctx.enter_context(nc.semaphore(name))

        def sb(stack, name, shape, dt=F32):
            return stack.enter_context(nc.sbuf_tensor(name, shape, dt))

        x = sb(ctx, "x", [P, TILES, HID])
        acc = sb(ctx, "acc", [P, TILES, HID])
        xn_hi = sb(ctx, "xn_hi", [P, KT, T], F32R)
        xn_lo = sb(ctx, "xn_lo", [P, KT, T], F32R)
        ident = sb(ctx, "ident", [P, P])
        bq = sb(ctx, "bq", [P, KV])
        fsc = sb(ctx, "fsc", [P, 2, FT])
        down_row = sb(ctx, "down_row", [P, HID])
        bias_row = sb(ctx, "bias_row", [P, HID])
        cos_sin = sb(ctx, "cos_sin", [P, 2, 2, D // 2])
        masks = sb(ctx, "masks", [P, 2 * P])
        stats = sb(ctx, "stats", [P, TILES, 6])
        mean_var = sb(ctx, "mean_var", [P, TILES, 2])
        stats2 = sb(ctx, "stats2", [P, TILES, 6])
        mean_var2 = sb(ctx, "mean_var2", [P, TILES, 2])
        var_eps = sb(ctx, "var_eps", [P, 2, TILES])
        rstd = sb(ctx, "rstd", [P, 2, TILES])
        minus_half = sb(ctx, "minus_half", [P, 2])
        d_hi = sb(ctx, "d_hi", [P, KT, HID], F32R)
        d_lo = sb(ctx, "d_lo", [P, KT, HID], F32R)

        with ExitStack() as part:
            a_raw = sb(part, "a_raw", [P, 2, A_W])
            a_hi = sb(part, "a_hi", [P, 2, A_W], F32R)
            a_lo = sb(part, "a_lo", [P, 2, A_W], F32R)
            wo_raw = sb(part, "wo_raw", [P, 2, G, HID])
            wo_pair = sb(part, "wo_pair", [P, 2, HID])
            wo_sum = sb(part, "wo_sum", [P, HID])
            wos_hi = sb(part, "wos_hi", [P, 2, HID], F32R)
            wos_lo = sb(part, "wos_lo", [P, 2, HID], F32R)
            mw_hi = sb(part, "mw_hi", [P, 2, HID], F32R)
            mw_lo = sb(part, "mw_lo", [P, 2, HID], F32R)
            z_col = sb(part, "z_col", [P, KV])
            z_rep = sb(part, "z_rep", [P, KV, P])
            zeros = sb(part, "zeros", [P, P])
            expq = sb(part, "expq", [P, T])
            reluq = sb(part, "reluq", [P, T])
            sq = sb(part, "sq", [P, T])
            sq_hi = sb(part, "sq_hi", [P, T], F32R)
            sq_lo = sb(part, "sq_lo", [P, T], F32R)
            den_eps = sb(part, "den_eps", [P, TILES])
            rden = sb(part, "rden", [P, TILES])
        with ExitStack() as part:
            f_raw = sb(part, "f_raw", [P, 2, F_W], I32)
            f_hi = sb(part, "f_hi", [P, 2, F_W], F32R)
            f_lo = sb(part, "f_lo", [P, 2, F_W], F32R)
            silu = sb(part, "silu", [P, T])
            hid = sb(part, "hid", [P, 2, T])
            hid_hi = sb(part, "hid_hi", [P, 2, T], F32R)
            hid_lo = sb(part, "hid_lo", [P, 2, T], F32R)
            dq_raw = sb(part, "dq_raw", [P, HID], I32)
            dzp_raw = sb(part, "dzp_raw", [P, HID])
            dsc_raw = sb(part, "dsc_raw", [P, HID])
            dq_f = sb(part, "dq_f", [P, HID])
        with ExitStack() as part:
            qkv_raw = sb(part, "qkv_raw", [P, QKV_W])
            qkv_hi = sb(part, "qkv_hi", [P, QKV_W], F32R)
            qkv_lo = sb(part, "qkv_lo", [P, QKV_W], F32R)
            lwo_raw = sb(part, "lwo_raw", [P, WO_W])
            lwo_hi = sb(part, "lwo_hi", [P, WO_W], F32R)
            lwo_lo = sb(part, "lwo_lo", [P, WO_W], F32R)
            by_cos = sb(part, "by_cos", [P, 2, G + 1, 2, D // 2])
            by_sin = sb(part, "by_sin", [P, 2, G + 1, 2, D // 2])
            turned = sb(part, "turned", [P, 2, G + 1, 2, D // 2])
            qkT = sb(part, "qkT", [P, (2 * G + 2) * P])
            v_hi = sb(part, "v_hi", [P, 4, 2, D], F32R)
            v_lo = sb(part, "v_lo", [P, 4, 2, D], F32R)
            probs = sb(part, "probs", [P, 3 * G * P])
            row_max = sb(part, "row_max", [P, 2 * G])
            neg_max = sb(part, "neg_max", [P, 2 * G])
            row_sum = sb(part, "row_sum", [P, 2 * G])
            row_inv = sb(part, "row_inv", [P, 2 * G])
            pT_hi = sb(part, "pT_hi", [P, 3, G * P], F32R)
            pT_lo = sb(part, "pT_lo", [P, 3, G * P], F32R)
            oT_hi = sb(part, "oT_hi", [P, 2, G * P], F32R)
            oT_lo = sb(part, "oT_lo", [P, 2, G * P], F32R)

        bank = [ctx.enter_context(nc.psum_tensor(f"bank{i}", [P, 512], F32)) for i in range(8)]

        early_consts_in = sem("early_consts_in")
        late_consts_in = sem("late_consts_in")
        x_loaded = [sem(f"x_loaded{t}") for t in range(TILES)]
        consts_set = sem("consts_set")
        z_set = sem("z_set")
        ln_scaled = sem("ln_scaled")
        ln_stats = sem("ln_stats")
        ln_mean = sem("ln_mean")
        ln_var = sem("ln_var")
        ln_rstd = sem("ln_rstd")
        ln_out = sem("ln_out")
        x_added = sem("x_added")
        ln2_stats = sem("ln2_stats")
        ln2_mean = sem("ln2_mean")
        ln2_var = sem("ln2_var")
        ln2_rstd = sem("ln2_rstd")
        xn_ready = sem("xn_ready")
        xn_turned = sem("xn_turned")
        xn_hi_set = sem("xn_hi_set")
        xn_lo_set = sem("xn_lo_set")
        acc_zero = sem("acc_zero")
        a_loaded = [sem(f"a_loaded{s}") for s in range(2)]
        wo_loaded = [sem(f"wo_loaded{s}") for s in range(2)]
        a_hi_set = sem("a_hi_set")
        a_lo_set = sem("a_lo_set")
        wo_pairs = sem("wo_pairs")
        wo_summed = sem("wo_summed")
        wos_hi_set = sem("wos_hi_set")
        wos_lo_set = sem("wos_lo_set")
        a_proj = sem("a_proj")
        a_exp = sem("a_exp")
        a_relu = sem("a_relu")
        sq_set = sem("sq_set")
        sq_hi_set = sem("sq_hi_set")
        sq_lo_set = sem("sq_lo_set")
        mw_done = sem("mw_done")
        mw_hi_set = sem("mw_hi_set")
        mw_lo_set = sem("mw_lo_set")
        den_done = sem("den_done")
        den_read = sem("den_read")
        rden_set = sem("rden_set")
        a_out = sem("a_out")
        a_acc = sem("a_acc")
        f_loaded = [sem(f"f_loaded{s}") for s in range(2)]
        f_hi_set = sem("f_hi_set")
        f_lo_set = sem("f_lo_set")
        f_gate = sem("f_gate")
        f_up = sem("f_up")
        silu_set = sem("silu_set")
        hid_set = sem("hid_set")
        hid_hi_set = sem("hid_hi_set")
        hid_lo_set = sem("hid_lo_set")
        f_down = sem("f_down")
        f_acc = sem("f_acc")
        d_loaded = sem("d_loaded")
        d_step = sem("d_step")
        qkv_loaded = sem("qkv_loaded")
        lwo_loaded = sem("lwo_loaded")
        qkv_hi_set = sem("qkv_hi_set")
        qkv_lo_set = sem("qkv_lo_set")
        lwo_hi_set = sem("lwo_hi_set")
        lwo_lo_set = sem("lwo_lo_set")
        q_proj = sem("q_proj")
        kv_proj = sem("kv_proj")
        q_cos = sem("q_cos")
        q_sin = sem("q_sin")
        k_cos = sem("k_cos")
        k_sin = sem("k_sin")
        turned_set = sem("turned_set")
        qk_turned = sem("qk_turned")
        qkT_set = sem("qkT_set")
        v_hi_set = sem("v_hi_set")
        v_lo_set = sem("v_lo_set")
        score_done = sem("score_done")
        masked_set = sem("masked_set")
        neg_max_set = sem("neg_max_set")
        exp_set = sem("exp_set")
        row_inv_set = sem("row_inv_set")
        probs_set = sem("probs_set")
        pT_done = sem("pT_done")
        pT_hi_set = sem("pT_hi_set")
        pT_lo_set = sem("pT_lo_set")
        pv_done = sem("pv_done")
        oT_hi_set = sem("oT_hi_set")
        oT_lo_set = sem("oT_lo_set")
        l_out = sem("l_out")
        l_acc = sem("l_acc")
        d_out = sem("d_out")
        stored = sem("stored")

        waits_passed = sem("waits_passed")

        def slots(eng, slot):
            for b in range(4):
                slot(0, b, True, b >= 1, b >= 2)
            with eng.Fori(1, KV) as g:
                for b in range(4):
                    slot(g, b, True, True, True)
            slot(KV, 0, False, True, True)
            slot(KV, 1, False, False, True)

        def wait_apart(eng, semaphore, value):
            eng.wait_ge(semaphore, value)
            if not isinstance(value, int):
                eng.sem_inc(waits_passed, 1)

        block = ctx.enter_context(nc.Block())

        @block.sync
        def _(sync):
            for t in range(TILES):
                sync.dma_start(x[:, t, :], x_in[t * P:(t + 1) * P, :]).then_inc(x_loaded[t], 16)
            sync.dma_start(ident[:], ident_in).then_inc(early_consts_in, 16)
            sync.dma_start(bq[:], a_bq).then_inc(early_consts_in, 16)
            sync.dma_start(z_col[:], a_z).then_inc(early_consts_in, 16)

            def load_head(h, s):
                sync.dma_start(a_raw[:, s, :], a_w[bass.ds(h, 1), :, :].rearrange("a p n -> p (a n)"))\
                    .then_inc(a_loaded[s], 16)
                sync.dma_start(wo_raw[:, s, :, :].rearrange("p g n -> p (g n)"),
                               a_wo[bass.ds(h, 1), :, :].rearrange("a p n -> p (a n)")).then_inc(wo_loaded[s], 16)

            for s in range(2):
                load_head(s, s)
            sync.dma_start(fsc[:].rearrange("p a f -> p (a f)"), f_scale).then_inc(late_consts_in, 16)
            sync.dma_start(down_row[:], down_s).then_inc(late_consts_in, 16)
            sync.dma_start(bias_row[:], d_bias).then_inc(late_consts_in, 16)
            sync.dma_start(cos_sin[:].rearrange("p a b f -> p (a b f)"), rope).then_inc(late_consts_in, 16)
            sync.dma_start(masks[:], mask).then_inc(late_consts_in, 16)
            with sync.Fori(1, KV // 2) as i:
                for s in range(2):
                    sync.wait_ge(a_lo_set, 2 * i + s - 1)
                    sync.wait_ge(wo_pairs, 2 * i + s - 1)
                    load_head(2 * i + s, s)

            def load_slice(f, s):
                sync.dma_start(f_raw[:, s, :], f_w[bass.ds(f, 1), :, :].rearrange("a p n -> p (a n)"))\
                    .then_inc(f_loaded[s], 16)

            sync.wait_ge(xn_ready, 2 * TILES)
            for s in range(2):
                load_slice(s, s)
            with sync.Fori(1, FT // 2) as i:
                for s in range(2):
                    sync.wait_ge(f_lo_set, 2 * i + s - 1)
                    load_slice(2 * i + s, s)
            for k in range(KT):
                if k:
                    sync.wait_ge(d_step, 5 * k)
                for dst, src in ((dq_raw, d_q), (dzp_raw, d_zp), (dsc_raw, d_scale)):
                    sync.dma_start(dst[:], src[k * P:(k + 1) * P, :]).then_inc(d_loaded, 16)

            def load_qkv(g):
                sync.dma_start(qkv_raw[:], l_qkv[bass.ds(g, 1), :, :].rearrange("a p n -> p (a n)"))\
                    .then_inc(qkv_loaded, 16)

            def load_lwo(g):
                sync.dma_start(lwo_raw[:], l_wo[bass.ds(g, 1), :, :].rearrange("a p n -> p (a n)"))\
                    .then_inc(lwo_loaded, 16)

            sync.wait_ge(xn_ready, 3 * TILES)
            sync.wait_ge(d_step, 5 * KT)
            load_qkv(0)
            load_lwo(0)
            with sync.Fori(1, KV) as g:
                sync.wait_ge(qkv_lo_set, KT * g)
                load_qkv(g)
                sync.wait_ge(lwo_lo_set, G * g)
                load_lwo(g)
            for t in range(TILES):
                sync.wait_ge(x_added, 3 * TILES + t + 1)
                sync.dma_start(out[t * P:(t + 1) * P, :], x[:, t, :]).then_inc(stored, 16)
            sync.wait_ge(stored, 16 * TILES)

        @block.gpsimd
        def _(pool):
            nc.gpsimd.memset(minus_half[:], -0.5).then_inc(consts_set, 1)
            nc.gpsimd.memset(zeros[:], 0.0).then_inc(consts_set, 1)

            def powers(k):
                for s in range(TILES // 2 + 1):
                    c = s
                    if k > 0 and c < TILES // 2:
                        pool.wait_ge(ln_var, (k - 1) * TILES // 2 + c + 1)
                        nc.gpsimd.tensor_tensor(rstd[:, 0, 2 * c:2 * c + 2], var_eps[:, 0, 2 * c:2 * c + 2],
                                                minus_half[:], ALU.pow).then_inc(ln_rstd, 1)
                    c = s - 1
                    if k < 4 and c >= 0:
                        pool.wait_ge(ln2_var, k * TILES // 2 + c + 1)
                        nc.gpsimd.tensor_tensor(rstd[:, 1, 2 * c:2 * c + 2], var_eps[:, 1, 2 * c:2 * c + 2],
                                                minus_half[:], ALU.pow).then_inc(ln2_rstd, 1)

            def clear_acc(k):
                for t in range(TILES):
                    pool.wait_ge(xn_turned, k * TILES + t + 1)
                    nc.gpsimd.memset(acc[:, t, :], 0.0).then_inc(acc_zero, 1)

            pool.wait_ge(consts_set, 2)
            pool.wait_ge(early_consts_in, 16 * 3)
            for h in range(KV):
                nc.gpsimd.tensor_scalar(z_rep[:, h, :], zeros[:], 1.0, z_col[:, h:h + 1], ALU.mult, ALU.add)\
                    .then_inc(z_set, 1)

            def prepare_head(h, s, first):
                wait_apart(pool, a_loaded[s], 16 * (h // 2 + 1) if first else 16 * h[1])
                hh = h if first else h[0]
                if not first:
                    wait_apart(pool, mw_done, hh - 1)
                nc.gpsimd.tensor_scalar(a_hi[:, s, :], a_raw[:, s, :], 1.0, 1.0, ALU.mult, ALU.mult)\
                    .then_inc(a_hi_set, 1)
                pool.wait_ge(a_hi_set, hh + 1)
                nc.gpsimd.tensor_tensor(a_lo[:, s, :], a_raw[:, s, :], a_hi[:, s, :].bitcast(F32), ALU.subtract)\
                    .then_inc(a_lo_set, 1)
                pool.wait_ge(wo_loaded[s], 16 * (h // 2 + 1) if first else 16 * h[1])
                if not (first and h == 0):
                    pool.wait_ge(wo_summed, hh)
                nc.gpsimd.tensor_tensor(wo_pair[:], wo_raw[:, s, 0:2, :], wo_raw[:, s, 2:4, :], ALU.add)\
                    .then_inc(wo_pairs, 1)
                pool.wait_ge(wo_pairs, hh + 1)
                if not (first and h == 0):
                    pool.wait_ge(wos_lo_set, hh)
                nc.gpsimd.tensor_tensor(wo_sum[:], wo_pair[:, 0, :], wo_pair[:, 1, :], ALU.add).then_inc(wo_summed, 1)
                wait_apart(pool, wo_summed, hh + 1)
                nc.gpsimd.tensor_scalar(wos_hi[:, s, :], wo_sum[:], 1.0, 1.0, ALU.mult, ALU.mult)\
                    .then_inc(wos_hi_set, 1)
                pool.wait_ge(wos_hi_set, hh + 1)
                nc.gpsimd.tensor_tensor(wos_lo[:, s, :], wo_sum[:], wos_hi[:, s, :].bitcast(F32), ALU.subtract)\
                    .then_inc(wos_lo_set, 1)

            for s in range(2):
                prepare_head(s, s, True)
            powers(0)
            clear_acc(0)
            with pool.Fori(1, KV // 2) as i:
                for s in range(2):
                    prepare_head((2 * i + s, i + 1), s, False)
            powers(1)

            def split_slice(f, s, loads, used):
                wait_apart(pool, f_loaded[s], 16 * loads)
                if used is not None:
                    wait_apart(pool, f_down, used)
                nc.gpsimd.tensor_scalar(f_hi[:, s, :], f_raw[:, s, :], 1.0, 1.0, ALU.mult, ALU.mult)\
                    .then_inc(f_hi_set, 1)

            for s in range(2):
                split_slice(s, s, 1, None)
            clear_acc(1)
            with pool.Fori(1, FT // 2) as i:
                for s in range(2):
                    split_slice(2 * i + s, s, i + 1, TILES * i)

            for k in range(KT):
                pool.wait_ge(d_loaded, 48 * (k + 1))
                if k:
                    pool.wait_ge(d_step, 5 * k)
                nc.gpsimd.tensor_scalar(dq_f[:], dq_raw[:], 1.0, 1.0, ALU.mult, ALU.mult).then_inc(d_step, 1)
                pool.wait_ge(d_step, 5 * k + 1)
                nc.gpsimd.tensor_tensor(dq_f[:], dq_f[:], dzp_raw[:], ALU.subtract).then_inc(d_step, 1)
                pool.wait_ge(d_step, 5 * k + 2)
                nc.gpsimd.tensor_tensor(dq_f[:], dq_f[:], dsc_raw[:], ALU.mult).then_inc(d_step, 1)
                pool.wait_ge(d_step, 5 * k + 3)
                nc.gpsimd.tensor_scalar(d_hi[:, k, :], dq_f[:], 1.0, 1.0, ALU.mult, ALU.mult).then_inc(d_step, 1)
                pool.wait_ge(d_step, 5 * k + 4)
                nc.gpsimd.tensor_tensor(d_lo[:, k, :], dq_f[:], d_hi[:, k, :].bitcast(F32), ALU.subtract)\
                    .then_inc(d_step, 1)
            powers(2)

            def slot(g, b, first, second, third):
                u = 4 * g + b
                if first and b == 0:
                    wait_apart(pool, qkv_loaded, 16 * (g + 1))
                    for k in range(KT):
                        if not isinstance(g, int):
                            wait_apart(pool, q_proj, 8 * g)
                        c = slice(k * QKV_W // KT, (k + 1) * QKV_W // KT)
                        nc.gpsimd.tensor_scalar(qkv_hi[:, c], qkv_raw[:, c], 1.0, 1.0, ALU.mult, ALU.mult)\
                            .then_inc(qkv_hi_set, 1)
                if first and b == 2:
                    wait_apart(pool, lwo_loaded, 16 * (g + 1))
                    for h in range(G):
                        if not isinstance(g, int):
                            wait_apart(pool, l_out, 8 * g)
                        c = slice(h * HID, (h + 1) * HID)
                        nc.gpsimd.tensor_scalar(lwo_hi[:, c], lwo_raw[:, c], 1.0, 1.0, ALU.mult, ALU.mult)\
                            .then_inc(lwo_hi_set, 1)
                if first:
                    if second:
                        pool.wait_ge(qk_turned, 3 * u)
                    for t in range(2):
                        pool.wait_ge(q_sin, 2 * u + t + 1)
                        nc.gpsimd.tensor_tensor(turned[:, t, 0:G, 0, :], by_cos[:, t, 0:G, 0, :],
                                                by_sin[:, t, 0:G, 1, :], ALU.subtract).then_inc(turned_set, 1)
                        nc.gpsimd.tensor_tensor(turned[:, t, 0:G, 1, :], by_sin[:, t, 0:G, 0, :],
                                                by_cos[:, t, 0:G, 1, :], ALU.add).then_inc(turned_set, 1)
                    pool.wait_ge(k_sin, u + 1)
                    nc.gpsimd.tensor_tensor(turned[:, :, G, 0, :], by_cos[:, :, G, 0, :], by_sin[:, :, G, 1, :],
                                            ALU.subtract).then_inc(turned_set, 1)
                    nc.gpsimd.tensor_tensor(turned[:, :, G, 1, :], by_sin[:, :, G, 0, :], by_cos[:, :, G, 1, :],
                                            ALU.add).then_inc(turned_set, 1)
                if second:
                    wait_apart(pool, row_inv_set, u)
                    for j in range(2 * G):
                        c = slice(j * P, (j + 1) * P) if j < G else slice((2 * j - G) * P, (2 * j - G + 2) * P)
                        nc.gpsimd.tensor_scalar(probs[:, c], probs[:, c], row_inv[:, j:j + 1], 1.0,
                                                ALU.mult, ALU.mult).then_inc(probs_set, 1)

            clear_acc(2)
            slots(pool, slot)
            powers(3)
            powers(4)

        @block.scalar
        def _(act):
            def turn_hi(k):
                for t in range(TILES):
                    act.wait_ge(xn_turned, k * TILES + t + 1)
                    if t == 0 and k == 2:
                        act.wait_ge(f_gate, 2 * FT)
                    nc.scalar.activation(xn_hi[:, :, t * P:(t + 1) * P],
                                         bank[4 + t % 4][:, :].rearrange("p (k c) -> p k c", k=KT), ACT.Copy)\
                        .then_inc(xn_hi_set, 1)

            turn_hi(0)
            act.wait_ge(early_consts_in, 16 * 3)

            def head(h, s, first):
                for j in range(2):
                    c = slice(j * HALF, (j + 1) * HALF)
                    wait_apart(act, a_proj, 2 * h + j + 1)
                    if not first:
                        wait_apart(act, sq_set, 2 * h + j - 1)
                    nc.scalar.activation(expq[:, c], bank[j][:, :], ACT.Exp, bias=bq[:, bass.ds(h, 1)])\
                        .then_inc(a_exp, 1)
                    nc.scalar.activation(reluq[:, c], bank[j][:, :], ACT.Relu, bias=bq[:, bass.ds(h, 1)])\
                        .then_inc(a_relu, 1)
                    act.wait_ge(sq_set, 2 * h + j + 1)
                    if not first:
                        act.wait_ge(a_out, 8 * h - 4 + 4 * j)
                    nc.scalar.activation(sq_hi[:, c], sq[:, c], ACT.Copy).then_inc(sq_hi_set, 1)
                act.wait_ge(mw_done, h + 1)
                nc.scalar.activation(mw_hi[:, s, :], bank[2 + s][:, :], ACT.Copy).then_inc(mw_hi_set, 1)

            head(0, 0, True)
            head(1, 1, False)
            with act.Fori(1, KV // 2) as i:
                for s in range(2):
                    head(2 * i + s, s, False)
            turn_hi(1)
            act.wait_ge(late_consts_in, 16 * 5)

            def slice_(f, s, pair, first):
                for j in range(2):
                    c = slice(j * HALF, (j + 1) * HALF)
                    wait_apart(act, f_gate, 2 * f + j + 1)
                    if not (first and s == 0):
                        wait_apart(act, hid_set, 2 * f + j - 1)
                    nc.scalar.activation(silu[:, c], bank[j][:, :], ACT.Silu, scale=fsc[:, 0, bass.ds(f, 1)])\
                        .then_inc(silu_set, 1)
                    act.wait_ge(hid_set, 2 * f + j + 1)
                    if not first:
                        act.wait_ge(f_down, 8 * pair - 4 + 4 * j)
                    nc.scalar.activation(hid_hi[:, s, c], hid[:, s, c], ACT.Copy).then_inc(hid_hi_set, 1)

            for s in range(2):
                slice_(s, s, 0, True)
            with act.Fori(1, FT // 2) as i:
                for s in range(2):
                    slice_(2 * i + s, s, i, False)
            turn_hi(2)

            def slot(g, b, first, second, third):
                u = 4 * g + b
                if second:
                    v = u - 1
                    for j in range(3):
                        act.wait_ge(qk_turned, 3 * v + j + 1)
                        if third:
                            act.wait_ge(score_done, 3 * v)
                        n = 512 if j < 2 else 256
                        nc.scalar.activation(qkT[:, j * 512:j * 512 + n], bank[2 + j % 2][:, 0:n], ACT.Copy)\
                            .then_inc(qkT_set, 1)
                if third:
                    w = u - 2
                    for j in range(3):
                        act.wait_ge(pT_done, 3 * w + j + 1)
                        if not (isinstance(w, int) and w == 0):
                            act.wait_ge(pv_done, 2 * w)
                        nc.scalar.activation(pT_hi[:, j, :], bank[2 + (j + 1) % 2][:, :], ACT.Copy)\
                            .then_inc(pT_hi_set, 1)
                if first:
                    act.wait_ge(kv_proj, u + 1)
                    if not isinstance(g, int):
                        act.wait_ge(pv_done, 2 * (u - 3))
                    kv = bank[(3 * b + 1) % 2][:, :].rearrange("p (t a d) -> p t a d", t=2, a=2)
                    act.wait_ge(k_sin, u + 1)
                    nc.scalar.activation(v_hi[:, b, :, :], kv[:, :, 1, :], ACT.Copy).then_inc(v_hi_set, 1)
                if third:
                    for t in range(2):
                        act.wait_ge(pv_done, 2 * w + t + 1)
                        if not (isinstance(w, int) and w == 0):
                            act.wait_ge(l_out, 2 * w)
                        nc.scalar.activation(oT_hi[:, t, :], bank[6 + t][:, :], ACT.Copy).then_inc(oT_hi_set, 1)
                if second:
                    act.wait_ge(neg_max_set, u)
                    for j in range(2 * G):
                        c = slice(j * P, (j + 1) * P) if j < G else slice((2 * j - G) * P, (2 * j - G + 2) * P)
                        if j == 0 and third:
                            act.wait_ge(row_inv_set, v)
                        nc.scalar.activation(probs[:, c], probs[:, c], ACT.Exp, bias=neg_max[:, j:j + 1],
                                             scale=SCALE, accum_out=row_sum[:, j:j + 1]).then_inc(exp_set, 1)

            slots(act, slot)
            turn_hi(3)

        @block.vector
        def _(dve):
            pairs = TILES // 2

            def norm(k):
                def out_norm(c):
                    for t in (2 * c, 2 * c + 1):
                        if k == 2:
                            nc.vector.tensor_tensor(acc[:, t, :], acc[:, t, :], down_row[:], ALU.mult)\
                                .then_inc(ln_scaled, 1)
                        if k == 4:
                            dve.wait_ge(d_out, t + 1)
                            nc.vector.tensor_tensor(acc[:, t, :], bank[t % 4][:, :], bias_row[:], ALU.add)\
                                .then_inc(ln_scaled, 1)
                    for t in (2 * c, 2 * c + 1):
                        if k in (2, 4):
                            dve.wait_ge(ln_scaled, (k // 2 - 1) * TILES + t + 1)
                        nc.vector.bn_stats(stats[:, t, :], acc[:, t, :]).then_inc(ln_stats, 1)
                    for t in (2 * c, 2 * c + 1):
                        dve.wait_ge(ln_stats, (k - 1) * TILES + t + 1)
                        nc.vector.bn_aggr(mean_var[:, t, :], stats[:, t, :]).then_inc(ln_mean, 1)
                    dve.wait_ge(ln_mean, (k - 1) * TILES + 2 * c + 2)
                    nc.vector.tensor_scalar(var_eps[:, 0, 2 * c:2 * c + 2], mean_var[:, 2 * c:2 * c + 2, 1],
                                            LN_EPS, None, ALU.add).then_inc(ln_var, 1)

                def residual(c):
                    if k:
                        dve.wait_ge(ln_rstd, (k - 1) * pairs + c + 1)
                        for t in (2 * c, 2 * c + 1):
                            nc.vector.tensor_scalar(acc[:, t, :], acc[:, t, :], mean_var[:, t, 0:1],
                                                    rstd[:, 0, t:t + 1], ALU.subtract, ALU.mult).then_inc(ln_out, 1)
                        for t in (2 * c, 2 * c + 1):
                            dve.wait_ge(ln_out, (k - 1) * TILES + t + 1)
                            nc.vector.tensor_tensor(x[:, t, :], x[:, t, :], acc[:, t, :], ALU.add).then_inc(x_added, 1)
                    if k == 4:
                        return
                    for t in (2 * c, 2 * c + 1):
                        if k:
                            dve.wait_ge(x_added, (k - 1) * TILES + t + 1)
                        else:
                            dve.wait_ge(x_loaded[t], 16)
                        nc.vector.bn_stats(stats2[:, t, :], x[:, t, :]).then_inc(ln2_stats, 1)
                    for t in (2 * c, 2 * c + 1):
                        dve.wait_ge(ln2_stats, k * TILES + t + 1)
                        nc.vector.bn_aggr(mean_var2[:, t, :], stats2[:, t, :]).then_inc(ln2_mean, 1)
                    dve.wait_ge(ln2_mean, k * TILES + 2 * c + 2)
                    nc.vector.tensor_scalar(var_eps[:, 1, 2 * c:2 * c + 2], mean_var2[:, 2 * c:2 * c + 2, 1],
                                            LN_EPS, None, ALU.add).then_inc(ln2_var, 1)

                def in_norm(c):
                    dve.wait_ge(ln2_rstd, k * pairs + c + 1)
                    for t in (2 * c, 2 * c + 1):
                        nc.vector.tensor_scalar(acc[:, t, :], x[:, t, :], mean_var2[:, t, 0:1], rstd[:, 1, t:t + 1],
                                                ALU.subtract, ALU.mult).then_inc(xn_ready, 1)

                def turn_lo(c):
                    for t in (2 * c, 2 * c + 1):
                        n = k * TILES + t + 1
                        dve.wait_ge(xn_hi_set, n)
                        s = slice(t * P, (t + 1) * P)
                        nc.vector.tensor_tensor(xn_lo[:, :, s], bank[4 + t % 4][:, :].rearrange("p (k c) -> p k c", k=KT),
                                                xn_hi[:, :, s].bitcast(F32), ALU.subtract).then_inc(xn_lo_set, 1)

                for s in range(pairs + 3):
                    if k and s < pairs:
                        out_norm(s)
                    if 0 <= s - 1 < pairs:
                        residual(s - 1)
                    if k < 4 and 0 <= s - 2 < pairs:
                        in_norm(s - 2)
                    if k < 4 and 0 <= s - 3 < pairs:
                        turn_lo(s - 3)

            norm(0)
            dve.wait_ge(acc_zero, TILES)

            def head(h, s, first):
                for j in range(2):
                    c = slice(j * HALF, (j + 1) * HALF)
                    dve.wait_ge(a_relu, 2 * h + j + 1)
                    if not first:
                        dve.wait_ge(sq_lo_set, 2 * h + j - 1)
                        dve.wait_ge(sq_hi_set, 2 * h + j - 1)
                        dve.wait_ge(a_out, 8 * h - 4 + 4 * j)
                    nc.vector.scalar_tensor_tensor(out=sq[:, c], in0=expq[:, c], scalar=1.0, in1=reluq[:, c],
                                                   op0=ALU.min, op1=ALU.add).then_inc(sq_set, 1)
                    dve.wait_ge(sq_hi_set, 2 * h + j + 1)
                    nc.vector.tensor_tensor(sq_lo[:, c], sq[:, c], sq_hi[:, c].bitcast(F32), ALU.subtract)\
                        .then_inc(sq_lo_set, 1)
                dve.wait_ge(mw_hi_set, h + 1)
                nc.vector.tensor_tensor(mw_lo[:, s, :], bank[2 + s][:, :], mw_hi[:, s, :].bitcast(F32), ALU.subtract)\
                    .then_inc(mw_lo_set, 1)
                for j in range(2):
                    dve.wait_ge(den_done, 2 * h + j + 1)
                    if not first:
                        dve.wait_ge(a_acc, 8 * h)
                    nc.vector.tensor_scalar(den_eps[:, 4 * j:4 * j + 4], bank[j][:, 0:4 * DEN_STEP:DEN_STEP],
                                            DEN_EPS, None, ALU.add).then_inc(den_read, 1)
                    dve.wait_ge(den_read, 2 * h + j + 1)
                    nc.vector.reciprocal(rden[:, 4 * j:4 * j + 4], den_eps[:, 4 * j:4 * j + 4]).then_inc(rden_set, 1)
                    dve.wait_ge(rden_set, 2 * h + j + 1)
                    for t in range(4 * j, 4 * j + 4):
                        dve.wait_ge(a_out, 8 * h + t + 1)
                        if not first:
                            dve.wait_ge(a_acc, 8 * h + t - 7)
                        nc.vector.scalar_tensor_tensor(out=acc[:, t, :], in0=bank[4 + t % 4][:, :],
                                                       scalar=rden[:, t:t + 1], in1=acc[:, t, :],
                                                       op0=ALU.mult, op1=ALU.add).then_inc(a_acc, 1)

            head(0, 0, True)
            head(1, 1, False)
            with dve.Fori(1, KV // 2) as i:
                for s in range(2):
                    head(2 * i + s, s, False)
            dve.wait_ge(a_acc, 8 * KV)
            dve.wait_ge(late_consts_in, 16 * 5)
            norm(1)
            dve.wait_ge(acc_zero, 2 * TILES)

            def pair(p, first):
                for s in range(2):
                    dve.wait_ge(f_hi_set, 2 * p + s + 1)
                    if not first:
                        dve.wait_ge(f_down, 8 * p)
                    nc.vector.tensor_tensor(f_lo[:, s, :], f_raw[:, s, :], f_hi[:, s, :].bitcast(F32), ALU.subtract)\
                        .then_inc(f_lo_set, 1)
                for s in range(2):
                    f = 2 * p + s
                    for j in range(2):
                        c = slice(j * HALF, (j + 1) * HALF)
                        dve.wait_ge(silu_set, 2 * f + j + 1)
                        dve.wait_ge(f_up, 2 * f + j + 1)
                        if not first:
                            dve.wait_ge(hid_lo_set, 2 * f + j - 3)
                            dve.wait_ge(hid_hi_set, 2 * f + j - 3)
                        nc.vector.scalar_tensor_tensor(out=hid[:, s, c], in0=bank[2 + j][:, :],
                                                       scalar=fsc[:, 1, bass.ds(f, 1)], in1=silu[:, c],
                                                       op0=ALU.mult, op1=ALU.mult).then_inc(hid_set, 1)
                        dve.wait_ge(hid_hi_set, 2 * f + j + 1)
                        nc.vector.tensor_tensor(hid_lo[:, s, c], hid[:, s, c], hid_hi[:, s, c].bitcast(F32),
                                                ALU.subtract).then_inc(hid_lo_set, 1)
                for t in range(TILES):
                    dve.wait_ge(f_down, 8 * p + t + 1)
                    if not first:
                        dve.wait_ge(f_acc, 8 * p + t - 7)
                    nc.vector.tensor_tensor(acc[:, t, :], bank[4 + t % 4][:, :], acc[:, t, :], ALU.add)\
                        .then_inc(f_acc, 1)

            pair(0, True)
            with dve.Fori(1, FT // 2) as p:
                pair(p, False)
            dve.wait_ge(f_acc, 8 * (FT // 2))
            norm(2)
            dve.wait_ge(acc_zero, 3 * TILES)

            def slot(g, b, first, second, third):
                u = 4 * g + b
                v, w = u - 1, u - 2
                if first and b == 0:
                    for k in range(KT):
                        dve.wait_ge(qkv_hi_set, KT * g + k + 1)
                        c = slice(k * QKV_W // KT, (k + 1) * QKV_W // KT)
                        nc.vector.tensor_tensor(qkv_lo[:, c], qkv_raw[:, c], qkv_hi[:, c].bitcast(F32), ALU.subtract)\
                            .then_inc(qkv_lo_set, 1)
                if first and b == 2:
                    for h in range(G):
                        dve.wait_ge(lwo_hi_set, G * g + h + 1)
                        c = slice(h * HID, (h + 1) * HID)
                        nc.vector.tensor_tensor(lwo_lo[:, c], lwo_raw[:, c], lwo_hi[:, c].bitcast(F32), ALU.subtract)\
                            .then_inc(lwo_lo_set, 1)

                def products(t):
                    q = bank[(3 * b + 2 * t) % 2][:, :].rearrange("p (h a f) -> p h a f", h=G, a=2)
                    dve.wait_ge(q_proj, 2 * u + t + 1)
                    if second:
                        dve.wait_ge(turned_set, 6 * u)
                    for a, dst, done in ((0, by_cos, q_cos), (1, by_sin, q_sin)):
                        tab = cos_sin[:, a, t, None, None, :].to_broadcast([P, G, 2, D // 2])
                        nc.vector.tensor_tensor(dst[:, t, 0:G, :, :], q, tab, ALU.mult).then_inc(done, 1)

                if first:
                    products(0)
                if third:
                    for j in range(3):
                        dve.wait_ge(pT_hi_set, 3 * w + j + 1)
                        nc.vector.tensor_tensor(pT_lo[:, j, :], bank[2 + (j + 1) % 2][:, :],
                                                pT_hi[:, j, :].bitcast(F32), ALU.subtract).then_inc(pT_lo_set, 1)
                if first:
                    kv = bank[(3 * b + 1) % 2][:, :].rearrange("p (t c a f) -> p t c a f", t=2, c=2, a=2)
                    dve.wait_ge(kv_proj, u + 1)
                    for a, dst, done in ((0, by_cos, k_cos), (1, by_sin, k_sin)):
                        tab = cos_sin[:, a, :, None, :].to_broadcast([P, 2, 2, D // 2])
                        nc.vector.tensor_tensor(dst[:, :, G, :, :], kv[:, :, 0, :, :], tab, ALU.mult).then_inc(done, 1)
                    products(1)
                    dve.wait_ge(v_hi_set, u + 1)
                    kv = bank[(3 * b + 1) % 2][:, :].rearrange("p (t a d) -> p t a d", t=2, a=2)
                    nc.vector.tensor_tensor(v_lo[:, b, :, :], kv[:, :, 1, :], v_hi[:, b, :, :].bitcast(F32),
                                            ALU.subtract).then_inc(v_lo_set, 1)
                if third:
                    for t in range(2):
                        dve.wait_ge(oT_hi_set, 2 * w + t + 1)
                        nc.vector.tensor_tensor(oT_lo[:, t, :], bank[6 + t][:, :], oT_hi[:, t, :].bitcast(F32),
                                                ALU.subtract).then_inc(oT_lo_set, 1)
                if second:
                    if third:
                        dve.wait_ge(pT_done, 3 * w + 3)
                    for j in range(2 * G):
                        sbank = 4 + (3 * (b - 1) + (0 if j < G else 1 + (j - G) // 2)) % 2
                        wait_apart(dve, score_done, 3 * v + (1 if j < G else 2 + (j - G) // 2))
                        if j < G:
                            c, sc, m = slice(j * P, (j + 1) * P), slice(j * P, (j + 1) * P), masks[:, P:2 * P]
                        else:
                            c = slice((2 * j - G) * P, (2 * j - G + 2) * P)
                            sc, m = slice((j % 2) * 2 * P, (j % 2 + 1) * 2 * P), masks[:, :]
                        nc.vector.tensor_tensor_reduce(out=probs[:, c], in0=bank[sbank][:, sc], in1=m, scale=1.0,
                                                       scalar=LOWEST, op0=ALU.add, op1=ALU.max,
                                                       accum_out=row_max[:, j:j + 1]).then_inc(masked_set, 1)
                    dve.wait_ge(masked_set, 8 * v + 8)
                    if third:
                        dve.wait_ge(exp_set, 8 * v)
                    nc.vector.tensor_scalar(neg_max[:], row_max[:], -SCALE, None, ALU.mult).then_inc(neg_max_set, 1)
                if third:
                    for t in range(2):
                        dve.wait_ge(l_out, 2 * w + t + 1)
                        r = 2 * ((b - 2) % 4) + t
                        if not (isinstance(w, int) and w == 0):
                            dve.wait_ge(l_acc, 2 * w)
                        nc.vector.tensor_tensor(acc[:, r, :], bank[6 + t][:, :], acc[:, r, :], ALU.add)\
                            .then_inc(l_acc, 1)
                if second:
                    dve.wait_ge(exp_set, 8 * v + 8)
                    if third:
                        dve.wait_ge(probs_set, 8 * v)
                    nc.vector.reciprocal(row_inv[:], row_sum[:]).then_inc(row_inv_set, 1)

            slots(dve, slot)
            dve.wait_ge(l_acc, 8 * KV)
            norm(3)
            norm(4)

        @block.tensor
        def _(pe):
            def product(o, lhs, rhs, start, stop):
                nc.tensor.matmul(o, lhs[0], rhs[0], start=start, stop=False)
                nc.tensor.matmul(o, lhs[0], rhs[1], start=False, stop=False)
                return nc.tensor.matmul(o, lhs[1], rhs[0], start=False, stop=stop)

            def turn(k):
                for t in range(TILES):
                    pe.wait_ge(xn_ready, k * TILES + t + 1)
                    if t >= 4:
                        pe.wait_ge(xn_lo_set, k * TILES + t - 3)
                    for i in range(KT):
                        last = nc.tensor.transpose(bank[4 + t % 4][:, i * P:(i + 1) * P],
                                                   acc[:, t, i * P:(i + 1) * P], ident[:])
                    last.then_inc(xn_turned, 1)

            pe.wait_ge(early_consts_in, 16 * 3)
            turn(0)

            def head(h, s, first):
                pe.wait_ge(a_lo_set, h + 1)
                for j in range(2):
                    c = slice(j * HALF, (j + 1) * HALF)
                    if first:
                        pe.wait_ge(xn_lo_set, 4 * j + 4)
                    else:
                        pe.wait_ge(den_read, 2 * h + j - 1)
                    for k in range(KT):
                        w = slice(k * D, (k + 1) * D)
                        last = product(bank[j][:, :], (a_hi[:, s, w], a_lo[:, s, w]),
                                       (xn_hi[:, k, c], xn_lo[:, k, c]), k == 0, k == KT - 1)
                    last.then_inc(a_proj, 1)
                m = slice(KT * D, A_W)
                pe.wait_ge(wos_lo_set, h + 1)
                if not first:
                    pe.wait_ge(mw_lo_set, h - 1) if s == 0 else pe.wait_ge(mw_lo_set, h)
                product(bank[2 + s][:, :], (a_hi[:, s, m], a_lo[:, s, m]), (wos_hi[:, s, :], wos_lo[:, s, :]),
                        True, True).then_inc(mw_done, 1)
                if first:
                    pe.wait_ge(z_set, KV)
                for j in range(2):
                    pe.wait_ge(sq_set, 2 * h + j + 1)
                    for t in range(4 * j, 4 * j + 4):
                        o = (t % 4) * DEN_STEP
                        last = nc.tensor.matmul(bank[j][:, o:o + P], sq[:, t * P:(t + 1) * P], z_rep[:, bass.ds(h, 1), :].rearrange("p a c -> p (a c)"),
                                                start=True, stop=True)
                    last.then_inc(den_done, 1)
                    pe.wait_ge(sq_lo_set, 2 * h + j + 1)
                    pe.wait_ge(mw_lo_set, h + 1)
                    for t in range(4 * j, 4 * j + 4):
                        if not (first and t < 4):
                            pe.wait_ge(a_acc, 8 * h + t - 3)
                        c = slice(t * P, (t + 1) * P)
                        product(bank[4 + t % 4][:, :], (sq_hi[:, c], sq_lo[:, c]), (mw_hi[:, s, :], mw_lo[:, s, :]),
                                True, True).then_inc(a_out, 1)

            head(0, 0, True)
            head(1, 1, False)
            with pe.Fori(1, KV // 2) as i:
                for s in range(2):
                    head(2 * i + s, s, False)
            turn(1)

            def pair(p, first):
                for s in range(2):
                    f = 2 * p + s
                    pe.wait_ge(f_lo_set, f + 1)
                    for j in range(2):
                        c = slice(j * HALF, (j + 1) * HALF)
                        if first:
                            pe.wait_ge(xn_lo_set, TILES + 4 * j + 4)
                        for a, done in ((0, f_gate), (1, f_up)):
                            if not (first and s == 0):
                                pe.wait_ge(silu_set, 2 * f + j - 1) if a == 0 else pe.wait_ge(hid_set, 2 * f + j - 1)
                            for k in range(KT):
                                w = slice((a * KT + k) * P, (a * KT + k + 1) * P)
                                last = product(bank[2 * a + j][:, :], (f_hi[:, s, w], f_lo[:, s, w]),
                                               (xn_hi[:, k, c], xn_lo[:, k, c]), k == 0, k == KT - 1)
                            last.then_inc(done, 1)
                d = slice(2 * KT * P, F_W)
                for t in range(TILES):
                    if t % 4 == 0:
                        pe.wait_ge(hid_lo_set, 4 * p + 3 + t // 4)
                    if not (first and t < 4):
                        pe.wait_ge(f_acc, 8 * p + t - 3)
                    c = slice(t * P, (t + 1) * P)
                    for s in range(2):
                        last = product(bank[4 + t % 4][:, :], (hid_hi[:, s, c], hid_lo[:, s, c]),
                                       (f_hi[:, s, d], f_lo[:, s, d]), s == 0, s == 1)
                    last.then_inc(f_down, 1)

            pair(0, True)
            with pe.Fori(1, FT // 2) as p:
                pair(p, False)
            turn(2)

            def slot(g, b, first, second, third):
                u = 4 * g + b
                v, w = u - 1, u - 2

                def project(t, what):
                    r = 2 * b + t
                    c = slice(r * P, (r + 1) * P)
                    for k in range(KT):
                        base = k * QKV_W // KT
                        ws = slice(base, base + G * D) if what == "q" else slice(base + G * D, base + (G + 2) * D)
                        o = bank[(3 * b + 2 * t) % 2][:, :] if what == "q" else \
                            bank[(3 * b + 1) % 2][:, t * 2 * D:(t + 1) * 2 * D]
                        last = product(o, (xn_hi[:, k, c], xn_lo[:, k, c]), (qkv_hi[:, ws], qkv_lo[:, ws]),
                                       k == 0, k == KT - 1)
                    return last

                if first:
                    if b == 0:
                        pe.wait_ge(qkv_lo_set, KT * (g + 1))
                    if isinstance(g, int):
                        pe.wait_ge(xn_lo_set, 2 * TILES + 2 * b + 2)
                    if second:
                        pe.wait_ge(q_sin, 2 * u)
                        pe.wait_ge(v_lo_set, u)
                    project(0, "q").then_inc(q_proj, 1)
                    project(0, "kv")
                if second:
                    pe.wait_ge(turned_set, 6 * u)
                    for j in range(3):
                        if j == 0 and third and not (isinstance(u, int) and u < 3):
                            pe.wait_ge(pT_lo_set, 3 * w - 1)
                        if j == 1 and third and not (isinstance(u, int) and u < 3):
                            pe.wait_ge(pT_lo_set, 3 * w)
                        if j == 2:
                            pe.wait_ge(qkT_set, 3 * v + 1)
                        for i in range(4 if j < 2 else 2):
                            src = turned[:, j, i, :, :] if j < 2 else turned[:, i, G, :, :]
                            last = nc.tensor.transpose(bank[2 + j % 2][:, i * P:(i + 1) * P],
                                                       src.rearrange("p a f -> p (a f)"), ident[:])
                        last.then_inc(qk_turned, 1)
                if third:
                    pe.wait_ge(probs_set, 8 * w + 8)
                    for j in range(3):
                        if second and j < 2:
                            pe.wait_ge(qkT_set, 3 * v + 2 + j)
                        if not second and j < 2:
                            pe.wait_ge(pT_lo_set, 3 * w)
                        if j == 2:
                            pe.wait_ge(pT_lo_set, 3 * w + 1)
                        for h in range(G):
                            o = h * P if j == 0 else (G + 2 * h + j - 1) * P
                            last = nc.tensor.transpose(bank[2 + (j + 1) % 2][:, h * P:(h + 1) * P],
                                                       probs[:, o:o + P], ident[:])
                        last.then_inc(pT_done, 1)
                if first:
                    project(1, "kv").then_inc(kv_proj, 1)
                    pe.wait_ge(q_sin, 2 * u + 1)
                    project(1, "q").then_inc(q_proj, 1)
                if third:
                    s = (b - 2) % 4
                    pe.wait_ge(v_lo_set, w + 1)
                    for t in range(2):
                        pe.wait_ge(pT_lo_set, 3 * w + 1 + 2 * t)
                        if not (isinstance(w, int) and w == 0):
                            pe.wait_ge(l_acc, 2 * w - 1 + t)
                        o = bank[6 + t][:, :]
                        if t == 0:
                            last = product(o, (v_hi[:, s, 0, :], v_lo[:, s, 0, :]), (pT_hi[:, 0, :], pT_lo[:, 0, :]),
                                           True, True)
                        else:
                            product(o, (v_hi[:, s, 0, :], v_lo[:, s, 0, :]), (pT_hi[:, 1, :], pT_lo[:, 1, :]),
                                    True, False)
                            last = product(o, (v_hi[:, s, 1, :], v_lo[:, s, 1, :]), (pT_hi[:, 2, :], pT_lo[:, 2, :]),
                                           False, True)
                        last.then_inc(pv_done, 1)
                if second:
                    pe.wait_ge(qkT_set, 3 * v + 3)
                    for j in range(3):
                        o = bank[4 + (3 * (b - 1) + j) % 2]
                        if j == 2:
                            pe.wait_ge(masked_set, 8 * v + G)
                        elif third:
                            pe.wait_ge(masked_set, 8 * w + G + 2 * (j + 1))
                        if j == 0:
                            for h in range(G):
                                last = nc.tensor.matmul(o[:, h * P:(h + 1) * P], qkT[:, h * P:(h + 1) * P],
                                                        qkT[:, 2 * G * P:(2 * G + 1) * P], start=True, stop=True)
                        else:
                            for i in range(2):
                                h = G + 2 * (j - 1) + i
                                last = nc.tensor.matmul(o[:, i * 2 * P:(i + 1) * 2 * P], qkT[:, h * P:(h + 1) * P],
                                                        qkT[:, 2 * G * P:(2 * G + 2) * P], start=True, stop=True)
                        last.then_inc(score_done, 1)
                if third:
                    if b == 2:
                        pe.wait_ge(lwo_lo_set, G * (g + 1))
                    for t in range(2):
                        pe.wait_ge(oT_lo_set, 2 * w + t + 1)
                        for h in range(G):
                            c, n = slice(h * P, (h + 1) * P), slice(h * HID, (h + 1) * HID)
                            last = product(bank[6 + t][:, :], (oT_hi[:, t, c], oT_lo[:, t, c]),
                                           (lwo_hi[:, n], lwo_lo[:, n]), h == 0, h == G - 1)
                        last.then_inc(l_out, 1)

            slots(pe, slot)
            turn(3)

            pe.wait_ge(d_step, 5 * KT)
            for t in range(TILES):
                pe.wait_ge(xn_lo_set, 3 * TILES + t + 1)
                if t >= 4:
                    pe.wait_ge(ln_scaled, TILES + t - 3)
                c = slice(t * P, (t + 1) * P)
                for k in range(KT):
                    last = product(bank[t % 4][:, :], (xn_hi[:, k, c], xn_lo[:, k, c]), (d_hi[:, k, :], d_lo[:, k, :]),
                                   k == 0, k == KT - 1)
                last.then_inc(d_out, 1)


def kernel(**inputs):
    import numpy as np
    import concourse.bacc as bacc
    from concourse.bass_utils import run_bass_kernel_spmd as run

    a = {name: np.asarray(value) for name, value in inputs.items()}

    def by_partition(w, tiles):
        return w.reshape(tiles, P, -1).transpose(1, 0, 2).reshape(P, -1)

    wq = a["L0_attn_Wq"].reshape(KV, G, D, HID)[:, 0]
    a_w = np.stack([np.concatenate([by_partition(wq[h].T, KT), a["L0_attn_M"][h].T], 1) for h in range(KV)])
    a_wo = a["L0_attn_Wo"].T.reshape(KV, G, D, HID).transpose(0, 2, 1, 3).reshape(KV, D, G * HID)
    a_bq = a["L0_attn_bq"].reshape(KV, G, D)[:, 0].T
    gate, up, down = (a[f"L0_ffn_{n}_t"] for n in ("gate", "up", "down"))
    f_w = np.stack([np.concatenate([by_partition(gate[f:f + P].T, KT), by_partition(up[f:f + P].T, KT),
                                    down[:, f:f + P].T], 1) for f in range(0, FF, P)])
    f_scale = np.concatenate([a["L0_ffn_gate_s"].reshape(FT, P).T, a["L0_ffn_up_s"].reshape(FT, P).T], 1)
    wq, wk, wv = (a[f"L1_attn_w{n}"].reshape(KT, P, KV, -1) for n in "qkv")
    l_qkv = np.concatenate([wq, wk, wv], 3).transpose(2, 1, 0, 3).reshape(KV, P, QKV_W)
    l_wo = a["L1_attn_wo"].reshape(KV, G, D, HID).transpose(0, 2, 1, 3).reshape(KV, D, WO_W)
    size = HID // a["L1_ffn_zp"].shape[1]
    half = D // 2
    freq = np.float32(10000.0) ** (-np.arange(half, dtype=np.float32) / np.float32(half))
    angle = np.arange(2 * P, dtype=np.float32)[:, None] * freq[None, :]
    rope = np.stack([np.cos(angle), np.sin(angle)]).reshape(2, 2, P, half).transpose(2, 0, 1, 3).reshape(P, -1)
    i, j = np.arange(P)[:, None], np.arange(P)[None, :]
    low = np.float32(LOWEST)
    mask = np.concatenate([np.where(j > i, np.float32(0), low), np.where(j <= i, np.float32(0), low)], 1)

    arrays = {
        "x_in": a["L0_attn_hidden_states"].reshape(T, HID),
        "a_w": a_w, "a_wo": a_wo, "a_z": a["L0_attn_z"].T, "a_bq": a_bq,
        "f_w": f_w, "f_scale": f_scale, "down_s": np.broadcast_to(a["L0_ffn_down_s"], (P, HID)),
        "l_qkv": l_qkv, "l_wo": l_wo,
        "d_q": a["L1_ffn_weight_q"].T, "d_zp": np.repeat(a["L1_ffn_zp"].T, size, 0),
        "d_scale": np.repeat(a["L1_ffn_scale"].T, size, 0), "d_bias": np.broadcast_to(a["L1_ffn_bias"], (P, HID)),
        "rope": rope.astype(np.float32), "mask": mask.astype(np.float32), "ident_in": np.eye(P, dtype=np.float32),
    }
    arrays = {name: np.ascontiguousarray(value) for name, value in arrays.items()}
    nc = bacc.Bacc("TRN2", target_bir_lowering=False, num_devices=1)
    args = {name: nc.dram_tensor(name, value.shape, mybir.dt.from_np(value.dtype), kind="ExternalInput").ap()
            for name, value in arrays.items()}
    result = nc.dram_tensor("result", (T, HID), F32, kind="ExternalOutput").ap()
    build(nc, out=result, **args)
    r = run(nc, [arrays], core_ids=[0])
    return r.results[0]["result"].reshape(4, 256, HID)
```

```python
from contextlib import ExitStack

import concourse.bass as bass
from concourse import mybir

F32 = mybir.dt.float32
F32R = mybir.dt.float32r
I32 = mybir.dt.int32
ALU = mybir.AluOpType
ACT = mybir.ActivationFunctionType

P = 128
T = 1024
TILES = T // P
HALF = T // 2
HID = 512
CHUNKS = TILES // 2
STEPS = CHUNKS + 2
KT = HID // P
D = 128
KV = 8
G = 4
FF = 1792
FT = FF // P
SCALE = float(D) ** -0.5
LN_EPS = 1e-5
DEN_EPS = 1e-6
LOWEST = -3.4028234663852886e38

A_W = KT * D + D
F_W = 2 * KT * P + HID
QKV_W = KT * (G + 2) * D
WO_W = G * HID
A_FLOATS = 6 * A_W + 8 * HID + 3 * HID + 8 * HID + KV + KV * P + P + 5 * T + 2 * TILES + 64
DEN_STEP = 48


def build(nc, x_in, a_w, a_wo, a_z, a_bq, f_w, f_scale, down_s, l_qkv, l_wo, d_q, d_zp, d_scale, d_bias,
          rope, mask, ident_in, out):
    with ExitStack() as ctx:
        def sem(name):
            return ctx.enter_context(nc.semaphore(name))

        def sb(stack, name, shape, dt=F32):
            return stack.enter_context(nc.sbuf_tensor(name, shape, dt))

        x = sb(ctx, "x", [P, TILES, HID])
        acc = sb(ctx, "acc", [P, TILES, HID])
        xn_hi = sb(ctx, "xn_hi", [P, KT, T], F32R)
        xn_lo = sb(ctx, "xn_lo", [P, KT, T], F32R)
        ident = sb(ctx, "ident", [P, P])
        bq = sb(ctx, "bq", [P, KV])
        fsc = sb(ctx, "fsc", [P, 2, FT])
        down_row = sb(ctx, "down_row", [P, HID])
        cos_sin = sb(ctx, "cos_sin", [P, 2, 2, D // 2])
        masks = sb(ctx, "masks", [P, 2 * P])
        stats = sb(ctx, "stats", [P, TILES, 6])
        mean_var = sb(ctx, "mean_var", [P, TILES, 2])
        stats2 = sb(ctx, "stats2", [P, TILES, 6])
        mean_var2 = sb(ctx, "mean_var2", [P, TILES, 2])
        var_eps = sb(ctx, "var_eps", [P, 2, TILES])
        rstd = sb(ctx, "rstd", [P, 2, TILES])
        minus_half = sb(ctx, "minus_half", [P, 2])
        shift = sb(ctx, "shift", [P, 2, TILES])

        with ExitStack() as part:
            a_raw = sb(part, "a_raw", [P, 2, A_W])
            a_hi = sb(part, "a_hi", [P, 2, A_W], F32R)
            a_lo = sb(part, "a_lo", [P, 2, A_W], F32R)
            wo_raw = sb(part, "wo_raw", [P, 2, G, HID])
            wo_pair = sb(part, "wo_pair", [P, 2, HID])
            wo_sum = sb(part, "wo_sum", [P, HID])
            wos_hi = sb(part, "wos_hi", [P, 2, HID], F32R)
            wos_lo = sb(part, "wos_lo", [P, 2, HID], F32R)
            mw_hi = sb(part, "mw_hi", [P, 2, HID], F32R)
            mw_lo = sb(part, "mw_lo", [P, 2, HID], F32R)
            z_col = sb(part, "z_col", [P, KV])
            z_rep = sb(part, "z_rep", [P, KV, P])
            zeros = sb(part, "zeros", [P, P])
            expq = sb(part, "expq", [P, T])
            reluq = sb(part, "reluq", [P, T])
            sq = sb(part, "sq", [P, T])
            sq_hi = sb(part, "sq_hi", [P, T], F32R)
            sq_lo = sb(part, "sq_lo", [P, T], F32R)
            den_eps = sb(part, "den_eps", [P, TILES])
            rden = sb(part, "rden", [P, TILES])
        with ExitStack() as part:
            silu = sb(part, "silu", [P, T])
            hid = sb(part, "hid", [P, 2, T])
            hid_hi = sb(part, "hid_hi", [P, 2, T], F32R)
            hid_lo = sb(part, "hid_lo", [P, 2, T], F32R)
            f_odd_hi = sb(part, "f_odd_hi", [P, 2, F_W], F32R)
            f_odd_lo = sb(part, "f_odd_lo", [P, 2, F_W], F32R)
            sb(part, "behind_linear_attention", [P, A_FLOATS - 5 * T - 2 * T - 4 * F_W])
            f_raw = sb(part, "f_raw", [P, 2, F_W], I32)
            f_even_hi = sb(part, "f_even_hi", [P, 2, F_W], F32R)
            f_even_lo = sb(part, "f_even_lo", [P, 2, F_W], F32R)
        f_hi, f_lo = (f_even_hi, f_odd_hi), (f_even_lo, f_odd_lo)
        def in_place(stack, name, width):
            with ExitStack() as raw_part:
                raw = sb(raw_part, name + "_raw", [P, width])
            return raw, sb(stack, name + "_lo", [P, width], F32R)

        with ExitStack() as part:
            qkv_odd_hi = sb(part, "qkv_odd_hi", [P, QKV_W], F32R)
            qkv_odd_raw, qkv_odd_lo = in_place(part, "qkv_odd", QKV_W)
            lwo_even_hi = sb(part, "lwo_even_hi", [P, WO_W], F32R)
            lwo_even_raw, lwo_even_lo = in_place(part, "lwo_even", WO_W)
            lwo_odd_hi = sb(part, "lwo_odd_hi", [P, WO_W], F32R)
            lwo_odd_raw, lwo_odd_lo = in_place(part, "lwo_odd", WO_W)
            by_cos = sb(part, "by_cos", [P, 2, G + 1, 2, D // 2])
            by_sin = sb(part, "by_sin", [P, 2, G + 1, 2, D // 2])
            turned = sb(part, "turned", [P, 2, G + 1, 2, D // 2])
            qkT = sb(part, "qkT", [P, (2 * G + 2) * P])
            v_hi = sb(part, "v_hi", [P, 4, 2, D], F32R)
            v_lo = sb(part, "v_lo", [P, 4, 2, D], F32R)
            probs = sb(part, "probs", [P, 3 * G * P])
            row_max = sb(part, "row_max", [P, 2 * G])
            neg_max = sb(part, "neg_max", [P, 2 * G])
            row_sum = sb(part, "row_sum", [P, 2 * G])
            row_inv = sb(part, "row_inv", [P, 2 * G])
            pT_hi = sb(part, "pT_hi", [P, 3, G * P], F32R)
            pT_lo = sb(part, "pT_lo", [P, 3, G * P], F32R)
            oT_hi = sb(part, "oT_hi", [P, 2, G * P], F32R)
            oT_lo = sb(part, "oT_lo", [P, 2, G * P], F32R)
            bias_row = sb(part, "bias_row", [P, HID])
            used = HID + 2 * QKV_W + 4 * WO_W + 3 * 2 * (G + 1) * D + (2 * G + 2) * P + 8 * 2 * D + 3 * G * P \
                + 8 * G + 6 * G * P + 4 * G * P
            assert used <= A_FLOATS + 6 * F_W
            sb(part, "behind_ffn", [P, A_FLOATS + 6 * F_W - used])
            with ExitStack() as first_set:
                qkv_even_hi = sb(first_set, "qkv_even_hi", [P, QKV_W], F32R)
                qkv_even_raw, qkv_even_lo = in_place(first_set, "qkv_even", QKV_W)
            d_hi = sb(part, "d_hi", [P, KT, HID], F32R)
            d_lo = sb(part, "d_lo", [P, KT, HID], F32R)
            dq_raw = sb(part, "dq_raw", [P, HID], I32)
            dzp_raw = sb(part, "dzp_raw", [P, HID])
            dsc_raw = sb(part, "dsc_raw", [P, HID])
            dq_f = sb(part, "dq_f", [P, HID])
        qkv_hi, qkv_raw, qkv_lo = (qkv_even_hi, qkv_odd_hi), (qkv_even_raw, qkv_odd_raw), (qkv_even_lo, qkv_odd_lo)
        lwo_hi, lwo_raw, lwo_lo = (lwo_even_hi, lwo_odd_hi), (lwo_even_raw, lwo_odd_raw), (lwo_even_lo, lwo_odd_lo)

        bank = [ctx.enter_context(nc.psum_tensor(f"bank{i}", [P, 512], F32)) for i in range(8)]

        early_consts_in = sem("early_consts_in")
        late_consts_in = sem("late_consts_in")
        bias_in = sem("bias_in")
        x_loaded = [sem(f"x_loaded{t}") for t in range(TILES)]
        consts_set = sem("consts_set")
        z_set = sem("z_set")
        ln_biased = sem("ln_biased")
        down_scaled = sem("down_scaled")
        ln_stats = sem("ln_stats")
        ln_mean = sem("ln_mean")
        ln_var = sem("ln_var")
        ln_rstd = sem("ln_rstd")
        ln_shift = sem("ln_shift")
        ln_out = sem("ln_out")
        x_added = sem("x_added")
        ln2_stats = sem("ln2_stats")
        ln2_mean = sem("ln2_mean")
        ln2_var = sem("ln2_var")
        ln2_rstd = sem("ln2_rstd")
        ln2_shift = sem("ln2_shift")
        xn_ready = sem("xn_ready")
        xn_turned = sem("xn_turned")
        xn_hi_set = sem("xn_hi_set")
        xn_lo_set = sem("xn_lo_set")
        acc_zero = sem("acc_zero")
        a_loaded = [sem(f"a_loaded{s}") for s in range(2)]
        wo_loaded = [sem(f"wo_loaded{s}") for s in range(2)]
        a_hi_set = sem("a_hi_set")
        a_lo_set = sem("a_lo_set")
        wo_pairs = sem("wo_pairs")
        wo_summed = sem("wo_summed")
        wos_hi_set = sem("wos_hi_set")
        wos_lo_set = sem("wos_lo_set")
        a_proj = sem("a_proj")
        a_exp = sem("a_exp")
        a_relu = sem("a_relu")
        sq_set = sem("sq_set")
        sq_hi_set = sem("sq_hi_set")
        sq_lo_set = sem("sq_lo_set")
        mw_done = sem("mw_done")
        mw_hi_set = sem("mw_hi_set")
        mw_lo_set = sem("mw_lo_set")
        den_done = sem("den_done")
        den_read = sem("den_read")
        rden_set = sem("rden_set")
        a_out = sem("a_out")
        a_acc = sem("a_acc")
        f_loaded = [sem(f"f_loaded{s}") for s in range(2)]
        f_hi_set = sem("f_hi_set")
        f_lo_set = sem("f_lo_set")
        f_gate = sem("f_gate")
        f_up = sem("f_up")
        silu_set = sem("silu_set")
        hid_set = sem("hid_set")
        hid_hi_set = sem("hid_hi_set")
        hid_lo_set = sem("hid_lo_set")
        f_down = sem("f_down")
        f_acc = sem("f_acc")
        d_loaded = sem("d_loaded")
        d_step = sem("d_step")
        qkv_loaded = [sem(f"qkv_loaded{s}") for s in range(2)]
        lwo_loaded = [sem(f"lwo_loaded{s}") for s in range(2)]
        qkv_hi_set = sem("qkv_hi_set")
        qkv_lo_set = sem("qkv_lo_set")
        lwo_hi_set = sem("lwo_hi_set")
        lwo_lo_set = sem("lwo_lo_set")
        q_proj = sem("q_proj")
        kv_proj = sem("kv_proj")
        q_cos = sem("q_cos")
        q_sin = sem("q_sin")
        k_cos = sem("k_cos")
        k_sin = sem("k_sin")
        turned_set = sem("turned_set")
        qk_turned = sem("qk_turned")
        qkT_set = sem("qkT_set")
        v_hi_set = sem("v_hi_set")
        v_lo_set = sem("v_lo_set")
        score_done = sem("score_done")
        masked_set = sem("masked_set")
        neg_max_set = sem("neg_max_set")
        exp_set = sem("exp_set")
        row_inv_set = sem("row_inv_set")
        probs_set = sem("probs_set")
        pT_done = sem("pT_done")
        pT_hi_set = sem("pT_hi_set")
        pT_lo_set = sem("pT_lo_set")
        pv_done = sem("pv_done")
        oT_hi_set = sem("oT_hi_set")
        oT_lo_set = sem("oT_lo_set")
        l_out = sem("l_out")
        l_acc = sem("l_acc")
        d_out = sem("d_out")
        stored = sem("stored")

        waits_passed = sem("waits_passed")

        def slots(eng, slot):
            for b in range(4):
                slot(0, 0, b, True, b >= 1, b >= 2)
            with eng.Fori(0, (KV - 2) // 2) as i:
                for s in range(2):
                    for b in range(4):
                        slot(2 * i + 1 + s, (1 + s) % 2, b, True, True, True)
            for b in range(4):
                slot(KV - 1, (KV - 1) % 2, b, True, True, True)
            slot(KV, KV % 2, 0, False, True, True)
            slot(KV, KV % 2, 1, False, False, True)

        def wait_apart(eng, semaphore, value):
            eng.wait_ge(semaphore, value)
            if not isinstance(value, int):
                eng.sem_inc(waits_passed, 1)

        block = ctx.enter_context(nc.Block())

        @block.sync
        def _(sync):
            def load_x(t):
                sync.dma_start(x[:, t, :], x_in[t * P:(t + 1) * P, :]).then_inc(x_loaded[t], 16)

            def load_a(h, s):
                sync.dma_start(a_raw[:, s, :], a_w[bass.ds(h, 1), :, :].rearrange("a p n -> p (a n)"))\
                    .then_inc(a_loaded[s], 16)

            def load_wo(h, s):
                sync.dma_start(wo_raw[:, s, :, :].rearrange("p g n -> p (g n)"),
                               a_wo[bass.ds(h, 1), :, :].rearrange("a p n -> p (a n)")).then_inc(wo_loaded[s], 16)

            for t in range(4):
                load_x(t)
            sync.dma_start(ident[:], ident_in).then_inc(early_consts_in, 16)
            sync.dma_start(bq[:], a_bq).then_inc(early_consts_in, 16)
            sync.dma_start(z_col[:], a_z).then_inc(early_consts_in, 16)
            load_a(0, 0)
            for t in range(4, TILES):
                load_x(t)
            load_wo(0, 0)
            load_a(1, 1)
            load_wo(1, 1)

            def load_slice(f, s):
                sync.dma_start(f_raw[:, s, :], f_w[bass.ds(f, 1), :, :].rearrange("a p n -> p (a n)"))\
                    .then_inc(f_loaded[s], 16)

            for s in range(2):
                load_slice(s, s)
            sync.dma_start(fsc[:].rearrange("p a f -> p (a f)"), f_scale).then_inc(late_consts_in, 16)
            sync.dma_start(down_row[:], down_s).then_inc(late_consts_in, 16)
            sync.dma_start(cos_sin[:].rearrange("p a b f -> p (a b f)"), rope).then_inc(late_consts_in, 16)
            sync.dma_start(masks[:], mask).then_inc(late_consts_in, 16)

            def load_qkv(g, s):
                sync.dma_start(qkv_raw[s][:], l_qkv[bass.ds(g, 1), :, :].rearrange("a p n -> p (a n)"))\
                    .then_inc(qkv_loaded[s], 16)

            def load_lwo(g, s):
                sync.dma_start(lwo_raw[s][:], l_wo[bass.ds(g, 1), :, :].rearrange("a p n -> p (a n)"))\
                    .then_inc(lwo_loaded[s], 16)

            load_qkv(0, 0)
            with sync.Fori(1, KV // 2) as i:
                for s in range(2):
                    sync.wait_ge(a_lo_set, 2 * i + s - 1)
                    load_a(2 * i + s, s)
                    sync.wait_ge(wo_pairs, 2 * i + s - 1)
                    load_wo(2 * i + s, s)
            with sync.Fori(1, FT // 2) as i:
                for s in range(2):
                    sync.wait_ge(f_lo_set, 2 * i + s - 1)
                    load_slice(2 * i + s, s)
            sync.wait_ge(f_acc, TILES * (FT // 2))
            load_lwo(0, 0)
            load_qkv(1, 1)
            load_lwo(1, 1)
            sync.dma_start(bias_row[:], d_bias).then_inc(bias_in, 16)

            def load_group(g, s):
                sync.wait_ge(q_proj, 8 * (g - 1))
                load_qkv(g, s)
                sync.wait_ge(l_out, 8 * (g - 1))
                load_lwo(g, s)

            with sync.Fori(1, (KV - 2) // 2 + 1) as i:
                for s in range(2):
                    load_group(2 * i + s, s)
            sync.wait_ge(q_proj, 8 * (KV - 1))
            for k in range(KT):
                if k:
                    sync.wait_ge(d_step, 5 * k)
                for dst, src in ((dq_raw, d_q), (dzp_raw, d_zp), (dsc_raw, d_scale)):
                    sync.dma_start(dst[:], src[k * P:(k + 1) * P, :]).then_inc(d_loaded, 16)
            for t in range(TILES):
                sync.wait_ge(x_added, 3 * TILES + t + 1)
                sync.dma_start(out[t * P:(t + 1) * P, :], x[:, t, :]).then_inc(stored, 16)
            sync.wait_ge(stored, 16 * TILES)

        @block.gpsimd
        def _(pool):
            nc.gpsimd.memset(minus_half[:], -0.5).then_inc(consts_set, 1)
            nc.gpsimd.memset(zeros[:], 0.0).then_inc(consts_set, 1)

            def norm_step(k, s):
                if k and s < CHUNKS:
                    two = slice(2 * s, 2 * s + 2)
                    if k == 2:
                        for t in (2 * s, 2 * s + 1):
                            pool.wait_ge(f_acc, TILES * (FT // 2 - 1) + t + 1)
                            nc.gpsimd.tensor_tensor(acc[:, t, :], acc[:, t, :], down_row[:], ALU.mult)\
                                .then_inc(down_scaled, 1)
                    pool.wait_ge(ln_var, (k - 1) * CHUNKS + s + 1)
                    nc.gpsimd.tensor_tensor(rstd[:, 0, two], var_eps[:, 0, two], minus_half[:], ALU.pow)\
                        .then_inc(ln_rstd, 1)
                if k < 4 and 0 <= s - 1 < CHUNKS:
                    two = slice(2 * s - 2, 2 * s)
                    pool.wait_ge(ln2_var, k * CHUNKS + s)
                    nc.gpsimd.tensor_tensor(rstd[:, 1, two], var_eps[:, 1, two], minus_half[:], ALU.pow)\
                        .then_inc(ln2_rstd, 1)
                if k and s < CHUNKS:
                    for t in (2 * s, 2 * s + 1):
                        pool.wait_ge(ln_out, (k - 1) * TILES + t + 1)
                        nc.gpsimd.tensor_tensor(x[:, t, :], x[:, t, :], acc[:, t, :], ALU.add).then_inc(x_added, 1)

            def norm(k):
                for s in range(STEPS):
                    norm_step(k, s)

            def clear_acc(k):
                for t in range(TILES):
                    pool.wait_ge(xn_turned, k * TILES + t + 1)
                    nc.gpsimd.memset(acc[:, t, :], 0.0).then_inc(acc_zero, 1)

            pool.wait_ge(consts_set, 2)
            norm(0)

            def prepare_head(h, s, first):
                wait_apart(pool, a_loaded[s], 16 * (h // 2 + 1) if first else 16 * h[1])
                hh = h if first else h[0]
                if not first:
                    wait_apart(pool, mw_done, hh - 1)
                    wait_apart(pool, a_proj, 2 * hh - 2)
                nc.gpsimd.tensor_scalar(a_hi[:, s, :], a_raw[:, s, :], 1.0, 1.0, ALU.mult, ALU.mult)\
                    .then_inc(a_hi_set, 1)
                pool.wait_ge(a_hi_set, hh + 1)
                nc.gpsimd.tensor_tensor(a_lo[:, s, :], a_raw[:, s, :], a_hi[:, s, :].bitcast(F32), ALU.subtract)\
                    .then_inc(a_lo_set, 1)
                pool.wait_ge(wo_loaded[s], 16 * (h // 2 + 1) if first else 16 * h[1])
                if not (first and h == 0):
                    pool.wait_ge(wo_summed, hh)
                nc.gpsimd.tensor_tensor(wo_pair[:], wo_raw[:, s, 0:2, :], wo_raw[:, s, 2:4, :], ALU.add)\
                    .then_inc(wo_pairs, 1)
                pool.wait_ge(wo_pairs, hh + 1)
                if not (first and h == 0):
                    pool.wait_ge(wos_lo_set, hh)
                nc.gpsimd.tensor_tensor(wo_sum[:], wo_pair[:, 0, :], wo_pair[:, 1, :], ALU.add).then_inc(wo_summed, 1)
                wait_apart(pool, wo_summed, hh + 1)
                nc.gpsimd.tensor_scalar(wos_hi[:, s, :], wo_sum[:], 1.0, 1.0, ALU.mult, ALU.mult)\
                    .then_inc(wos_hi_set, 1)
                pool.wait_ge(wos_hi_set, hh + 1)
                nc.gpsimd.tensor_tensor(wos_lo[:, s, :], wo_sum[:], wos_hi[:, s, :].bitcast(F32), ALU.subtract)\
                    .then_inc(wos_lo_set, 1)

            prepare_head(0, 0, True)
            for h in range(KV):
                nc.gpsimd.tensor_scalar(z_rep[:, h, :], zeros[:], 1.0, z_col[:, h:h + 1], ALU.mult, ALU.add)\
                    .then_inc(z_set, 1)
            clear_acc(0)
            prepare_head(1, 1, True)

            def split_slice(f, s, odd, loads, used):
                pool.wait_ge(f_loaded[s], 16 * loads)
                if used is not None:
                    wait_apart(pool, f_down, used)
                nc.gpsimd.tensor_scalar(f_hi[odd][:, s, :], f_raw[:, s, :], 1.0, 1.0, ALU.mult, ALU.mult)\
                    .then_inc(f_hi_set, 1)

            for s in range(2):
                split_slice(s, s, 0, 1, None)
            with pool.Fori(1, KV // 2) as i:
                for s in range(2):
                    prepare_head((2 * i + s, i + 1), s, False)

            def split_qkv(g, s, k):
                wait_apart(pool, qkv_loaded[s], 8 * (g - s) + 16)
                c = slice(k * QKV_W // KT, (k + 1) * QKV_W // KT)
                nc.gpsimd.tensor_scalar(qkv_hi[s][:, c], qkv_raw[s][:, c], 1.0, 1.0, ALU.mult, ALU.mult)\
                    .then_inc(qkv_hi_set, 1)

            for k in range(KT):
                split_qkv(0, 0, k)
            norm(1)
            for s in range(2):
                split_slice(2 + s, s, 1, 2, None)
            clear_acc(1)

            def split_pair(p, odd, used):
                for s in range(2):
                    wait_apart(pool, f_loaded[s], 16 * (p + 1))
                    wait_apart(pool, f_down, used)
                    nc.gpsimd.tensor_scalar(f_hi[odd][:, s, :], f_raw[:, s, :], 1.0, 1.0, ALU.mult, ALU.mult)\
                        .then_inc(f_hi_set, 1)

            split_pair(2, 0, TILES)
            with pool.Fori(1, 3) as i:
                for odd in (1, 0):
                    split_pair(2 * i + 2 - odd, odd, TILES * (2 * i + 1 - odd))
            norm(2)
            clear_acc(2)

            def slot(g, parity, b, first, second, third):
                u = 4 * g + b
                last_group = isinstance(g, int) and g == KV - 1
                if first:
                    if second:
                        pool.wait_ge(qk_turned, 3 * u)

                    def turn_pairs(t, which, wait):
                        pool.wait_ge(*wait)
                        nc.gpsimd.tensor_tensor(turned[:, t, which, 0, :], by_cos[:, t, which, 0, :],
                                                by_sin[:, t, which, 1, :], ALU.subtract).then_inc(turned_set, 1)
                        nc.gpsimd.tensor_tensor(turned[:, t, which, 1, :], by_sin[:, t, which, 0, :],
                                                by_cos[:, t, which, 1, :], ALU.add).then_inc(turned_set, 1)

                    turn_pairs(0, slice(0, G), (q_sin, 2 * u + 1))
                    turn_pairs(slice(0, 2), G, (k_sin, u + 1))
                    turn_pairs(1, slice(0, G), (q_sin, 2 * u + 2))
                if first and b < 2:
                    for h in (2 * b, 2 * b + 1):
                        wait_apart(pool, lwo_loaded[parity], 8 * (g - parity) + 16)
                        c = slice(h * HID, (h + 1) * HID)
                        nc.gpsimd.tensor_scalar(lwo_hi[parity][:, c], lwo_raw[parity][:, c], 1.0, 1.0,
                                                ALU.mult, ALU.mult).then_inc(lwo_hi_set, 1)
                if first and not last_group:
                    split_qkv(g + 1, 1 - parity, b)
                if last_group:
                    k = b
                    pool.wait_ge(d_loaded, 48 * (k + 1))
                    nc.gpsimd.tensor_scalar(dq_f[:], dq_raw[:], 1.0, 1.0, ALU.mult, ALU.mult).then_inc(d_step, 1)
                    pool.wait_ge(d_step, 5 * k + 1)
                    nc.gpsimd.tensor_tensor(dq_f[:], dq_f[:], dzp_raw[:], ALU.subtract).then_inc(d_step, 1)
                    pool.wait_ge(d_step, 5 * k + 2)
                    nc.gpsimd.tensor_tensor(dq_f[:], dq_f[:], dsc_raw[:], ALU.mult).then_inc(d_step, 1)
                    pool.wait_ge(d_step, 5 * k + 3)
                    nc.gpsimd.tensor_scalar(d_hi[:, k, :], dq_f[:], 1.0, 1.0, ALU.mult, ALU.mult).then_inc(d_step, 1)
                    pool.wait_ge(d_step, 5 * k + 4)
                    nc.gpsimd.tensor_tensor(d_lo[:, k, :], dq_f[:], d_hi[:, k, :].bitcast(F32), ALU.subtract)\
                        .then_inc(d_step, 1)
                if second:
                    wait_apart(pool, row_inv_set, u)
                    for j in range(2 * G):
                        c = slice(j * P, (j + 1) * P) if j < G else slice((2 * j - G) * P, (2 * j - G + 2) * P)
                        nc.gpsimd.tensor_scalar(probs[:, c], probs[:, c], row_inv[:, j:j + 1], 1.0,
                                                ALU.mult, ALU.mult).then_inc(probs_set, 1)
                if third and isinstance(u, int) and u - 2 >= 4 * (KV - 1):
                    norm_step(3, u - 2 - 4 * (KV - 1))

            slots(pool, slot)
            for s in range(CHUNKS, STEPS):
                norm_step(3, s)
            norm(4)

        @block.scalar
        def _(act):
            def norm_step(k, s):
                if k < 4 and 0 <= s - 2 < CHUNKS:
                    for t in (2 * s - 4, 2 * s - 3):
                        act.wait_ge(xn_turned, k * TILES + t + 1)
                        nc.scalar.activation(xn_hi[:, :, t * P:(t + 1) * P],
                                             bank[4 + t % 4][:, :].rearrange("p (k c) -> p k c", k=KT), ACT.Copy)\
                            .then_inc(xn_hi_set, 1)
                if k and s < CHUNKS:
                    act.wait_ge(ln_shift, (k - 1) * CHUNKS + s + 1)
                    for t in (2 * s, 2 * s + 1):
                        nc.scalar.activation(acc[:, t, :], acc[:, t, :], ACT.Identity, bias=shift[:, 0, t:t + 1],
                                             scale=rstd[:, 0, t:t + 1]).then_inc(ln_out, 1)
                if k < 4 and 0 <= s - 1 < CHUNKS:
                    act.wait_ge(ln2_shift, k * CHUNKS + s)
                    for t in (2 * s - 2, 2 * s - 1):
                        nc.scalar.activation(acc[:, t, :], x[:, t, :], ACT.Identity, bias=shift[:, 1, t:t + 1],
                                             scale=rstd[:, 1, t:t + 1]).then_inc(xn_ready, 1)

            def norm(k):
                for s in range(STEPS):
                    norm_step(k, s)

            norm(0)
            act.wait_ge(early_consts_in, 16 * 3)

            def head(h, s, first):
                def mw():
                    act.wait_ge(mw_done, h + 1)
                    nc.scalar.activation(mw_hi[:, s, :], bank[2 + s][:, :], ACT.Copy).then_inc(mw_hi_set, 1)

                if not first:
                    mw()
                for j in range(2):
                    c = slice(j * HALF, (j + 1) * HALF)
                    wait_apart(act, a_proj, 2 * h + j + 1)
                    if not first:
                        wait_apart(act, sq_set, 2 * h + j - 1)
                    nc.scalar.activation(expq[:, c], bank[j][:, :], ACT.Exp, bias=bq[:, bass.ds(h, 1)])\
                        .then_inc(a_exp, 1)
                    nc.scalar.activation(reluq[:, c], bank[j][:, :], ACT.Relu, bias=bq[:, bass.ds(h, 1)])\
                        .then_inc(a_relu, 1)
                    act.wait_ge(sq_set, 2 * h + j + 1)
                    if not first:
                        act.wait_ge(a_out, 8 * h - 4 + 4 * j)
                    nc.scalar.activation(sq_hi[:, c], sq[:, c], ACT.Copy).then_inc(sq_hi_set, 1)
                if first:
                    mw()

            head(0, 0, True)
            head(1, 1, False)
            with act.Fori(1, KV // 2) as i:
                for s in range(2):
                    head(2 * i + s, s, False)
            norm(1)
            act.wait_ge(late_consts_in, 16 * 4)

            def slice_(f, s, pair, first):
                for j in range(2):
                    c = slice(j * HALF, (j + 1) * HALF)
                    wait_apart(act, f_gate, 2 * f + j + 1)
                    if not (first and s == 0):
                        wait_apart(act, hid_set, 2 * f + j - 1)
                    nc.scalar.activation(silu[:, c], bank[j][:, :], ACT.Silu, scale=fsc[:, 0, bass.ds(f, 1)])\
                        .then_inc(silu_set, 1)
                    act.wait_ge(hid_set, 2 * f + j + 1)
                    if not first:
                        act.wait_ge(f_down, 8 * pair - 4 + 4 * j)
                    nc.scalar.activation(hid_hi[:, s, c], hid[:, s, c], ACT.Copy).then_inc(hid_hi_set, 1)

            for s in range(2):
                slice_(s, s, 0, True)
            with act.Fori(1, FT // 2) as i:
                for s in range(2):
                    slice_(2 * i + s, s, i, False)
            norm(2)

            def slot(g, parity, b, first, second, third):
                u = 4 * g + b
                v, w = u - 1, u - 2

                def pT(j):
                    act.wait_ge(pT_done, 3 * w + j + 1)
                    if not (isinstance(w, int) and w == 0):
                        act.wait_ge(pv_done, 2 * w)
                    nc.scalar.activation(pT_hi[:, j, :], bank[2 + (j + 1) % 2][:, :], ACT.Copy).then_inc(pT_hi_set, 1)

                def oT(t):
                    act.wait_ge(pv_done, 2 * w + t + 1)
                    if not (isinstance(w, int) and w == 0):
                        act.wait_ge(l_out, 2 * w)
                    nc.scalar.activation(oT_hi[:, t, :], bank[6 + t][:, :], ACT.Copy).then_inc(oT_hi_set, 1)

                def exps(t):
                    act.wait_ge(neg_max_set, 2 * v + t + 1)
                    for j in range(t * G, (t + 1) * G):
                        c = slice(j * P, (j + 1) * P) if j < G else slice((2 * j - G) * P, (2 * j - G + 2) * P)
                        if j == 0 and third:
                            act.wait_ge(row_inv_set, v)
                        nc.scalar.activation(probs[:, c], probs[:, c], ACT.Exp, bias=neg_max[:, j:j + 1],
                                             scale=SCALE, accum_out=row_sum[:, j:j + 1]).then_inc(exp_set, 1)

                if second:
                    for j in range(3):
                        act.wait_ge(qk_turned, 3 * v + j + 1)
                        if third:
                            act.wait_ge(score_done, 3 * v)
                        n = 512 if j < 2 else 256
                        nc.scalar.activation(qkT[:, j * 512:j * 512 + n], bank[2 + j % 2][:, 0:n], ACT.Copy)\
                            .then_inc(qkT_set, 1)
                if third:
                    pT(0)
                    pT(1)
                if first:
                    act.wait_ge(kv_proj, u + 1)
                    if not (isinstance(g, int) and g == 0):
                        act.wait_ge(pv_done, 2 * (u - 3))
                    kv = bank[(3 * b + 1) % 2][:, :].rearrange("p (t a d) -> p t a d", t=2, a=2)
                    act.wait_ge(k_sin, u + 1)
                    nc.scalar.activation(v_hi[:, b, :, :], kv[:, :, 1, :], ACT.Copy).then_inc(v_hi_set, 1)
                if third:
                    pT(2)
                    oT(0)
                if second:
                    exps(0)
                if third:
                    oT(1)
                if second:
                    exps(1)
                if third and isinstance(u, int) and u - 2 >= 4 * (KV - 1):
                    norm_step(3, u - 2 - 4 * (KV - 1))

            slots(act, slot)
            for s in range(CHUNKS, STEPS):
                norm_step(3, s)
            norm(4)

        @block.vector
        def _(dve):
            def norm_step(k, s):
                if k and s < CHUNKS:
                    for t in (2 * s, 2 * s + 1):
                        if k == 1:
                            dve.wait_ge(a_acc, TILES * (KV - 1) + t + 1)
                        if k == 2:
                            dve.wait_ge(down_scaled, t + 1)
                        if k == 3:
                            dve.wait_ge(l_acc, TILES * (KV - 1) + t + 1)
                        if k == 4:
                            dve.wait_ge(d_out, t + 1)
                            nc.vector.tensor_tensor(acc[:, t, :], bank[t % 4][:, :], bias_row[:], ALU.add)\
                                .then_inc(ln_biased, 1)
                            dve.wait_ge(ln_biased, t + 1)
                        nc.vector.bn_stats(stats[:, t, :], acc[:, t, :]).then_inc(ln_stats, 1)
                    for t in (2 * s, 2 * s + 1):
                        dve.wait_ge(ln_stats, (k - 1) * TILES + t + 1)
                        nc.vector.bn_aggr(mean_var[:, t, :], stats[:, t, :]).then_inc(ln_mean, 1)
                    dve.wait_ge(ln_mean, (k - 1) * TILES + 2 * s + 2)
                    nc.vector.tensor_scalar(var_eps[:, 0, 2 * s:2 * s + 2], mean_var[:, 2 * s:2 * s + 2, 1],
                                            LN_EPS, None, ALU.add).then_inc(ln_var, 1)
                if k < 4 and 0 <= s - 1 < CHUNKS:
                    for t in (2 * s - 2, 2 * s - 1):
                        if k:
                            dve.wait_ge(x_added, (k - 1) * TILES + t + 1)
                        else:
                            dve.wait_ge(x_loaded[t], 16)
                        nc.vector.bn_stats(stats2[:, t, :], x[:, t, :]).then_inc(ln2_stats, 1)
                    for t in (2 * s - 2, 2 * s - 1):
                        dve.wait_ge(ln2_stats, k * TILES + t + 1)
                        nc.vector.bn_aggr(mean_var2[:, t, :], stats2[:, t, :]).then_inc(ln2_mean, 1)
                    dve.wait_ge(ln2_mean, k * TILES + 2 * s)
                    nc.vector.tensor_scalar(var_eps[:, 1, 2 * s - 2:2 * s], mean_var2[:, 2 * s - 2:2 * s, 1],
                                            LN_EPS, None, ALU.add).then_inc(ln2_var, 1)
                if k and s < CHUNKS:
                    dve.wait_ge(ln_rstd, (k - 1) * CHUNKS + s + 1)
                    two = slice(2 * s, 2 * s + 2)
                    nc.vector.scalar_tensor_tensor(out=shift[:, 0, two], in0=mean_var[:, two, 0], scalar=-1.0,
                                                   in1=rstd[:, 0, two], op0=ALU.mult, op1=ALU.mult)\
                        .then_inc(ln_shift, 1)
                if k < 4 and 0 <= s - 1 < CHUNKS:
                    dve.wait_ge(ln2_rstd, k * CHUNKS + s)
                    two = slice(2 * s - 2, 2 * s)
                    nc.vector.scalar_tensor_tensor(out=shift[:, 1, two], in0=mean_var2[:, two, 0], scalar=-1.0,
                                                   in1=rstd[:, 1, two], op0=ALU.mult, op1=ALU.mult)\
                        .then_inc(ln2_shift, 1)
                if k < 4 and 0 <= s - 2 < CHUNKS:
                    for t in (2 * s - 4, 2 * s - 3):
                        dve.wait_ge(xn_hi_set, k * TILES + t + 1)
                        c = slice(t * P, (t + 1) * P)
                        nc.vector.tensor_tensor(xn_lo[:, :, c], bank[4 + t % 4][:, :].rearrange("p (k c) -> p k c", k=KT),
                                                xn_hi[:, :, c].bitcast(F32), ALU.subtract).then_inc(xn_lo_set, 1)

            for s in range(STEPS):
                norm_step(0, s)

            def head(h, s, first, last):
                def mw():
                    dve.wait_ge(mw_hi_set, h + 1)
                    nc.vector.tensor_tensor(mw_lo[:, s, :], bank[2 + s][:, :], mw_hi[:, s, :].bitcast(F32),
                                            ALU.subtract).then_inc(mw_lo_set, 1)

                if not first:
                    mw()
                for j in range(2):
                    c = slice(j * HALF, (j + 1) * HALF)
                    dve.wait_ge(a_relu, 2 * h + j + 1)
                    if not first:
                        dve.wait_ge(sq_lo_set, 2 * h + j - 1)
                        dve.wait_ge(sq_hi_set, 2 * h + j - 1)
                        dve.wait_ge(a_out, 8 * h - 4 + 4 * j)
                    nc.vector.scalar_tensor_tensor(out=sq[:, c], in0=expq[:, c], scalar=1.0, in1=reluq[:, c],
                                                   op0=ALU.min, op1=ALU.add).then_inc(sq_set, 1)
                    dve.wait_ge(sq_hi_set, 2 * h + j + 1)
                    nc.vector.tensor_tensor(sq_lo[:, c], sq[:, c], sq_hi[:, c].bitcast(F32), ALU.subtract)\
                        .then_inc(sq_lo_set, 1)
                if first:
                    mw()
                    dve.wait_ge(acc_zero, TILES)
                for j in range(2):
                    dve.wait_ge(den_done, 2 * h + j + 1)
                    if not first:
                        dve.wait_ge(a_acc, 8 * h)
                    nc.vector.tensor_scalar(den_eps[:, 4 * j:4 * j + 4], bank[j][:, 0:4 * DEN_STEP:DEN_STEP],
                                            DEN_EPS, None, ALU.add).then_inc(den_read, 1)
                    dve.wait_ge(den_read, 2 * h + j + 1)
                    nc.vector.reciprocal(rden[:, 4 * j:4 * j + 4], den_eps[:, 4 * j:4 * j + 4]).then_inc(rden_set, 1)
                for j in range(2):
                    dve.wait_ge(rden_set, 2 * h + j + 1)
                    for t in range(4 * j, 4 * j + 4):
                        dve.wait_ge(a_out, 8 * h + t + 1)
                        if not first:
                            dve.wait_ge(a_acc, 8 * h + t - 7)
                        nc.vector.scalar_tensor_tensor(out=acc[:, t, :], in0=bank[4 + t % 4][:, :],
                                                       scalar=rden[:, t:t + 1], in1=acc[:, t, :],
                                                       op0=ALU.mult, op1=ALU.add).then_inc(a_acc, 1)
                        if last and t % 2 == 1:
                            norm_step(1, t // 2)

            def slice_lo(p, s, odd):
                dve.wait_ge(f_hi_set, 2 * p + s + 1)
                nc.vector.tensor_tensor(f_lo[odd][:, s, :], f_raw[:, s, :], f_hi[odd][:, s, :].bitcast(F32),
                                        ALU.subtract).then_inc(f_lo_set, 1)

            head(0, 0, True, False)
            head(1, 1, False, False)
            for s in range(2):
                slice_lo(0, s, 0)
            with dve.Fori(1, KV // 2 - 1) as i:
                for s in range(2):
                    head(2 * i + s, s, False, False)
            head(KV - 2, 0, False, False)
            head(KV - 1, 1, False, True)
            for s in range(CHUNKS, STEPS):
                norm_step(1, s)
            dve.wait_ge(late_consts_in, 16 * 4)
            dve.wait_ge(acc_zero, 2 * TILES)

            def pair(p, odd, first, last):
                for s in range(2):
                    f = 2 * p + s
                    if s == 1 and not last:
                        for s2 in range(2):
                            slice_lo(p + 1, s2, 1 - odd)
                    for j in range(2):
                        c = slice(j * HALF, (j + 1) * HALF)
                        dve.wait_ge(silu_set, 2 * f + j + 1)
                        dve.wait_ge(f_up, 2 * f + j + 1)
                        if not first:
                            dve.wait_ge(hid_lo_set, 2 * f + j - 3)
                            dve.wait_ge(hid_hi_set, 2 * f + j - 3)
                        nc.vector.scalar_tensor_tensor(out=hid[:, s, c], in0=bank[2 + j][:, :],
                                                       scalar=fsc[:, 1, bass.ds(f, 1)], in1=silu[:, c],
                                                       op0=ALU.mult, op1=ALU.mult).then_inc(hid_set, 1)
                        dve.wait_ge(hid_hi_set, 2 * f + j + 1)
                        nc.vector.tensor_tensor(hid_lo[:, s, c], hid[:, s, c], hid_hi[:, s, c].bitcast(F32),
                                                ALU.subtract).then_inc(hid_lo_set, 1)
                for t in range(TILES):
                    dve.wait_ge(f_down, 8 * p + t + 1)
                    if not first:
                        dve.wait_ge(f_acc, 8 * p + t - 7)
                    nc.vector.tensor_tensor(acc[:, t, :], bank[4 + t % 4][:, :], acc[:, t, :], ALU.add)\
                        .then_inc(f_acc, 1)
                    if last and t % 2 == 1:
                        norm_step(2, t // 2)

            def qkv_low(g, parity, k):
                dve.wait_ge(qkv_hi_set, KT * g + k + 1)
                c = slice(k * QKV_W // KT, (k + 1) * QKV_W // KT)
                nc.vector.tensor_tensor(qkv_lo[parity][:, c], qkv_raw[parity][:, c],
                                        qkv_hi[parity][:, c].bitcast(F32), ALU.subtract).then_inc(qkv_lo_set, 1)

            PAIRS = FT // 2
            pair(0, 0, True, False)
            for k in range(KT):
                qkv_low(0, 0, k)
            with dve.Fori(0, (PAIRS - 3) // 2) as i:
                pair(2 * i + 1, 1, False, False)
                pair(2 * i + 2, 0, False, False)
            pair(PAIRS - 2, 1, False, False)
            pair(PAIRS - 1, 0, False, True)
            for s in range(CHUNKS, STEPS):
                norm_step(2, s)
            dve.wait_ge(acc_zero, 3 * TILES)

            def slot(g, parity, b, first, second, third):
                u = 4 * g + b
                v, w = u - 1, u - 2
                last_group = isinstance(g, int) and g == KV - 1

                def products(t):
                    q = bank[(3 * b + 2 * t) % 2][:, :].rearrange("p (h a f) -> p h a f", h=G, a=2)
                    dve.wait_ge(q_proj, 2 * u + t + 1)
                    if second:
                        dve.wait_ge(turned_set, 6 * u)
                    for a, dst, done in ((0, by_cos, q_cos), (1, by_sin, q_sin)):
                        tab = cos_sin[:, a, t, None, None, :].to_broadcast([P, G, 2, D // 2])
                        nc.vector.tensor_tensor(dst[:, t, 0:G, :, :], q, tab, ALU.mult).then_inc(done, 1)

                def pT(j):
                    dve.wait_ge(pT_hi_set, 3 * w + j + 1)
                    nc.vector.tensor_tensor(pT_lo[:, j, :], bank[2 + (j + 1) % 2][:, :],
                                            pT_hi[:, j, :].bitcast(F32), ALU.subtract).then_inc(pT_lo_set, 1)

                def oT(t):
                    dve.wait_ge(oT_hi_set, 2 * w + t + 1)
                    nc.vector.tensor_tensor(oT_lo[:, t, :], bank[6 + t][:, :], oT_hi[:, t, :].bitcast(F32),
                                            ALU.subtract).then_inc(oT_lo_set, 1)

                def mask_max(j):
                    sbank = 4 + (3 * (b - 1) + (0 if j < G else 1 + (j - G) // 2)) % 2
                    wait_apart(dve, score_done, 3 * v + (1 if j < G else 2 + (j - G) // 2))
                    if j < G:
                        c, sc, m = slice(j * P, (j + 1) * P), slice(j * P, (j + 1) * P), masks[:, P:2 * P]
                    else:
                        c = slice((2 * j - G) * P, (2 * j - G + 2) * P)
                        sc, m = slice((j % 2) * 2 * P, (j % 2 + 1) * 2 * P), masks[:, :]
                    nc.vector.tensor_tensor_reduce(out=probs[:, c], in0=bank[sbank][:, sc], in1=m, scale=1.0,
                                                   scalar=LOWEST, op0=ALU.add, op1=ALU.max,
                                                   accum_out=row_max[:, j:j + 1]).then_inc(masked_set, 1)

                def negate(t):
                    dve.wait_ge(masked_set, 8 * v + G * (t + 1))
                    if third:
                        dve.wait_ge(exp_set, 8 * v)
                    nc.vector.tensor_scalar(neg_max[:, t * G:(t + 1) * G], row_max[:, t * G:(t + 1) * G],
                                            -SCALE, None, ALU.mult).then_inc(neg_max_set, 1)

                def add(t):
                    dve.wait_ge(l_out, 2 * w + t + 1)
                    r = 2 * ((b - 2) % 4) + t
                    if not (isinstance(w, int) and w == 0):
                        dve.wait_ge(l_acc, 2 * w)
                    nc.vector.tensor_tensor(acc[:, r, :], bank[6 + t][:, :], acc[:, r, :], ALU.add)\
                        .then_inc(l_acc, 1)

                if first:
                    products(0)
                if third:
                    pT(0)
                if first:
                    kv = bank[(3 * b + 1) % 2][:, :].rearrange("p (t c a f) -> p t c a f", t=2, c=2, a=2)
                    dve.wait_ge(kv_proj, u + 1)
                    for a, dst, done in ((0, by_cos, k_cos), (1, by_sin, k_sin)):
                        tab = cos_sin[:, a, :, None, :].to_broadcast([P, 2, 2, D // 2])
                        nc.vector.tensor_tensor(dst[:, :, G, :, :], kv[:, :, 0, :, :], tab, ALU.mult).then_inc(done, 1)
                if third:
                    pT(1)
                if first:
                    dve.wait_ge(v_hi_set, u + 1)
                    kv = bank[(3 * b + 1) % 2][:, :].rearrange("p (t a d) -> p t a d", t=2, a=2)
                    nc.vector.tensor_tensor(v_lo[:, b, :, :], kv[:, :, 1, :], v_hi[:, b, :, :].bitcast(F32),
                                            ALU.subtract).then_inc(v_lo_set, 1)
                    products(1)
                if third:
                    pT(2)
                if second:
                    if third:
                        dve.wait_ge(pT_done, 3 * w + 3)
                    for j in range(G):
                        mask_max(j)
                    negate(0)
                if third:
                    oT(0)
                if second:
                    for j in (4, 5):
                        mask_max(j)
                if third:
                    oT(1)
                if second:
                    for j in (6, 7):
                        mask_max(j)
                    negate(1)
                if first and not last_group:
                    qkv_low(g + 1, 1 - parity, b)
                if first and b < 2:
                    for h in (2 * b, 2 * b + 1):
                        dve.wait_ge(lwo_hi_set, G * g + h + 1)
                        c = slice(h * HID, (h + 1) * HID)
                        nc.vector.tensor_tensor(lwo_lo[parity][:, c], lwo_raw[parity][:, c],
                                                lwo_hi[parity][:, c].bitcast(F32), ALU.subtract)\
                            .then_inc(lwo_lo_set, 1)
                if third:
                    add(0)
                if second:
                    dve.wait_ge(exp_set, 8 * v + 8)
                    if third:
                        dve.wait_ge(probs_set, 8 * v)
                    nc.vector.reciprocal(row_inv[:], row_sum[:]).then_inc(row_inv_set, 1)
                if third:
                    add(1)
                if third and isinstance(u, int) and u - 2 >= 4 * (KV - 1):
                    norm_step(3, u - 2 - 4 * (KV - 1))

            slots(dve, slot)
            for s in range(CHUNKS, STEPS):
                norm_step(3, s)
            dve.wait_ge(bias_in, 16)
            for s in range(STEPS):
                norm_step(4, s)

        @block.tensor
        def _(pe):
            def product(o, lhs, rhs, start, stop):
                nc.tensor.matmul(o, lhs[0], rhs[0], start=start, stop=False)
                nc.tensor.matmul(o, lhs[0], rhs[1], start=False, stop=False)
                return nc.tensor.matmul(o, lhs[1], rhs[0], start=False, stop=stop)

            def turn(k, tiles):
                for t in tiles:
                    pe.wait_ge(xn_ready, k * TILES + t + 1)
                    if t >= 4:
                        pe.wait_ge(xn_lo_set, k * TILES + t - 3)
                    elif k == 1:
                        pe.wait_ge(a_acc, TILES * (KV - 1) + t + 5)
                    elif k == 2:
                        pe.wait_ge(f_acc, TILES * (FT // 2 - 1) + t + 5)
                    elif k == 3 and t < 2:
                        pe.wait_ge(masked_set, TILES * 4 * KV)
                    elif k == 3:
                        pe.wait_ge(l_acc, TILES * KV)
                    for i in range(KT):
                        last = nc.tensor.transpose(bank[4 + t % 4][:, i * P:(i + 1) * P],
                                                   acc[:, t, i * P:(i + 1) * P], ident[:])
                    last.then_inc(xn_turned, 1)

            def halves(j):
                return slice(j * HALF, (j + 1) * HALF)

            def a_project(h, s, j, first):
                if first:
                    pe.wait_ge(xn_lo_set, 4 * j + 4)
                else:
                    pe.wait_ge(den_read, 2 * h + j - 1)
                for k in range(KT):
                    w = slice(k * D, (k + 1) * D)
                    last = product(bank[j][:, :], (a_hi[:, s, w], a_lo[:, s, w]),
                                   (xn_hi[:, k, halves(j)], xn_lo[:, k, halves(j)]), k == 0, k == KT - 1)
                last.then_inc(a_proj, 1)

            def m_times_wo(h, s, used):
                m = slice(KT * D, A_W)
                pe.wait_ge(wos_lo_set, h + 1)
                if used:
                    pe.wait_ge(mw_lo_set, h - 1)
                product(bank[2 + s][:, :], (a_hi[:, s, m], a_lo[:, s, m]), (wos_hi[:, s, :], wos_lo[:, s, :]),
                        True, True).then_inc(mw_done, 1)

            def head(h, s, first, used):
                if not first:
                    pe.wait_ge(a_lo_set, h + 1)
                    m_times_wo(h, s, used)
                    for j in range(2):
                        a_project(h, s, j, False)
                for j in range(2):
                    pe.wait_ge(sq_set, 2 * h + j + 1)
                    for t in range(4 * j, 4 * j + 4):
                        o = (t % 4) * DEN_STEP
                        last = nc.tensor.matmul(bank[j][:, o:o + P], sq[:, t * P:(t + 1) * P],
                                                z_rep[:, bass.ds(h, 1), :].rearrange("p a c -> p (a c)"),
                                                start=True, stop=True)
                    last.then_inc(den_done, 1)
                    pe.wait_ge(sq_lo_set, 2 * h + j + 1)
                    pe.wait_ge(mw_lo_set, h + 1)
                    for t in range(4 * j, 4 * j + 4):
                        if not (first and t < 4):
                            pe.wait_ge(a_acc, 8 * h + t - 3)
                        c = slice(t * P, (t + 1) * P)
                        product(bank[4 + t % 4][:, :], (sq_hi[:, c], sq_lo[:, c]), (mw_hi[:, s, :], mw_lo[:, s, :]),
                                True, True).then_inc(a_out, 1)

            pe.wait_ge(early_consts_in, 16 * 3)
            turn(0, range(4))
            pe.wait_ge(a_lo_set, 1)
            a_project(0, 0, 0, True)
            turn(0, range(4, TILES))
            a_project(0, 0, 1, True)
            m_times_wo(0, 0, False)
            pe.wait_ge(z_set, KV)
            head(0, 0, True, False)
            head(1, 1, False, False)
            with pe.Fori(1, KV // 2) as i:
                for s in range(2):
                    head(2 * i + s, s, False, True)

            def gate_or_up(f, s, odd, j, a, first):
                if not first:
                    pe.wait_ge(silu_set if a == 0 else hid_set, 2 * f + j - 1)
                for k in range(KT):
                    w = slice((a * KT + k) * P, (a * KT + k + 1) * P)
                    last = product(bank[2 * a + j][:, :], (f_hi[odd][:, s, w], f_lo[odd][:, s, w]),
                                   (xn_hi[:, k, halves(j)], xn_lo[:, k, halves(j)]), k == 0, k == KT - 1)
                last.then_inc(f_up if a else f_gate, 1)

            def pair(p, odd, first):
                for s in range(2):
                    f = 2 * p + s
                    if not (first and s == 0):
                        pe.wait_ge(f_lo_set, f + 1)
                        for j in range(2):
                            for a in range(2):
                                gate_or_up(f, s, odd, j, a, False)
                d = slice(2 * KT * P, F_W)
                for t in range(TILES):
                    if t % 4 == 0:
                        pe.wait_ge(hid_lo_set, 4 * p + 3 + t // 4)
                    if not (first and t < 4):
                        pe.wait_ge(f_acc, 8 * p + t - 3)
                    c = slice(t * P, (t + 1) * P)
                    for s in range(2):
                        last = product(bank[4 + t % 4][:, :], (hid_hi[:, s, c], hid_lo[:, s, c]),
                                       (f_hi[odd][:, s, d], f_lo[odd][:, s, d]), s == 0, s == 1)
                    last.then_inc(f_down, 1)

            turn(1, range(4))
            pe.wait_ge(f_lo_set, 1)
            pe.wait_ge(xn_lo_set, TILES + 4)
            gate_or_up(0, 0, 0, 0, 0, True)
            turn(1, range(4, 6))
            gate_or_up(0, 0, 0, 0, 1, True)
            turn(1, range(6, TILES))
            pe.wait_ge(xn_lo_set, 2 * TILES)
            for a in range(2):
                gate_or_up(0, 0, 0, 1, a, True)
            pair(0, 0, True)
            with pe.Fori(0, (FT // 2 - 1) // 2) as i:
                pair(2 * i + 1, 1, False)
                pair(2 * i + 2, 0, False)

            def slot(g, parity, b, first, second, third):
                u = 4 * g + b
                v, w = u - 1, u - 2
                start = isinstance(u, int) and u == 0
                early = isinstance(u, int) and u < 3

                def project(t, what):
                    r = 2 * b + t
                    c = slice(r * P, (r + 1) * P)
                    if isinstance(g, int) and g == 0:
                        pe.wait_ge(xn_lo_set, 2 * TILES + r + 1)
                    for k in range(KT):
                        base = k * QKV_W // KT
                        ws = slice(base, base + G * D) if what == "q" else slice(base + G * D, base + (G + 2) * D)
                        o = bank[(3 * b + 2 * t) % 2][:, :] if what == "q" else \
                            bank[(3 * b + 1) % 2][:, t * 2 * D:(t + 1) * 2 * D]
                        last = product(o, (xn_hi[:, k, c], xn_lo[:, k, c]), (qkv_hi[parity][:, ws], qkv_lo[parity][:, ws]),
                                       k == 0, k == KT - 1)
                    return last

                def turn_qk(j):
                    if j < 2 and third and not early:
                        pe.wait_ge(pT_lo_set, 3 * w - 1 + j)
                    if j == 2:
                        pe.wait_ge(qkT_set, 3 * v + 1)
                    for i in range(4 if j < 2 else 2):
                        src = turned[:, j, i, :, :] if j < 2 else turned[:, i, G, :, :]
                        last = nc.tensor.transpose(bank[2 + j % 2][:, i * P:(i + 1) * P],
                                                   src.rearrange("p a f -> p (a f)"), ident[:])
                    last.then_inc(qk_turned, 1)

                def turn_p(j):
                    if j == 0:
                        pe.wait_ge(probs_set, 8 * w + 8)
                    if second and j < 2:
                        pe.wait_ge(qkT_set, 3 * v + 2 + j)
                    if not second and j < 2:
                        pe.wait_ge(pT_lo_set, 3 * w)
                    if j == 2:
                        pe.wait_ge(pT_lo_set, 3 * w + 1)
                    for h in range(G):
                        o = h * P if j == 0 else (G + 2 * h + j - 1) * P
                        last = nc.tensor.transpose(bank[2 + (j + 1) % 2][:, h * P:(h + 1) * P],
                                                   probs[:, o:o + P], ident[:])
                    last.then_inc(pT_done, 1)

                def times_v(t):
                    s = (b - 2) % 4
                    if t == 0:
                        pe.wait_ge(v_lo_set, w + 1)
                    pe.wait_ge(pT_lo_set, 3 * w + 1 + 2 * t)
                    if not (isinstance(w, int) and w == 0):
                        pe.wait_ge(l_acc, 2 * w - 1 + t)
                    o = bank[6 + t][:, :]
                    if t == 0:
                        last = product(o, (v_hi[:, s, 0, :], v_lo[:, s, 0, :]), (pT_hi[:, 0, :], pT_lo[:, 0, :]),
                                       True, True)
                    else:
                        product(o, (v_hi[:, s, 0, :], v_lo[:, s, 0, :]), (pT_hi[:, 1, :], pT_lo[:, 1, :]),
                                True, False)
                        last = product(o, (v_hi[:, s, 1, :], v_lo[:, s, 1, :]), (pT_hi[:, 2, :], pT_lo[:, 2, :]),
                                       False, True)
                    last.then_inc(pv_done, 1)

                def scores(j):
                    o = bank[4 + (3 * (b - 1) + j) % 2]
                    if j == 0:
                        pe.wait_ge(qkT_set, 3 * v + 3)
                        if isinstance(v, int) and v == 0:
                            pe.wait_ge(xn_lo_set, 3 * TILES)
                    if j == 2:
                        pe.wait_ge(masked_set, 8 * v + G)
                    elif third:
                        pe.wait_ge(masked_set, 8 * w + G + 2 * (j + 1))
                    if j == 0:
                        for h in range(G):
                            last = nc.tensor.matmul(o[:, h * P:(h + 1) * P], qkT[:, h * P:(h + 1) * P],
                                                    qkT[:, 2 * G * P:(2 * G + 1) * P], start=True, stop=True)
                    else:
                        for i in range(2):
                            h = G + 2 * (j - 1) + i
                            last = nc.tensor.matmul(o[:, i * 2 * P:(i + 1) * 2 * P], qkT[:, h * P:(h + 1) * P],
                                                    qkT[:, 2 * G * P:(2 * G + 2) * P], start=True, stop=True)
                    last.then_inc(score_done, 1)

                if first:
                    if b == 0:
                        pe.wait_ge(qkv_lo_set, KT * (g + 1))
                    if second:
                        pe.wait_ge(k_sin, u)
                        pe.wait_ge(v_lo_set, u)
                    project(0, "q").then_inc(q_proj, 1)
                if second:
                    pe.wait_ge(turned_set, 6 * u)
                    turn_qk(0)
                    turn_qk(1)
                if first:
                    if second:
                        pe.wait_ge(q_sin, 2 * u)
                    project(0, "kv")
                if second:
                    turn_qk(2)
                if third:
                    turn_p(0)
                if first:
                    project(1, "kv").then_inc(kv_proj, 1)
                    if start:
                        turn(2, range(4, TILES))
                if third:
                    turn_p(1)
                if first:
                    pe.wait_ge(q_sin, 2 * u + 1)
                    project(1, "q").then_inc(q_proj, 1)
                if third:
                    turn_p(2)
                if second:
                    scores(0)
                if third:
                    times_v(0)
                if second:
                    scores(1)
                if third:
                    times_v(1)
                if second:
                    scores(2)
                if third:
                    o_set = parity if b >= 2 else 1 - parity
                    if b == 2:
                        pe.wait_ge(lwo_lo_set, G * (g + 1))
                    for t in range(2):
                        pe.wait_ge(oT_lo_set, 2 * w + t + 1)
                        for h in range(G):
                            c, n = slice(h * P, (h + 1) * P), slice(h * HID, (h + 1) * HID)
                            last = product(bank[6 + t][:, :], (oT_hi[:, t, c], oT_lo[:, t, c]),
                                           (lwo_hi[o_set][:, n], lwo_lo[o_set][:, n]), h == 0, h == G - 1)
                        last.then_inc(l_out, 1)
                if isinstance(u, int) and u >= 4 * KV:
                    turn(3, range(2 * (u - 4 * KV), 2 * (u - 4 * KV) + 2))

            turn(2, range(4))
            slots(pe, slot)

            def last_layer(t):
                pe.wait_ge(xn_lo_set, 3 * TILES + t + 1)
                if t >= 4:
                    pe.wait_ge(ln_biased, t - 3)
                c = slice(t * P, (t + 1) * P)
                for k in range(KT):
                    last = product(bank[t % 4][:, :], (xn_hi[:, k, c], xn_lo[:, k, c]), (d_hi[:, k, :], d_lo[:, k, :]),
                                   k == 0, k == KT - 1)
                last.then_inc(d_out, 1)

            pe.wait_ge(d_step, 5 * KT)
            turn(3, range(4, 6))
            last_layer(0)
            last_layer(1)
            turn(3, range(6, TILES))
            for t in range(2, TILES):
                last_layer(t)


def kernel(**inputs):
    import numpy as np
    import concourse.bacc as bacc
    from concourse.bass_utils import run_bass_kernel_spmd as run

    a = {name: np.asarray(value) for name, value in inputs.items()}

    def by_partition(w, tiles):
        return w.reshape(tiles, P, -1).transpose(1, 0, 2).reshape(P, -1)

    wq = a["L0_attn_Wq"].reshape(KV, G, D, HID)[:, 0]
    a_w = np.stack([np.concatenate([by_partition(wq[h].T, KT), a["L0_attn_M"][h].T], 1) for h in range(KV)])
    a_wo = a["L0_attn_Wo"].T.reshape(KV, G, D, HID).transpose(0, 2, 1, 3).reshape(KV, D, G * HID)
    a_bq = a["L0_attn_bq"].reshape(KV, G, D)[:, 0].T
    gate, up, down = (a[f"L0_ffn_{n}_t"] for n in ("gate", "up", "down"))
    f_w = np.stack([np.concatenate([by_partition(gate[f:f + P].T, KT), by_partition(up[f:f + P].T, KT),
                                    down[:, f:f + P].T], 1) for f in range(0, FF, P)])
    f_scale = np.concatenate([a["L0_ffn_gate_s"].reshape(FT, P).T, a["L0_ffn_up_s"].reshape(FT, P).T], 1)
    wq, wk, wv = (a[f"L1_attn_w{n}"].reshape(KT, P, KV, -1) for n in "qkv")
    l_qkv = np.concatenate([wq, wk, wv], 3).transpose(2, 1, 0, 3).reshape(KV, P, QKV_W)
    l_wo = a["L1_attn_wo"].reshape(KV, G, D, HID).transpose(0, 2, 1, 3).reshape(KV, D, WO_W)
    size = HID // a["L1_ffn_zp"].shape[1]
    half = D // 2
    freq = np.float32(10000.0) ** (-np.arange(half, dtype=np.float32) / np.float32(half))
    angle = np.arange(2 * P, dtype=np.float32)[:, None] * freq[None, :]
    rope = np.stack([np.cos(angle), np.sin(angle)]).reshape(2, 2, P, half).transpose(2, 0, 1, 3).reshape(P, -1)
    i, j = np.arange(P)[:, None], np.arange(P)[None, :]
    low = np.float32(LOWEST)
    mask = np.concatenate([np.where(j > i, np.float32(0), low), np.where(j <= i, np.float32(0), low)], 1)

    arrays = {
        "x_in": a["L0_attn_hidden_states"].reshape(T, HID),
        "a_w": a_w, "a_wo": a_wo, "a_z": a["L0_attn_z"].T, "a_bq": a_bq,
        "f_w": f_w, "f_scale": f_scale, "down_s": np.broadcast_to(a["L0_ffn_down_s"], (P, HID)),
        "l_qkv": l_qkv, "l_wo": l_wo,
        "d_q": a["L1_ffn_weight_q"].T, "d_zp": np.repeat(a["L1_ffn_zp"].T, size, 0),
        "d_scale": np.repeat(a["L1_ffn_scale"].T, size, 0), "d_bias": np.broadcast_to(a["L1_ffn_bias"], (P, HID)),
        "rope": rope.astype(np.float32), "mask": mask.astype(np.float32), "ident_in": np.eye(P, dtype=np.float32),
    }
    arrays = {name: np.ascontiguousarray(value) for name, value in arrays.items()}
    nc = bacc.Bacc("TRN2", target_bir_lowering=False, num_devices=1)
    args = {name: nc.dram_tensor(name, value.shape, mybir.dt.from_np(value.dtype), kind="ExternalInput").ap()
            for name, value in arrays.items()}
    result = nc.dram_tensor("result", (T, HID), F32, kind="ExternalOutput").ap()
    build(nc, out=result, **args)
    r = run(nc, [arrays], core_ids=[0])
    return r.results[0]["result"].reshape(4, 256, HID)
```

```python
from contextlib import ExitStack

import concourse.bass as bass
from concourse import mybir

F32 = mybir.dt.float32
F32R = mybir.dt.float32r
I32 = mybir.dt.int32
ALU = mybir.AluOpType
ACT = mybir.ActivationFunctionType

P = 128
T = 1024
TILES = T // P
HALF = T // 2
HID = 512
CHUNKS = TILES // 2
STEPS = CHUNKS + 2
KT = HID // P
D = 128
KV = 8
G = 4
FF = 1792
FT = FF // P
SCALE = float(D) ** -0.5
LN_EPS = 1e-5
DEN_EPS = 1e-6
LOWEST = -3.4028234663852886e38

A_W = KT * D + D
F_W = 2 * KT * P + HID
QKV_W = KT * (G + 2) * D
WO_W = G * HID
A_USED = 6 * A_W + (8 + 3 + 8) * HID + KV + KV * P + P + 5 * T + 2 * TILES
F_USED = HID + 7 * T + 6 * F_W
L_USED = HID + 2 * QKV_W + 4 * WO_W + (21 * G + 9) * P + 22 * D + 4 * 2 * G
PREFETCH = A_USED + 528
FIRST_GROUP = PREFETCH + 6 * F_W
assert F_USED < PREFETCH and L_USED < FIRST_GROUP
DEN_STEP = 48


def build(nc, x_in, a_w, a_wo, a_z, a_bq, f_w, f_scale, down_s, l_qkv, l_wo, d_q, d_zp, d_scale, d_bias,
          rope, rope_turned, mask, ident_in, out):
    with ExitStack() as ctx:
        def sem(name):
            return ctx.enter_context(nc.semaphore(name))

        def sb(stack, name, shape, dt=F32):
            return stack.enter_context(nc.sbuf_tensor(name, shape, dt))

        x = sb(ctx, "x", [P, TILES, HID])
        acc = sb(ctx, "acc", [P, TILES, HID])
        xn_hi = sb(ctx, "xn_hi", [P, KT, T], F32R)
        xn_lo = sb(ctx, "xn_lo", [P, KT, T], F32R)
        ident = sb(ctx, "ident", [P, P])
        bq = sb(ctx, "bq", [P, KV])
        fsc = sb(ctx, "fsc", [P, 2, FT])
        cos_sin = sb(ctx, "cos_sin", [P, 2, 2, D // 2])
        masks = sb(ctx, "masks", [P, 2 * P])
        stats = sb(ctx, "stats", [P, TILES, 6])
        mean_var = sb(ctx, "mean_var", [P, TILES, 2])
        stats2 = sb(ctx, "stats2", [P, TILES, 6])
        mean_var2 = sb(ctx, "mean_var2", [P, TILES, 2])
        var_eps = sb(ctx, "var_eps", [P, 2, TILES])
        rstd = sb(ctx, "rstd", [P, 2, TILES])
        minus_half = sb(ctx, "minus_half", [P, 2])
        ones = sb(ctx, "ones", [P, 1])
        lo_squares = sb(ctx, "lo_squares", [P, 1])
        inexact = sb(ctx, "inexact", [1, 2])
        shift = sb(ctx, "shift", [P, 2, TILES])

        with ExitStack() as part:
            a_raw = sb(part, "a_raw", [P, 2, A_W])
            a_hi = sb(part, "a_hi", [P, 2, A_W], F32R)
            a_lo = sb(part, "a_lo", [P, 2, A_W], F32R)
            wo_raw = sb(part, "wo_raw", [P, 2, G, HID])
            wo_pair = sb(part, "wo_pair", [P, 2, HID])
            wo_sum = sb(part, "wo_sum", [P, HID])
            wos_hi = sb(part, "wos_hi", [P, 2, HID], F32R)
            wos_lo = sb(part, "wos_lo", [P, 2, HID], F32R)
            mw_hi = sb(part, "mw_hi", [P, 2, HID], F32R)
            mw_lo = sb(part, "mw_lo", [P, 2, HID], F32R)
            z_col = sb(part, "z_col", [P, KV])
            z_rep = sb(part, "z_rep", [P, KV, P])
            zeros = sb(part, "zeros", [P, P])
            expq = sb(part, "expq", [P, T])
            reluq = sb(part, "reluq", [P, T])
            sq = sb(part, "sq", [P, T])
            sq_hi = sb(part, "sq_hi", [P, T], F32R)
            sq_lo = sb(part, "sq_lo", [P, T], F32R)
            den_eps = sb(part, "den_eps", [P, TILES])
            rden = sb(part, "rden", [P, TILES])
        with ExitStack() as part:
            down_row = sb(part, "down_row", [P, HID])
            silu = sb(part, "silu", [P, T])
            hid = sb(part, "hid", [P, 2, T])
            hid_hi = sb(part, "hid_hi", [P, 2, T], F32R)
            hid_lo = sb(part, "hid_lo", [P, 2, T], F32R)
            f_odd_hi = sb(part, "f_odd_hi", [P, 2, F_W], F32R)
            f_odd_lo = sb(part, "f_odd_lo", [P, 2, F_W], F32R)
            squares = sb(part, "squares", [P, 2, F_W])
            sb(part, "behind_linear_attention", [P, PREFETCH - F_USED])
            f_raw = sb(part, "f_raw", [P, 2, F_W], I32)
            f_even_hi = sb(part, "f_even_hi", [P, 2, F_W], F32R)
            f_even_lo = sb(part, "f_even_lo", [P, 2, F_W], F32R)
        f_hi, f_lo = (f_even_hi, f_odd_hi), (f_even_lo, f_odd_lo)
        def in_place(stack, name, width):
            with ExitStack() as raw_part:
                raw = sb(raw_part, name + "_raw", [P, width])
            return raw, sb(stack, name + "_lo", [P, width], F32R)

        with ExitStack() as part:
            bias_row = sb(part, "bias_row", [P, HID])
            qkv_odd_hi = sb(part, "qkv_odd_hi", [P, QKV_W], F32R)
            qkv_odd_raw, qkv_odd_lo = in_place(part, "qkv_odd", QKV_W)
            lwo_even_hi = sb(part, "lwo_even_hi", [P, WO_W], F32R)
            lwo_even_raw, lwo_even_lo = in_place(part, "lwo_even", WO_W)
            lwo_odd_hi = sb(part, "lwo_odd_hi", [P, WO_W], F32R)
            lwo_odd_raw, lwo_odd_lo = in_place(part, "lwo_odd", WO_W)
            cos_sin_T = sb(part, "cos_sin_T", [P, 2, 2 * P])
            q_by_cos = sb(part, "q_by_cos", [P, G // 2 * 2 * P])
            q_by_sin = sb(part, "q_by_sin", [P, G // 2 * 2 * P])
            k_by_cos = sb(part, "k_by_cos", [P, 2, 2, D // 2])
            k_by_sin = sb(part, "k_by_sin", [P, 2, 2, D // 2])
            k_rotated = sb(part, "k_rotated", [P, 2, 2, D // 2])
            qT = sb(part, "qT", [P, 2, 2, G, P])
            kT = sb(part, "kT", [P, P])
            q1T_hi = sb(part, "q1T_hi", [P, G, P], F32R)
            q1T_lo = sb(part, "q1T_lo", [P, G, P], F32R)
            kT_hi = sb(part, "kT_hi", [P, 2 * P], F32R)
            kT_lo = sb(part, "kT_lo", [P, 2 * P], F32R)
            v_hi = sb(part, "v_hi", [P, 4, 2, D], F32R)
            v_lo = sb(part, "v_lo", [P, 4, 2, D], F32R)
            probs = sb(part, "probs", [P, 3 * G * P])
            row_max = sb(part, "row_max", [P, 2 * G])
            neg_max = sb(part, "neg_max", [P, 2 * G])
            row_sum = sb(part, "row_sum", [P, 2 * G])
            row_inv = sb(part, "row_inv", [P, 2 * G])
            pT_hi = sb(part, "pT_hi", [P, 3, G * P], F32R)
            pT_lo = sb(part, "pT_lo", [P, 3, G * P], F32R)
            oT_hi = sb(part, "oT_hi", [P, 2, G * P], F32R)
            oT_lo = sb(part, "oT_lo", [P, 2, G * P], F32R)
            sb(part, "behind_ffn", [P, FIRST_GROUP - L_USED])
            with ExitStack() as first_set:
                qkv_even_hi = sb(first_set, "qkv_even_hi", [P, QKV_W], F32R)
                qkv_even_raw, qkv_even_lo = in_place(first_set, "qkv_even", QKV_W)
            d_hi = sb(part, "d_hi", [P, KT, HID], F32R)
            d_lo = sb(part, "d_lo", [P, KT, HID], F32R)
            dq_raw = sb(part, "dq_raw", [P, HID], I32)
            dzp_raw = sb(part, "dzp_raw", [P, HID])
            dsc_raw = sb(part, "dsc_raw", [P, HID])
            dq_f = sb(part, "dq_f", [P, HID])
        qkv_hi, qkv_raw, qkv_lo = (qkv_even_hi, qkv_odd_hi), (qkv_even_raw, qkv_odd_raw), (qkv_even_lo, qkv_odd_lo)
        lwo_hi, lwo_raw, lwo_lo = (lwo_even_hi, lwo_odd_hi), (lwo_even_raw, lwo_odd_raw), (lwo_even_lo, lwo_odd_lo)

        bank = [ctx.enter_context(nc.psum_tensor(f"bank{i}", [P, 512], F32)) for i in range(8)]

        early_consts_in = sem("early_consts_in")
        late_consts_in = sem("late_consts_in")
        bias_in = sem("bias_in")
        down_in = sem("down_in")
        rope_T_in = sem("rope_T_in")
        x_loaded = [sem(f"x_loaded{t}") for t in range(TILES)]
        consts_set = sem("consts_set")
        z_set = sem("z_set")
        ln_biased = sem("ln_biased")
        even_scaled = sem("even_scaled")
        odd_scaled = sem("odd_scaled")
        ln_stats = sem("ln_stats")
        ln_mean = sem("ln_mean")
        ln_var = sem("ln_var")
        ln_rstd = sem("ln_rstd")
        ln_shift = sem("ln_shift")
        ln_out = sem("ln_out")
        x_added = sem("x_added")
        odd_added = sem("odd_added")
        ln2_stats = sem("ln2_stats")
        ln2_mean = sem("ln2_mean")
        ln2_var = sem("ln2_var")
        ln2_rstd = sem("ln2_rstd")
        ln2_shift = sem("ln2_shift")
        xn_ready = sem("xn_ready")
        xn_turned = sem("xn_turned")
        xn_hi_set = sem("xn_hi_set")
        xn_lo_set = sem("xn_lo_set")
        acc_zero = sem("acc_zero")
        a_loaded = [sem(f"a_loaded{s}") for s in range(2)]
        wo_loaded = [sem(f"wo_loaded{s}") for s in range(2)]
        a_hi_set = sem("a_hi_set")
        a_lo_set = sem("a_lo_set")
        wo_pairs = sem("wo_pairs")
        wo_summed = sem("wo_summed")
        wos_hi_set = sem("wos_hi_set")
        wos_lo_set = sem("wos_lo_set")
        a_proj = sem("a_proj")
        a_exp = sem("a_exp")
        a_relu = sem("a_relu")
        sq_set = sem("sq_set")
        sq_hi_set = sem("sq_hi_set")
        sq_lo_set = sem("sq_lo_set")
        mw_done = sem("mw_done")
        mw_hi_set = sem("mw_hi_set")
        mw_lo_set = sem("mw_lo_set")
        den_done = sem("den_done")
        den_read = sem("den_read")
        rden_set = sem("rden_set")
        a_out = sem("a_out")
        a_acc = sem("a_acc")
        f_loaded = [sem(f"f_loaded{s}") for s in range(2)]
        f_hi_set = sem("f_hi_set")
        f_lo_set = sem("f_lo_set")
        squares_set = sem("squares_set")
        squares_summed = sem("squares_summed")
        inexact_set = sem("inexact_set")
        f_gate = sem("f_gate")
        f_up = sem("f_up")
        silu_set = sem("silu_set")
        hid_set = sem("hid_set")
        hid_hi_set = sem("hid_hi_set")
        hid_lo_set = sem("hid_lo_set")
        f_down = sem("f_down")
        f_acc = sem("f_acc")
        d_loaded = sem("d_loaded")
        d_step = sem("d_step")
        qkv_loaded = [sem(f"qkv_loaded{s}") for s in range(2)]
        lwo_loaded = [sem(f"lwo_loaded{s}") for s in range(2)]
        qkv_hi_set = sem("qkv_hi_set")
        qkv_lo_set = sem("qkv_lo_set")
        lwo_hi_set = sem("lwo_hi_set")
        lwo_lo_set = sem("lwo_lo_set")
        q_proj = sem("q_proj")
        kv_proj = sem("kv_proj")
        q_cos = sem("q_cos")
        q_sin = sem("q_sin")
        k_cos = sem("k_cos")
        k_sin = sem("k_sin")
        q_swapped = sem("q_swapped")
        qT_set = sem("qT_set")
        k_rotated_set = sem("k_rotated_set")
        k_turned = sem("k_turned")
        kT_set = sem("kT_set")
        k_hi_set = sem("k_hi_set")
        k_lo_set = sem("k_lo_set")
        q1_hi_set = sem("q1_hi_set")
        q1_lo_set = sem("q1_lo_set")
        v_hi_set = sem("v_hi_set")
        v_lo_set = sem("v_lo_set")
        score_done = sem("score_done")
        masked_set = sem("masked_set")
        neg_max_set = sem("neg_max_set")
        exp_set = sem("exp_set")
        row_inv_set = sem("row_inv_set")
        probs_set = sem("probs_set")
        pT_done = sem("pT_done")
        pT_hi_set = sem("pT_hi_set")
        pT_lo_set = sem("pT_lo_set")
        pv_done = sem("pv_done")
        oT_hi_set = sem("oT_hi_set")
        oT_lo_set = sem("oT_lo_set")
        l_out = sem("l_out")
        l_acc = sem("l_acc")
        d_out = sem("d_out")
        stored = sem("stored")

        waits_passed = sem("waits_passed")

        def slots(eng, slot):
            for b in range(4):
                slot(0, 0, b, True, b >= 1, b >= 2)
            with eng.Fori(0, (KV - 2) // 2) as i:
                for s in range(2):
                    for b in range(4):
                        slot(2 * i + 1 + s, (1 + s) % 2, b, True, True, True)
            for b in range(4):
                slot(KV - 1, (KV - 1) % 2, b, True, True, True)
            slot(KV, KV % 2, 0, False, True, True)
            slot(KV, KV % 2, 1, False, False, True)

        def wait_apart(eng, semaphore, value):
            eng.wait_ge(semaphore, value)
            if not isinstance(value, int):
                eng.sem_inc(waits_passed, 1)

        block = ctx.enter_context(nc.Block())

        @block.sync
        def _(sync):
            def load_x(t):
                sync.dma_start(x[:, t, :], x_in[t * P:(t + 1) * P, :]).then_inc(x_loaded[t], 16)

            def load_a(h, s):
                sync.dma_start(a_raw[:, s, :], a_w[bass.ds(h, 1), :, :].rearrange("a p n -> p (a n)"))\
                    .then_inc(a_loaded[s], 16)

            def load_wo(h, s):
                sync.dma_start(wo_raw[:, s, :, :].rearrange("p g n -> p (g n)"),
                               a_wo[bass.ds(h, 1), :, :].rearrange("a p n -> p (a n)")).then_inc(wo_loaded[s], 16)

            for t in range(4):
                load_x(t)
            sync.dma_start(ident[:], ident_in).then_inc(early_consts_in, 16)
            sync.dma_start(bq[:], a_bq).then_inc(early_consts_in, 16)
            sync.dma_start(z_col[:], a_z).then_inc(early_consts_in, 16)
            load_a(0, 0)
            for t in range(4, TILES):
                load_x(t)
            load_wo(0, 0)
            load_a(1, 1)
            load_wo(1, 1)

            def load_slice(f, s):
                sync.dma_start(f_raw[:, s, :], f_w[bass.ds(f, 1), :, :].rearrange("a p n -> p (a n)"))\
                    .then_inc(f_loaded[s], 16)

            for s in range(2):
                load_slice(s, s)
            sync.dma_start(fsc[:].rearrange("p a f -> p (a f)"), f_scale).then_inc(late_consts_in, 16)
            sync.dma_start(cos_sin[:].rearrange("p a b f -> p (a b f)"), rope).then_inc(late_consts_in, 16)
            sync.dma_start(masks[:], mask).then_inc(late_consts_in, 16)

            def load_qkv(g, s):
                sync.dma_start(qkv_raw[s][:], l_qkv[bass.ds(g, 1), :, :].rearrange("a p n -> p (a n)"))\
                    .then_inc(qkv_loaded[s], 16)

            def load_lwo(g, s):
                sync.dma_start(lwo_raw[s][:], l_wo[bass.ds(g, 1), :, :].rearrange("a p n -> p (a n)"))\
                    .then_inc(lwo_loaded[s], 16)

            load_qkv(0, 0)
            with sync.Fori(1, KV // 2) as i:
                for s in range(2):
                    sync.wait_ge(a_lo_set, 2 * i + s - 1)
                    load_a(2 * i + s, s)
                    sync.wait_ge(wo_pairs, 2 * i + s - 1)
                    load_wo(2 * i + s, s)
            with sync.Fori(1, FT // 2) as i:
                for s in range(2):
                    sync.wait_ge(f_lo_set, 6 * i + 3 * s - 3)
                    load_slice(2 * i + s, s)
            sync.wait_ge(f_acc, TILES)
            sync.dma_start(down_row[:], down_s).then_inc(down_in, 16)
            sync.wait_ge(f_acc, TILES * (FT // 2))
            sync.dma_start(cos_sin_T[:].rearrange("p a n -> p (a n)"), rope_turned).then_inc(rope_T_in, 16)
            load_lwo(0, 0)
            load_qkv(1, 1)
            load_lwo(1, 1)
            sync.wait_ge(x_added, 2 * TILES)
            sync.dma_start(bias_row[:], d_bias).then_inc(bias_in, 16)

            def load_group(g, s):
                sync.wait_ge(q_proj, 8 * (g - 1))
                load_qkv(g, s)
                sync.wait_ge(l_out, 8 * (g - 1))
                load_lwo(g, s)

            with sync.Fori(1, (KV - 2) // 2 + 1) as i:
                for s in range(2):
                    load_group(2 * i + s, s)
            sync.wait_ge(q_proj, 8 * (KV - 1))
            for k in range(KT):
                if k:
                    sync.wait_ge(d_step, 5 * k)
                for dst, src in ((dq_raw, d_q), (dzp_raw, d_zp), (dsc_raw, d_scale)):
                    sync.dma_start(dst[:], src[k * P:(k + 1) * P, :]).then_inc(d_loaded, 16)
            for t in range(TILES):
                sync.wait_ge(odd_added, t // 2 + 1) if t % 2 else sync.wait_ge(x_added, 3 * TILES + t // 2 + 1)
                sync.dma_start(out[t * P:(t + 1) * P, :], x[:, t, :]).then_inc(stored, 16)
            sync.wait_ge(stored, 16 * TILES)

        @block.gpsimd
        def _(pool):
            nc.gpsimd.memset(minus_half[:], -0.5).then_inc(consts_set, 1)
            nc.gpsimd.memset(zeros[:], 0.0).then_inc(consts_set, 1)
            nc.gpsimd.memset(ones[:], 1.0).then_inc(consts_set, 1)

            def powers(k, s):
                def scale_even(t):
                    pool.wait_ge(f_acc, TILES * (FT // 2 - 1) + t + 1)
                    nc.gpsimd.tensor_tensor(acc[:, t, :], acc[:, t, :], down_row[:], ALU.mult)\
                        .then_inc(even_scaled, 1)

                def output_power():
                    if k and s < CHUNKS:
                        two = slice(2 * s, 2 * s + 2)
                        if k == 2 and s == 0:
                            pool.wait_ge(down_in, 16)
                            scale_even(0)
                            scale_even(2)
                        pool.wait_ge(ln_var, (k - 1) * CHUNKS + s + 1)
                        nc.gpsimd.tensor_tensor(rstd[:, 0, two], var_eps[:, 0, two], minus_half[:], ALU.pow)\
                            .then_inc(ln_rstd, 1)

                def new_power():
                    if k < 4 and 0 <= s - 1 < CHUNKS:
                        two = slice(2 * s - 2, 2 * s)
                        pool.wait_ge(ln2_var, k * CHUNKS + s)
                        nc.gpsimd.tensor_tensor(rstd[:, 1, two], var_eps[:, 1, two], minus_half[:], ALU.pow)\
                            .then_inc(ln2_rstd, 1)

                output_power()
                new_power()
                if k == 2 and s + 2 < CHUNKS:
                    scale_even(2 * s + 4)

            def sums(k, s):
                if k and s < CHUNKS:
                    for t in (2 * s, 2 * s + 1)[:1 if k == 4 else 2]:
                        pool.wait_ge(ln_out, (k - 1) * TILES + t + 1)
                        nc.gpsimd.tensor_tensor(x[:, t, :], x[:, t, :], acc[:, t, :], ALU.add).then_inc(x_added, 1)

            def norm_step(k, s):
                powers(k, s)
                sums(k, s)

            def norm(k):
                for s in range(STEPS):
                    norm_step(k, s)

            def clear_acc(k):
                for t in range(TILES):
                    pool.wait_ge(xn_turned, k * TILES + t + 1)
                    nc.gpsimd.memset(acc[:, t, :], 0.0).then_inc(acc_zero, 1)

            pool.wait_ge(consts_set, 3)

            def prepare_head(h, s, first):
                wait_apart(pool, a_loaded[s], 16 * (h // 2 + 1) if first else 16 * h[1])
                hh = h if first else h[0]
                if not first:
                    wait_apart(pool, mw_done, hh - 1)
                    wait_apart(pool, a_proj, 2 * hh - 2)
                nc.gpsimd.tensor_scalar(a_hi[:, s, :], a_raw[:, s, :], 1.0, 1.0, ALU.mult, ALU.mult)\
                    .then_inc(a_hi_set, 1)
                pool.wait_ge(a_hi_set, hh + 1)
                nc.gpsimd.tensor_tensor(a_lo[:, s, :], a_raw[:, s, :], a_hi[:, s, :].bitcast(F32), ALU.subtract)\
                    .then_inc(a_lo_set, 1)
                if first and h == 0:
                    for step in range(3, STEPS):
                        norm_step(0, step)
                pool.wait_ge(wo_loaded[s], 16 * (h // 2 + 1) if first else 16 * h[1])
                if not (first and h == 0):
                    pool.wait_ge(wo_summed, hh)
                nc.gpsimd.tensor_tensor(wo_pair[:], wo_raw[:, s, 0:2, :], wo_raw[:, s, 2:4, :], ALU.add)\
                    .then_inc(wo_pairs, 1)
                pool.wait_ge(wo_pairs, hh + 1)
                if not (first and h == 0):
                    pool.wait_ge(wos_lo_set, hh)
                nc.gpsimd.tensor_tensor(wo_sum[:], wo_pair[:, 0, :], wo_pair[:, 1, :], ALU.add).then_inc(wo_summed, 1)
                wait_apart(pool, wo_summed, hh + 1)
                nc.gpsimd.tensor_scalar(wos_hi[:, s, :], wo_sum[:], 1.0, 1.0, ALU.mult, ALU.mult)\
                    .then_inc(wos_hi_set, 1)
                pool.wait_ge(wos_hi_set, hh + 1)
                nc.gpsimd.tensor_tensor(wos_lo[:, s, :], wo_sum[:], wos_hi[:, s, :].bitcast(F32), ALU.subtract)\
                    .then_inc(wos_lo_set, 1)

            for step in range(3):
                norm_step(0, step)
            prepare_head(0, 0, True)
            for h in range(KV):
                nc.gpsimd.tensor_scalar(z_rep[:, h, :], zeros[:], 1.0, z_col[:, h:h + 1], ALU.mult, ALU.add)\
                    .then_inc(z_set, 1)
            clear_acc(0)
            prepare_head(1, 1, True)

            def split_slice(f, s, odd, loads, used):
                pool.wait_ge(f_loaded[s], 16 * loads)
                if used is not None:
                    wait_apart(pool, f_down, used)
                nc.gpsimd.tensor_scalar(f_hi[odd][:, s, :], f_raw[:, s, :], 1.0, 1.0, ALU.mult, ALU.mult)\
                    .then_inc(f_hi_set, 1)

            for s in range(2):
                prepare_head((2 + s, 2), s, False)
            for s in range(2):
                split_slice(s, s, 0, 1, None)
            with pool.Fori(2, KV // 2) as i:
                for s in range(2):
                    prepare_head((2 * i + s, i + 1), s, False)

            def split_qkv(g, s, k):
                wait_apart(pool, qkv_loaded[s], 8 * (g - s) + 16)
                c = slice(k * QKV_W // KT, (k + 1) * QKV_W // KT)
                nc.gpsimd.tensor_scalar(qkv_hi[s][:, c], qkv_raw[s][:, c], 1.0, 1.0, ALU.mult, ALU.mult)\
                    .then_inc(qkv_hi_set, 1)

            pool.wait_ge(squares_set, 1)
            norm(1)
            for s in range(2):
                split_slice(2 + s, s, 1, 2, None)
            clear_acc(1)

            def split_pair(p, odd, used):
                for s in range(2):
                    wait_apart(pool, f_loaded[s], 16 * (p + 1))
                    wait_apart(pool, f_down, used)
                    nc.gpsimd.tensor_scalar(f_hi[odd][:, s, :], f_raw[:, s, :], 1.0, 1.0, ALU.mult, ALU.mult)\
                        .then_inc(f_hi_set, 1)

            for k in range(KT):
                split_qkv(0, 0, k)
            split_pair(2, 0, TILES)
            with pool.Fori(1, 3) as i:
                for odd in (1, 0):
                    split_pair(2 * i + 2 - odd, odd, TILES * (2 * i + 1 - odd))
            norm(2)
            clear_acc(2)

            def slot(g, parity, b, first, second, third):
                u = 4 * g + b
                last_group = isinstance(g, int) and g == KV - 1
                start = isinstance(u, int) and u == 0

                def split_weights():
                    if first and b < 2:
                        for h in (2 * b, 2 * b + 1):
                            wait_apart(pool, lwo_loaded[parity], 8 * (g - parity) + 16)
                            c = slice(h * HID, (h + 1) * HID)
                            nc.gpsimd.tensor_scalar(lwo_hi[parity][:, c], lwo_raw[parity][:, c], 1.0, 1.0,
                                                    ALU.mult, ALU.mult).then_inc(lwo_hi_set, 1)
                    if first and not last_group:
                        split_qkv(g + 1, 1 - parity, b)

                if first:

                    def rotate_q(j):
                        pool.wait_ge(q_sin, 2 * u + j + 1)
                        if not (isinstance(u, int) and u < 2):
                            pool.wait_ge(score_done, 3 * (u - 1))
                        shape = dict(h=G // 2, t=2)
                        nc.gpsimd.tensor_tensor(
                            qT[:, b % 2, :, 2 * j:2 * j + 2, :].rearrange("p t h c -> p h t c"),
                            q_by_cos[:].rearrange("p (h t c) -> p h t c", **shape),
                            q_by_sin[:].rearrange("p (h t c) -> p h t c", **shape), ALU.add)\
                            .then_inc(qT_set, 1)

                    if start:
                        split_weights()
                    rotate_q(0)
                    pool.wait_ge(k_sin, u + 1)
                    if second:
                        pool.wait_ge(k_turned, u)
                    nc.gpsimd.tensor_tensor(k_rotated[:, :, 0, :], k_by_cos[:, :, 0, :], k_by_sin[:, :, 1, :],
                                            ALU.subtract).then_inc(k_rotated_set, 1)
                    nc.gpsimd.tensor_tensor(k_rotated[:, :, 1, :], k_by_sin[:, :, 0, :], k_by_cos[:, :, 1, :],
                                            ALU.add).then_inc(k_rotated_set, 1)
                    rotate_q(1)
                if first and not start:
                    split_weights()
                if last_group:
                    k = b
                    pool.wait_ge(d_loaded, 48 * (k + 1))
                    nc.gpsimd.tensor_scalar(dq_f[:], dq_raw[:], 1.0, 1.0, ALU.mult, ALU.mult).then_inc(d_step, 1)
                    pool.wait_ge(d_step, 5 * k + 1)
                    nc.gpsimd.tensor_tensor(dq_f[:], dq_f[:], dzp_raw[:], ALU.subtract).then_inc(d_step, 1)
                    pool.wait_ge(d_step, 5 * k + 2)
                    nc.gpsimd.tensor_tensor(dq_f[:], dq_f[:], dsc_raw[:], ALU.mult).then_inc(d_step, 1)
                    pool.wait_ge(d_step, 5 * k + 3)
                    nc.gpsimd.tensor_scalar(d_hi[:, k, :], dq_f[:], 1.0, 1.0, ALU.mult, ALU.mult).then_inc(d_step, 1)
                    pool.wait_ge(d_step, 5 * k + 4)
                    nc.gpsimd.tensor_tensor(d_lo[:, k, :], dq_f[:], d_hi[:, k, :].bitcast(F32), ALU.subtract)\
                        .then_inc(d_step, 1)
                norming = third and isinstance(u, int) and u - 3 >= 4 * (KV - 1)
                if norming:
                    powers(3, u - 3 - 4 * (KV - 1))
                if second:
                    wait_apart(pool, row_inv_set, u)
                    for j in range(2 * G):
                        c = slice(j * P, (j + 1) * P) if j < G else slice((2 * j - G) * P, (2 * j - G + 2) * P)
                        nc.gpsimd.tensor_scalar(probs[:, c], probs[:, c], row_inv[:, j:j + 1], 1.0,
                                                ALU.mult, ALU.mult).then_inc(probs_set, 1)
                if norming:
                    sums(3, u - 3 - 4 * (KV - 1))

            slots(pool, slot)
            for s in range(CHUNKS - 1, STEPS):
                norm_step(3, s)
            norm(4)

        @block.scalar
        def _(act):
            def norm_step(k, s):
                if k < 4 and 0 <= s - 2 < CHUNKS:
                    for t in (2 * s - 4, 2 * s - 3):
                        act.wait_ge(xn_turned, k * TILES + t + 1)
                        nc.scalar.activation(xn_hi[:, :, t * P:(t + 1) * P],
                                             bank[4 + t % 4][:, :].rearrange("p (k c) -> p k c", k=KT), ACT.Copy)\
                            .then_inc(xn_hi_set, 1)
                def output():
                    if k and s < CHUNKS:
                        act.wait_ge(ln_shift, (k - 1) * CHUNKS + s + 1)
                        for t in (2 * s, 2 * s + 1):
                            nc.scalar.activation(acc[:, t, :], acc[:, t, :], ACT.Identity, bias=shift[:, 0, t:t + 1],
                                                 scale=rstd[:, 0, t:t + 1]).then_inc(ln_out, 1)

                def new_input():
                    if k < 4 and 0 <= s - 1 < CHUNKS:
                        act.wait_ge(ln2_shift, k * CHUNKS + s)
                        for t in (2 * s - 2, 2 * s - 1):
                            nc.scalar.activation(acc[:, t, :], x[:, t, :], ACT.Identity, bias=shift[:, 1, t:t + 1],
                                                 scale=rstd[:, 1, t:t + 1]).then_inc(xn_ready, 1)

                output()
                new_input()

            def norm(k):
                for s in range(STEPS):
                    norm_step(k, s)

            norm(0)
            act.wait_ge(early_consts_in, 16 * 3)

            def head(h, s, first):
                def mw():
                    act.wait_ge(mw_done, h + 1)
                    nc.scalar.activation(mw_hi[:, s, :], bank[2 + s][:, :], ACT.Copy).then_inc(mw_hi_set, 1)

                if not first:
                    mw()
                for j in range(2):
                    c = slice(j * HALF, (j + 1) * HALF)
                    wait_apart(act, a_proj, 2 * h + j + 1)
                    if not first:
                        wait_apart(act, sq_set, 2 * h + j - 1)
                    nc.scalar.activation(expq[:, c], bank[j][:, :], ACT.Exp, bias=bq[:, bass.ds(h, 1)])\
                        .then_inc(a_exp, 1)
                    nc.scalar.activation(reluq[:, c], bank[j][:, :], ACT.Relu, bias=bq[:, bass.ds(h, 1)])\
                        .then_inc(a_relu, 1)
                    if first and j == 1:
                        mw()
                    act.wait_ge(sq_set, 2 * h + j + 1)
                    if not first:
                        act.wait_ge(a_out, 8 * h - 4 + 4 * j)
                    nc.scalar.activation(sq_hi[:, c], sq[:, c], ACT.Copy).then_inc(sq_hi_set, 1)

            head(0, 0, True)
            head(1, 1, False)

            def square_lows(p, odd, first):
                act.wait_ge(f_lo_set, 6 * (p + 1))
                if not first:
                    act.wait_ge(squares_summed, p)
                not_read = qkv_even_hi[:].rearrange("p (s n) -> p s n", s=2) if first else squares[:]
                nc.scalar.activation(not_read, f_lo[odd][:, :, :].bitcast(F32), ACT.Square,
                                     accum_out=lo_squares[:]).then_inc(squares_set, 1)

            with act.Fori(1, KV // 2) as i:
                for s in range(2):
                    head(2 * i + s, s, False)
            square_lows(0, 0, True)
            norm(1)
            act.wait_ge(late_consts_in, 16 * 3)

            def slice_(f, s, pair, first):
                for j in range(2):
                    c = slice(j * HALF, (j + 1) * HALF)
                    wait_apart(act, f_gate, 2 * f + j + 1)
                    if not (first and s == 0):
                        wait_apart(act, hid_set, 2 * f + j - 1)
                    nc.scalar.activation(silu[:, c], bank[j][:, :], ACT.Silu, scale=fsc[:, 0, bass.ds(f, 1)])\
                        .then_inc(silu_set, 1)
                    act.wait_ge(hid_set, 2 * f + j + 1)
                    if not first:
                        act.wait_ge(f_down, 8 * pair - 4 + 4 * j)
                    nc.scalar.activation(hid_hi[:, s, c], hid[:, s, c], ACT.Copy).then_inc(hid_hi_set, 1)

            for s in range(2):
                slice_(s, s, 0, True)
            square_lows(1, 1, False)
            with act.Fori(0, (FT // 2 - 3) // 2) as i:
                for odd in (1, 0):
                    for s in range(2):
                        slice_(4 * i + 4 - 2 * odd + s, s, 2 * i + 2 - odd, False)
                    square_lows(2 * i + 3 - odd, 1 - odd, False)
            for p in (FT // 2 - 2, FT // 2 - 1):
                for s in range(2):
                    slice_(2 * p + s, s, p, False)
                if p < FT // 2 - 1:
                    square_lows(p + 1, (p + 1) % 2, False)
            for s in range(STEPS - 1):
                norm_step(2, s)

            def slot(g, parity, b, first, second, third):
                u = 4 * g + b
                v, w = u - 1, u - 2

                def pT(j):
                    act.wait_ge(pT_done, 3 * w + j + 1)
                    if not (isinstance(w, int) and w == 0):
                        act.wait_ge(pv_done, 2 * w)
                    nc.scalar.activation(pT_hi[:, j, :], bank[2 + (j + 1) % 2][:, :], ACT.Copy).then_inc(pT_hi_set, 1)

                def oT(t):
                    act.wait_ge(pv_done, 2 * w + t + 1)
                    if not (isinstance(w, int) and w == 0):
                        act.wait_ge(l_out, 2 * w)
                    nc.scalar.activation(oT_hi[:, t, :], bank[6 + t][:, :], ACT.Copy).then_inc(oT_hi_set, 1)

                def exps(t):
                    act.wait_ge(neg_max_set, 2 * v + t + 1)
                    for j in range(t * G, (t + 1) * G):
                        c = slice(j * P, (j + 1) * P) if j < G else slice((2 * j - G) * P, (2 * j - G + 2) * P)
                        if j == 0 and third:
                            act.wait_ge(row_inv_set, v)
                        nc.scalar.activation(probs[:, c], probs[:, c], ACT.Exp, bias=neg_max[:, j:j + 1],
                                             scale=SCALE, accum_out=row_sum[:, j:j + 1]).then_inc(exp_set, 1)

                if second:
                    act.wait_ge(k_turned, v + 1)
                    if third:
                        act.wait_ge(score_done, 3 * v)
                    nc.scalar.activation(kT_hi[:], bank[2][:, 0:2 * P], ACT.Copy).then_inc(k_hi_set, 1)
                    nc.scalar.activation(kT[:], bank[2][:, 0:P], ACT.Copy).then_inc(kT_set, 1)
                    act.wait_ge(qT_set, 2 * v + 2)
                    nc.scalar.activation(q1T_hi[:], qT[:, (b - 1) % 2, 1, :, :], ACT.Copy).then_inc(q1_hi_set, 1)
                if third:
                    pT(0)
                    pT(1)
                if first:
                    act.wait_ge(kv_proj, u + 1)
                    if not (isinstance(g, int) and g == 0):
                        act.wait_ge(pv_done, 2 * (u - 3))
                    kv = bank[(3 * b + 1) % 2][:, :].rearrange("p (t a d) -> p t a d", t=2, a=2)
                    act.wait_ge(k_sin, u + 1)
                    nc.scalar.activation(v_hi[:, b, :, :], kv[:, :, 1, :], ACT.Copy).then_inc(v_hi_set, 1)
                    if isinstance(u, int) and u == 0:
                        norm_step(2, STEPS - 1)
                if third:
                    pT(2)
                    oT(0)
                if second:
                    exps(0)
                if third:
                    oT(1)
                if second:
                    exps(1)
                if third and isinstance(u, int) and u - 3 >= 4 * (KV - 1):
                    norm_step(3, u - 3 - 4 * (KV - 1))

            slots(act, slot)
            for s in range(CHUNKS - 1, STEPS):
                norm_step(3, s)
            norm(4)

        @block.vector
        def _(dve):
            def norm_step(k, s):
                def statistics():
                    if k and s < CHUNKS:
                        for t in (2 * s, 2 * s + 1):
                            if k == 1:
                                dve.wait_ge(a_acc, TILES * (KV - 1) + t + 1)
                            if k == 2:
                                dve.wait_ge(odd_scaled if t % 2 else even_scaled, t // 2 + 1)
                            if k == 3:
                                dve.wait_ge(l_acc, TILES * (KV - 1) + t + 1)
                            if k == 4:
                                dve.wait_ge(d_out, t + 1)
                                nc.vector.tensor_tensor(acc[:, t, :], bank[t % 4][:, :], bias_row[:], ALU.add)\
                                    .then_inc(ln_biased, 1)
                                dve.wait_ge(ln_biased, t + 1)
                            nc.vector.bn_stats(stats[:, t, :], acc[:, t, :]).then_inc(ln_stats, 1)
                        for t in (2 * s, 2 * s + 1):
                            dve.wait_ge(ln_stats, (k - 1) * TILES + t + 1)
                            nc.vector.bn_aggr(mean_var[:, t, :], stats[:, t, :]).then_inc(ln_mean, 1)
                        dve.wait_ge(ln_mean, (k - 1) * TILES + 2 * s + 2)
                        nc.vector.tensor_scalar(var_eps[:, 0, 2 * s:2 * s + 2], mean_var[:, 2 * s:2 * s + 2, 1],
                                                LN_EPS, None, ALU.add).then_inc(ln_var, 1)

                def new_statistics():
                    if k < 4 and 0 <= s - 1 < CHUNKS:
                        for t in (2 * s - 2, 2 * s - 1):
                            if k:
                                dve.wait_ge(x_added, (k - 1) * TILES + t + 1)
                            else:
                                dve.wait_ge(x_loaded[t], 16)
                            nc.vector.bn_stats(stats2[:, t, :], x[:, t, :]).then_inc(ln2_stats, 1)
                        for t in (2 * s - 2, 2 * s - 1):
                            dve.wait_ge(ln2_stats, k * TILES + t + 1)
                            nc.vector.bn_aggr(mean_var2[:, t, :], stats2[:, t, :]).then_inc(ln2_mean, 1)
                        dve.wait_ge(ln2_mean, k * TILES + 2 * s)
                        nc.vector.tensor_scalar(var_eps[:, 1, 2 * s - 2:2 * s], mean_var2[:, 2 * s - 2:2 * s, 1],
                                                LN_EPS, None, ALU.add).then_inc(ln2_var, 1)

                def output_shift():
                    if k and s < CHUNKS:
                        dve.wait_ge(ln_rstd, (k - 1) * CHUNKS + s + 1)
                        two = slice(2 * s, 2 * s + 2)
                        nc.vector.scalar_tensor_tensor(out=shift[:, 0, two], in0=mean_var[:, two, 0], scalar=-1.0,
                                                       in1=rstd[:, 0, two], op0=ALU.mult, op1=ALU.mult)\
                            .then_inc(ln_shift, 1)

                def low_parts(s):
                    if k < 4 and 0 <= s - 2 < CHUNKS:
                        for t in (2 * s - 4, 2 * s - 3):
                            dve.wait_ge(xn_hi_set, k * TILES + t + 1)
                            c = slice(t * P, (t + 1) * P)
                            nc.vector.tensor_tensor(xn_lo[:, :, c], bank[4 + t % 4][:, :].rearrange("p (k c) -> p k c", k=KT),
                                                    xn_hi[:, :, c].bitcast(F32), ALU.subtract).then_inc(xn_lo_set, 1)

                def new_shift():
                    if k < 4 and 0 <= s - 1 < CHUNKS:
                        dve.wait_ge(ln2_rstd, k * CHUNKS + s)
                        two = slice(2 * s - 2, 2 * s)
                        nc.vector.scalar_tensor_tensor(out=shift[:, 1, two], in0=mean_var2[:, two, 0], scalar=-1.0,
                                                       in1=rstd[:, 1, two], op0=ALU.mult, op1=ALU.mult)\
                            .then_inc(ln2_shift, 1)

                if k:
                    statistics()
                    new_statistics()
                    output_shift()
                    low_parts(s)
                    new_shift()
                else:
                    new_statistics()
                    low_parts(s - 1)
                    new_shift()

            for s in range(STEPS + 1):
                norm_step(0, s)

            def head(h, s, first, last, lows):
                def mw():
                    dve.wait_ge(mw_hi_set, h + 1)
                    nc.vector.tensor_tensor(mw_lo[:, s, :], bank[2 + s][:, :], mw_hi[:, s, :].bitcast(F32),
                                            ALU.subtract).then_inc(mw_lo_set, 1)

                def acc_tile(t):
                    if t % 4 == 0:
                        dve.wait_ge(rden_set, 2 * h + t // 4 + 1)
                    dve.wait_ge(a_out, 8 * h + t + 1)
                    if not first:
                        dve.wait_ge(a_acc, 8 * h + t - 7)
                    nc.vector.scalar_tensor_tensor(out=acc[:, t, :], in0=bank[4 + t % 4][:, :],
                                                   scalar=rden[:, t:t + 1], in1=acc[:, t, :],
                                                   op0=ALU.mult, op1=ALU.add).then_inc(a_acc, 1)

                def elu(j):
                    c = slice(j * HALF, (j + 1) * HALF)
                    dve.wait_ge(a_relu, 2 * h + j + 1)
                    if not first:
                        dve.wait_ge(sq_lo_set, 2 * h + j - 1)
                        dve.wait_ge(sq_hi_set, 2 * h + j - 1)
                        dve.wait_ge(a_out, 8 * h - 4 + 4 * j)
                    nc.vector.scalar_tensor_tensor(out=sq[:, c], in0=expq[:, c], scalar=1.0, in1=reluq[:, c],
                                                   op0=ALU.min, op1=ALU.add).then_inc(sq_set, 1)

                def elu_low(j):
                    c = slice(j * HALF, (j + 1) * HALF)
                    dve.wait_ge(sq_hi_set, 2 * h + j + 1)
                    nc.vector.tensor_tensor(sq_lo[:, c], sq[:, c], sq_hi[:, c].bitcast(F32), ALU.subtract)\
                        .then_inc(sq_lo_set, 1)
                def denominator(j):
                    dve.wait_ge(den_done, 2 * h + j + 1)
                    if not first:
                        dve.wait_ge(a_acc, 8 * h)
                    nc.vector.tensor_scalar(den_eps[:, 4 * j:4 * j + 4], bank[j][:, 0:4 * DEN_STEP:DEN_STEP],
                                            DEN_EPS, None, ALU.add).then_inc(den_read, 1)
                    dve.wait_ge(den_read, 2 * h + j + 1)
                    nc.vector.reciprocal(rden[:, 4 * j:4 * j + 4], den_eps[:, 4 * j:4 * j + 4]).then_inc(rden_set, 1)

                if not first:
                    mw()
                for n in lows:
                    slice_lo(0, n // 3, 0, n % 3)
                elu(0)
                elu_low(0)
                denominator(0)
                elu(1)
                if first:
                    mw()
                    dve.wait_ge(acc_zero, TILES)
                acc_tile(0)
                acc_tile(1)
                elu_low(1)
                if last:
                    norm_step(1, 0)
                acc_tile(2)
                acc_tile(3)
                denominator(1)
                if last:
                    norm_step(1, 1)
                for t in range(4, TILES):
                    acc_tile(t)
                if last:
                    flag(0, 0)
                    norm_step(1, 2)
                    norm_step(1, 3)

            def slice_lo(p, s, odd, i):
                if i == 0:
                    dve.wait_ge(f_hi_set, 2 * p + s + 1)
                c = slice(i * HID, (i + 1) * HID)
                nc.vector.tensor_tensor(f_lo[odd][:, s, c], f_raw[:, s, c], f_hi[odd][:, s, c].bitcast(F32),
                                        ALU.subtract).then_inc(f_lo_set, 1)

            def flag(p, odd):
                dve.wait_ge(squares_summed, p + 1)
                nc.vector.tensor_scalar(inexact[:, odd:odd + 1], bank[0][0:1, 0:1], 1.0, None, ALU.mult)\
                    .then_inc(inexact_set, 1)

            head(0, 0, True, False, ())
            head(1, 1, False, False, ())
            with dve.Fori(1, KV // 2 - 1) as i:
                for s in range(2):
                    head(2 * i + s, s, False, False, ())
            head(KV - 2, 0, False, False, (0, 1, 2))
            head(KV - 1, 1, False, True, (3, 4, 5))
            for s in range(CHUNKS, STEPS):
                norm_step(1, s)
            dve.wait_ge(late_consts_in, 16 * 3)
            dve.wait_ge(acc_zero, 2 * TILES)

            def pair(p, odd, first, last):
                for s in range(2):
                    f = 2 * p + s
                    for j in range(2):
                        c = slice(j * HALF, (j + 1) * HALF)
                        dve.wait_ge(silu_set, 2 * f + j + 1)
                        dve.wait_ge(f_up, 2 * f + j + 1)
                        if not first:
                            dve.wait_ge(hid_lo_set, 2 * f + j - 3)
                            dve.wait_ge(hid_hi_set, 2 * f + j - 3)
                        nc.vector.scalar_tensor_tensor(out=hid[:, s, c], in0=bank[2 + j][:, :],
                                                       scalar=fsc[:, 1, bass.ds(f, 1)], in1=silu[:, c],
                                                       op0=ALU.mult, op1=ALU.mult).then_inc(hid_set, 1)
                        dve.wait_ge(hid_hi_set, 2 * f + j + 1)
                        nc.vector.tensor_tensor(hid_lo[:, s, c], hid[:, s, c], hid_hi[:, s, c].bitcast(F32),
                                                ALU.subtract).then_inc(hid_lo_set, 1)
                        n = 2 * s + j
                        if n < 3 and not last:
                            for m in (2 * n, 2 * n + 1):
                                slice_lo(p + 1, m // 3, 1 - odd, m % 3)
                for t in range(TILES):
                    dve.wait_ge(f_down, 8 * p + t + 1)
                    if not first:
                        dve.wait_ge(f_acc, 8 * p + t - 7)
                    nc.vector.tensor_tensor(acc[:, t, :], bank[4 + t % 4][:, :], acc[:, t, :], ALU.add)\
                        .then_inc(f_acc, 1)
                    if t == TILES - 3 and not last:
                        flag(p + 1, 1 - odd)
                    if last and t % 2 == 1:
                        dve.wait_ge(down_in, 16)
                        dve.wait_ge(f_acc, 8 * p + t + 1)
                        nc.vector.tensor_tensor(acc[:, t, :], acc[:, t, :], down_row[:], ALU.mult)\
                            .then_inc(odd_scaled, 1)
                        if t >= 3:
                            norm_step(2, t // 2 - 1)

            def qkv_low(g, parity, k):
                dve.wait_ge(qkv_hi_set, KT * g + k + 1)
                c = slice(k * QKV_W // KT, (k + 1) * QKV_W // KT)
                nc.vector.tensor_tensor(qkv_lo[parity][:, c], qkv_raw[parity][:, c],
                                        qkv_hi[parity][:, c].bitcast(F32), ALU.subtract).then_inc(qkv_lo_set, 1)

            PAIRS = FT // 2
            pair(0, 0, True, False)
            for k in range(KT):
                qkv_low(0, 0, k)
            with dve.Fori(0, (PAIRS - 3) // 2) as i:
                pair(2 * i + 1, 1, False, False)
                pair(2 * i + 2, 0, False, False)
            pair(PAIRS - 2, 1, False, False)
            pair(PAIRS - 1, 0, False, True)
            for s in range(CHUNKS - 1, STEPS - 1):
                norm_step(2, s)
            dve.wait_ge(rope_T_in, 16)

            def slot(g, parity, b, first, second, third):
                u = 4 * g + b
                v, w = u - 1, u - 2
                last_group = isinstance(g, int) and g == KV - 1

                def products(j):
                    q = bank[(3 * b + 2 * j) % 2][:, :].rearrange("p (h c) -> p h c", h=G // 2)
                    by_cos = q_by_cos[:].rearrange("p (h c) -> p h c", h=G // 2)
                    by_sin = q_by_sin[:].rearrange("p (h c) -> p h c", h=G // 2)
                    dve.wait_ge(q_proj, 2 * u + j + 1)
                    if second or j:
                        dve.wait_ge(qT_set, 2 * u + j)
                    nc.vector.tensor_tensor(by_cos, q, cos_sin_T[:, 0, None, :].to_broadcast([P, G // 2, 2 * P]),
                                            ALU.mult).then_inc(q_cos, 1)
                    for source, to, done in ((slice(0, P // 2), slice(P // 2, P), q_swapped),
                                             (slice(P // 2, P), slice(0, P // 2), q_sin)):
                        tab = cos_sin_T[source, 1, None, :].to_broadcast([P // 2, G // 2, 2 * P])
                        nc.vector.tensor_tensor(by_sin[to], q[source], tab, ALU.mult).then_inc(done, 1)

                def pT(j):
                    dve.wait_ge(pT_hi_set, 3 * w + j + 1)
                    nc.vector.tensor_tensor(pT_lo[:, j, :], bank[2 + (j + 1) % 2][:, :],
                                            pT_hi[:, j, :].bitcast(F32), ALU.subtract).then_inc(pT_lo_set, 1)

                def oT(t):
                    dve.wait_ge(oT_hi_set, 2 * w + t + 1)
                    nc.vector.tensor_tensor(oT_lo[:, t, :], bank[6 + t][:, :], oT_hi[:, t, :].bitcast(F32),
                                            ALU.subtract).then_inc(oT_lo_set, 1)

                def mask_max(j):
                    sbank = 4 + (3 * (b - 1) + (0 if j < G else 1 + (j - G) // 2)) % 2
                    wait_apart(dve, score_done, 3 * v + (1 if j < G else 2 + (j - G) // 2))
                    if j < G:
                        c, sc, m = slice(j * P, (j + 1) * P), slice(j * P, (j + 1) * P), masks[:, P:2 * P]
                    else:
                        c = slice((2 * j - G) * P, (2 * j - G + 2) * P)
                        sc, m = slice((j % 2) * 2 * P, (j % 2 + 1) * 2 * P), masks[:, :]
                    nc.vector.tensor_tensor_reduce(out=probs[:, c], in0=bank[sbank][:, sc], in1=m, scale=1.0,
                                                   scalar=LOWEST, op0=ALU.add, op1=ALU.max,
                                                   accum_out=row_max[:, j:j + 1]).then_inc(masked_set, 1)

                def negate(t):
                    dve.wait_ge(masked_set, 8 * v + G * (t + 1))
                    if third:
                        dve.wait_ge(exp_set, 8 * v)
                    nc.vector.tensor_scalar(neg_max[:, t * G:(t + 1) * G], row_max[:, t * G:(t + 1) * G],
                                            -SCALE, None, ALU.mult).then_inc(neg_max_set, 1)

                def add(t):
                    if isinstance(w, int) and w == 0:
                        dve.wait_ge(acc_zero, 3 * TILES)
                    dve.wait_ge(l_out, 2 * w + t + 1)
                    r = 2 * ((b - 2) % 4) + t
                    if not (isinstance(w, int) and w == 0):
                        dve.wait_ge(l_acc, 2 * w)
                    nc.vector.tensor_tensor(acc[:, r, :], bank[6 + t][:, :], acc[:, r, :], ALU.add)\
                        .then_inc(l_acc, 1)

                def weight_lows():
                    if first and not last_group:
                        qkv_low(g + 1, 1 - parity, b)
                    if first and b < 2:
                        for h in (2 * b, 2 * b + 1):
                            dve.wait_ge(lwo_hi_set, G * g + h + 1)
                            c = slice(h * HID, (h + 1) * HID)
                            nc.vector.tensor_tensor(lwo_lo[parity][:, c], lwo_raw[parity][:, c],
                                                    lwo_hi[parity][:, c].bitcast(F32), ALU.subtract)\
                                .then_inc(lwo_lo_set, 1)

                start = isinstance(u, int) and u == 0
                if first:
                    products(0)
                if second:
                    dve.wait_ge(k_hi_set, v + 1)
                    dve.wait_ge(kT_set, v + 1)
                    if third:
                        dve.wait_ge(score_done, 3 * v)
                    nc.vector.tensor_tensor(kT_lo[:], bank[2][:, 0:2 * P], kT_hi[:].bitcast(F32), ALU.subtract)\
                        .then_inc(k_lo_set, 1)
                    dve.wait_ge(q1_hi_set, v + 1)
                    nc.vector.tensor_tensor(q1T_lo[:], qT[:, (b - 1) % 2, 1, :, :], q1T_hi[:].bitcast(F32),
                                            ALU.subtract).then_inc(q1_lo_set, 1)
                if third:
                    pT(0)
                if first:
                    kv = bank[(3 * b + 1) % 2][:, :].rearrange("p (t c a f) -> p t c a f", t=2, c=2, a=2)
                    dve.wait_ge(kv_proj, u + 1)
                    if second:
                        dve.wait_ge(k_rotated_set, 2 * u)
                    for a, dst, done in ((0, k_by_cos, k_cos), (1, k_by_sin, k_sin)):
                        tab = cos_sin[:, a, :, None, :].to_broadcast([P, 2, 2, D // 2])
                        nc.vector.tensor_tensor(dst[:], kv[:, :, 0, :, :], tab, ALU.mult).then_inc(done, 1)
                if third:
                    pT(1)
                if first:
                    dve.wait_ge(v_hi_set, u + 1)
                    kv = bank[(3 * b + 1) % 2][:, :].rearrange("p (t a d) -> p t a d", t=2, a=2)
                    nc.vector.tensor_tensor(v_lo[:, b, :, :], kv[:, :, 1, :], v_hi[:, b, :, :].bitcast(F32),
                                            ALU.subtract).then_inc(v_lo_set, 1)
                if third:
                    pT(2)
                if first:
                    if start:
                        norm_step(2, STEPS - 1)
                        weight_lows()
                    products(1)
                if second:
                    if third:
                        dve.wait_ge(pT_done, 3 * w + 3)
                    for j in range(G):
                        mask_max(j)
                    negate(0)
                if third:
                    oT(0)
                if second:
                    for j in (4, 5):
                        mask_max(j)
                if third:
                    oT(1)
                if second:
                    for j in (6, 7):
                        mask_max(j)
                    negate(1)
                if not start:
                    weight_lows()
                norming = third and isinstance(u, int) and u - 3 >= 4 * (KV - 1)
                if norming:
                    norm_step(3, u - 3 - 4 * (KV - 1))
                elif third:
                    add(0)
                if second:
                    dve.wait_ge(exp_set, 8 * v + 8)
                    if third:
                        dve.wait_ge(probs_set, 8 * v)
                    nc.vector.reciprocal(row_inv[:], row_sum[:]).then_inc(row_inv_set, 1)
                if norming:
                    add(0)
                if third:
                    add(1)
            slots(dve, slot)
            def add_odd(s):
                t = 2 * s + 1
                dve.wait_ge(ln_out, 3 * TILES + t + 1)
                nc.vector.tensor_tensor(x[:, t, :], x[:, t, :], acc[:, t, :], ALU.add).then_inc(odd_added, 1)

            for s in range(CHUNKS - 1, STEPS - 1):
                norm_step(3, s)
            dve.wait_ge(bias_in, 16)
            norm_step(4, 0)
            norm_step(3, STEPS - 1)
            for s in range(1, CHUNKS):
                norm_step(4, s)
                add_odd(s - 1)
            add_odd(CHUNKS - 1)

        @block.tensor
        def _(pe):
            def product(o, lhs, rhs, start, stop):
                nc.tensor.matmul(o, lhs[0], rhs[0], start=start, stop=False)
                nc.tensor.matmul(o, lhs[0], rhs[1], start=False, stop=False)
                return nc.tensor.matmul(o, lhs[1], rhs[0], start=False, stop=stop)

            def turn(k, tiles):
                for t in tiles:
                    pe.wait_ge(xn_ready, k * TILES + t + 1)
                    if t >= 4:
                        pe.wait_ge(xn_lo_set, k * TILES + t - 3)
                    elif k == 1:
                        pe.wait_ge(a_acc, TILES * (KV - 1) + t + 5)
                    elif k == 2:
                        pe.wait_ge(f_acc, TILES * (FT // 2 - 1) + t + 5)
                    elif k == 3 and t < 2:
                        pe.wait_ge(masked_set, TILES * 4 * KV)
                    elif k == 3:
                        pe.wait_ge(l_acc, TILES * KV)
                    for i in range(KT):
                        last = nc.tensor.transpose(bank[4 + t % 4][:, i * P:(i + 1) * P],
                                                   acc[:, t, i * P:(i + 1) * P], ident[:])
                    last.then_inc(xn_turned, 1)

            def halves(j):
                return slice(j * HALF, (j + 1) * HALF)

            def a_project(h, s, j, first):
                if first:
                    pe.wait_ge(xn_lo_set, 4 * j + 4)
                else:
                    pe.wait_ge(den_read, 2 * h + j - 1)
                for k in range(KT):
                    w = slice(k * D, (k + 1) * D)
                    last = product(bank[j][:, :], (a_hi[:, s, w], a_lo[:, s, w]),
                                   (xn_hi[:, k, halves(j)], xn_lo[:, k, halves(j)]), k == 0, k == KT - 1)
                last.then_inc(a_proj, 1)

            def m_times_wo(h, s, used):
                m = slice(KT * D, A_W)
                pe.wait_ge(wos_lo_set, h + 1)
                if used:
                    pe.wait_ge(mw_lo_set, h - 1)
                product(bank[2 + s][:, :], (a_hi[:, s, m], a_lo[:, s, m]), (wos_hi[:, s, :], wos_lo[:, s, :]),
                        True, True).then_inc(mw_done, 1)

            def head(h, s, first, late, last):
                if not first:
                    for j in range(2):
                        a_project(h, s, j, False)
                    if not (last or late):
                        pe.wait_ge(a_lo_set, h + 2)
                        m_times_wo(h + 1, 1 - s, True)
                for j in range(2):
                    pe.wait_ge(sq_set, 2 * h + j + 1)
                    for t in range(4 * j, 4 * j + 4):
                        o = (t % 4) * DEN_STEP
                        last = nc.tensor.matmul(bank[j][:, o:o + P], sq[:, t * P:(t + 1) * P],
                                                z_rep[:, bass.ds(h, 1), :].rearrange("p a c -> p (a c)"),
                                                start=True, stop=True)
                    last.then_inc(den_done, 1)
                    pe.wait_ge(sq_lo_set, 2 * h + j + 1)
                    pe.wait_ge(mw_lo_set, h + 1)
                    for t in range(4 * j, 4 * j + 4):
                        if not (first and t < 4):
                            pe.wait_ge(a_acc, 8 * h + t - 3)
                        c = slice(t * P, (t + 1) * P)
                        product(bank[4 + t % 4][:, :], (sq_hi[:, c], sq_lo[:, c]), (mw_hi[:, s, :], mw_lo[:, s, :]),
                                True, True).then_inc(a_out, 1)

            pe.wait_ge(early_consts_in, 16 * 3)
            turn(0, range(6))
            pe.wait_ge(a_lo_set, 1)
            a_project(0, 0, 0, True)
            turn(0, range(6, TILES))
            a_project(0, 0, 1, True)
            m_times_wo(0, 0, False)
            pe.wait_ge(z_set, KV)
            head(0, 0, True, True, False)
            pe.wait_ge(a_lo_set, 2)
            m_times_wo(1, 1, False)
            head(1, 1, False, True, False)
            pe.wait_ge(a_lo_set, 3)
            m_times_wo(2, 0, True)
            with pe.Fori(1, KV // 2 - 1) as i:
                for s in range(2):
                    head(2 * i + s, s, False, False, False)
            head(KV - 2, 0, False, False, False)
            head(KV - 1, 1, False, False, True)

            def sum_squares(p):
                pe.wait_ge(squares_set, p + 1)
                nc.tensor.matmul(bank[0][0:1, 0:1], lo_squares[:], ones[:], start=True, stop=True)\
                    .then_inc(squares_summed, 1)

            def weight_first(exact, o, lhs, rhs, start, stop):
                if not exact:
                    return product(o, lhs, rhs, start, stop)
                nc.tensor.matmul(o, lhs[0], rhs[0], start=start, stop=False)
                return nc.tensor.matmul(o, lhs[0], rhs[1], start=False, stop=stop)

            def weight_last(exact, o, lhs, rhs, start, stop):
                if not exact:
                    return product(o, lhs, rhs, start, stop)
                nc.tensor.matmul(o, lhs[0], rhs[0], start=start, stop=False)
                return nc.tensor.matmul(o, lhs[1], rhs[0], start=False, stop=stop)

            def gate_or_up(exact, f, s, odd, j, a, first):
                if not first:
                    pe.wait_ge(silu_set if a == 0 else hid_set, 2 * f + j - 1)
                for k in range(KT):
                    w = slice((a * KT + k) * P, (a * KT + k + 1) * P)
                    last = weight_first(exact, bank[2 * a + j][:, :], (f_hi[odd][:, s, w], f_lo[odd][:, s, w]),
                                        (xn_hi[:, k, halves(j)], xn_lo[:, k, halves(j)]), k == 0, k == KT - 1)
                last.then_inc(f_up if a else f_gate, 1)

            def pair(exact, p, odd, first, last):
                if first:
                    pe.wait_ge(xn_lo_set, TILES + 4)
                    gate_or_up(exact, 0, 0, 0, 0, 0, True)
                    turn(1, range(4, 6))
                    gate_or_up(exact, 0, 0, 0, 0, 1, True)
                    turn(1, range(6, TILES))
                    pe.wait_ge(xn_lo_set, 2 * TILES)
                    for a in range(2):
                        gate_or_up(exact, 0, 0, 0, 1, a, True)
                for s in range(2):
                    if not (first and s == 0):
                        for j in range(2):
                            for a in range(2):
                                gate_or_up(exact, 2 * p + s, s, odd, j, a, False)
                d = slice(2 * KT * P, F_W)
                for t in range(TILES):
                    if t % 4 == 0:
                        pe.wait_ge(hid_lo_set, 4 * p + 3 + t // 4)
                    if not (first and t < 4):
                        pe.wait_ge(f_acc, 8 * p + t - 3)
                    c = slice(t * P, (t + 1) * P)
                    for s in range(2):
                        done = weight_last(exact, bank[4 + t % 4][:, :], (hid_hi[:, s, c], hid_lo[:, s, c]),
                                           (f_hi[odd][:, s, d], f_lo[odd][:, s, d]), s == 0, s == 1)
                    done.then_inc(f_down, 1)
                    if t == TILES - 4 and not last:
                        pe.wait_ge(silu_set, 4 * p + 4)
                        sum_squares(p + 1)

            def either(p, odd, first, last):
                wait_apart(pe, f_lo_set, 6 * (p + 1))
                wait_apart(pe, inexact_set, p + 1)
                low = pe.value_load(inexact[0:1, odd:odd + 1].bitcast(I32))
                with pe.If(low == 0):
                    pair(True, p, odd, first, last)
                with pe.Else():
                    pair(False, p, odd, first, last)

            pe.wait_ge(den_read, 2 * KV)
            sum_squares(0)
            turn(1, range(4))
            either(0, 0, True, False)
            with pe.Fori(0, (FT // 2 - 3) // 2) as i:
                either(2 * i + 1, 1, False, False)
                either(2 * i + 2, 0, False, False)
            either(FT // 2 - 2, 1, False, False)
            either(FT // 2 - 1, 0, False, True)

            def slot(g, parity, b, first, second, third):
                u = 4 * g + b
                v, w = u - 1, u - 2
                start = isinstance(u, int) and u == 0
                early = isinstance(u, int) and u < 3

                def project_q(j):
                    c = slice(2 * b * P, (2 * b + 2) * P)
                    if isinstance(g, int) and g == 0:
                        pe.wait_ge(xn_lo_set, 2 * TILES + 2 * b + 2)
                    for h in (0, 1):
                        for k in range(KT):
                            base = k * QKV_W // KT + (2 * j + h) * D
                            ws = slice(base, base + D)
                            last = product(bank[(3 * b + 2 * j) % 2][:, h * 2 * P:(h + 1) * 2 * P],
                                           (qkv_hi[parity][:, ws], qkv_lo[parity][:, ws]),
                                           (xn_hi[:, k, c], xn_lo[:, k, c]), k == 0, k == KT - 1)
                    last.then_inc(q_proj, 1)

                def project_kv(t):
                    r = 2 * b + t
                    c = slice(r * P, (r + 1) * P)
                    for k in range(KT):
                        base = k * QKV_W // KT
                        ws = slice(base + G * D, base + (G + 2) * D)
                        last = product(bank[(3 * b + 1) % 2][:, t * 2 * D:(t + 1) * 2 * D],
                                       (xn_hi[:, k, c], xn_lo[:, k, c]), (qkv_hi[parity][:, ws], qkv_lo[parity][:, ws]),
                                       k == 0, k == KT - 1)
                    return last

                def turn_k():
                    pe.wait_ge(k_rotated_set, 2 * u)
                    if third and not early:
                        pe.wait_ge(pT_lo_set, 3 * w - 1)
                    for t in range(2):
                        last = nc.tensor.transpose(bank[2][:, t * P:(t + 1) * P],
                                                   k_rotated[:, t, :, :].rearrange("p a f -> p (a f)"), ident[:])
                    last.then_inc(k_turned, 1)

                def turn_p(j):
                    if j == 0:
                        pe.wait_ge(probs_set, 8 * w + 8)
                    if second and j == 1:
                        pe.wait_ge(k_lo_set, v + 1)
                    elif j < 2 and not (isinstance(w, int) and w == 0):
                        pe.wait_ge(pT_lo_set, 3 * w)
                    if j == 2:
                        pe.wait_ge(pT_lo_set, 3 * w + 1)
                    for h in range(G):
                        o = h * P if j == 0 else (G + 2 * h + j - 1) * P
                        last = nc.tensor.transpose(bank[2 + (j + 1) % 2][:, h * P:(h + 1) * P],
                                                   probs[:, o:o + P], ident[:])
                    last.then_inc(pT_done, 1)

                def times_v(t):
                    s = (b - 2) % 4
                    if t == 0:
                        pe.wait_ge(v_lo_set, w + 1)
                    pe.wait_ge(pT_lo_set, 3 * w + 1 + 2 * t)
                    if not (isinstance(w, int) and w == 0):
                        pe.wait_ge(l_acc, 2 * w - 1 + t)
                    o = bank[6 + t][:, :]
                    if t == 0:
                        last = product(o, (v_hi[:, s, 0, :], v_lo[:, s, 0, :]), (pT_hi[:, 0, :], pT_lo[:, 0, :]),
                                       True, True)
                    else:
                        product(o, (v_hi[:, s, 0, :], v_lo[:, s, 0, :]), (pT_hi[:, 1, :], pT_lo[:, 1, :]),
                                True, False)
                        last = product(o, (v_hi[:, s, 1, :], v_lo[:, s, 1, :]), (pT_hi[:, 2, :], pT_lo[:, 2, :]),
                                       False, True)
                    last.then_inc(pv_done, 1)

                def scores(j):
                    o = bank[4 + (3 * (b - 1) + j) % 2]
                    if j == 0:
                        pe.wait_ge(kT_set, v + 1)
                        pe.wait_ge(qT_set, 2 * v + 2)
                    if j == 1:
                        pe.wait_ge(q1_lo_set, v + 1)
                        if isinstance(v, int) and v == 0:
                            pe.wait_ge(xn_lo_set, 3 * TILES)
                    if j == 2:
                        pe.wait_ge(masked_set, 8 * v + G)
                    elif third:
                        pe.wait_ge(masked_set, 8 * w + G + 2 * (j + 1))
                    if j == 0:
                        for h in range(G):
                            last = nc.tensor.matmul(o[:, h * P:(h + 1) * P], qT[:, (b - 1) % 2, 0, h, :],
                                                    kT[:], start=True, stop=True)
                    else:
                        for i in range(2):
                            h = 2 * (j - 1) + i
                            last = product(o[:, i * 2 * P:(i + 1) * 2 * P], (q1T_hi[:, h, :], q1T_lo[:, h, :]),
                                           (kT_hi[:], kT_lo[:]), True, True)
                    last.then_inc(score_done, 1)

                if first:
                    if b == 0:
                        pe.wait_ge(qkv_lo_set, KT * (g + 1))
                    if second:
                        pe.wait_ge(k_sin, u)
                        pe.wait_ge(v_lo_set, u)
                    project_q(0)
                if second:
                    turn_k()
                if first:
                    if second:
                        pe.wait_ge(q_sin, 2 * u)
                    if start:
                        turn(2, range(4, 6))
                    project_kv(0)
                if third:
                    turn_p(0)
                if first:
                    project_kv(1).then_inc(kv_proj, 1)
                    if start:
                        turn(2, range(6, TILES))
                if third:
                    turn_p(1)
                    turn_p(2)
                if first:
                    pe.wait_ge(q_sin, 2 * u + 1)
                    project_q(1)
                if second:
                    scores(0)
                if third:
                    times_v(0)
                if second:
                    scores(1)
                if third:
                    times_v(1)
                if second:
                    scores(2)
                if third:
                    o_set = parity if b >= 2 else 1 - parity
                    if b == 2:
                        pe.wait_ge(lwo_lo_set, G * (g + 1))
                    for t in range(2):
                        pe.wait_ge(oT_lo_set, 2 * w + t + 1)
                        for h in range(G):
                            c, n = slice(h * P, (h + 1) * P), slice(h * HID, (h + 1) * HID)
                            last = product(bank[6 + t][:, :], (oT_hi[:, t, c], oT_lo[:, t, c]),
                                           (lwo_hi[o_set][:, n], lwo_lo[o_set][:, n]), h == 0, h == G - 1)
                        last.then_inc(l_out, 1)
                if isinstance(u, int) and u == 4 * KV:
                    turn(3, range(2))

            turn(2, range(4))
            slots(pe, slot)

            def last_layer(t):
                pe.wait_ge(xn_lo_set, 3 * TILES + t + 1)
                if t >= 4:
                    pe.wait_ge(ln_biased, t - 3)
                c = slice(t * P, (t + 1) * P)
                for k in range(KT):
                    last = product(bank[t % 4][:, :], (xn_hi[:, k, c], xn_lo[:, k, c]), (d_hi[:, k, :], d_lo[:, k, :]),
                                   k == 0, k == KT - 1)
                last.then_inc(d_out, 1)

            pe.wait_ge(d_step, 5 * KT)
            last_layer(0)
            turn(3, range(2, 4))
            last_layer(1)
            turn(3, range(4, 6))
            last_layer(2)
            last_layer(3)
            turn(3, range(6, TILES))
            for t in range(4, TILES):
                last_layer(t)


def kernel(**inputs):
    import numpy as np
    import concourse.bacc as bacc
    from concourse.bass_utils import run_bass_kernel_spmd as run

    a = {name: np.asarray(value) for name, value in inputs.items()}

    def by_partition(w, tiles):
        return w.reshape(tiles, P, -1).transpose(1, 0, 2).reshape(P, -1)

    wq = a["L0_attn_Wq"].reshape(KV, G, D, HID)[:, 0]
    a_w = np.stack([np.concatenate([by_partition(wq[h].T, KT), a["L0_attn_M"][h].T], 1) for h in range(KV)])
    a_wo = a["L0_attn_Wo"].T.reshape(KV, G, D, HID).transpose(0, 2, 1, 3).reshape(KV, D, G * HID)
    a_bq = a["L0_attn_bq"].reshape(KV, G, D)[:, 0].T
    gate, up, down = (a[f"L0_ffn_{n}_t"] for n in ("gate", "up", "down"))
    f_w = np.stack([np.concatenate([by_partition(gate[f:f + P].T, KT), by_partition(up[f:f + P].T, KT),
                                    down[:, f:f + P].T], 1) for f in range(0, FF, P)])
    f_scale = np.concatenate([a["L0_ffn_gate_s"].reshape(FT, P).T, a["L0_ffn_up_s"].reshape(FT, P).T], 1)
    wq, wk, wv = (a[f"L1_attn_w{n}"].reshape(KT, P, KV, -1) for n in "qkv")
    l_qkv = np.concatenate([wq, wk, wv], 3).transpose(2, 1, 0, 3).reshape(KV, P, QKV_W)
    l_wo = a["L1_attn_wo"].reshape(KV, G, D, HID).transpose(0, 2, 1, 3).reshape(KV, D, WO_W)
    size = HID // a["L1_ffn_zp"].shape[1]
    half = D // 2
    freq = np.float32(10000.0) ** (-np.arange(half, dtype=np.float32) / np.float32(half))
    angle = np.arange(2 * P, dtype=np.float32)[:, None] * freq[None, :]
    rope = np.stack([np.cos(angle), np.sin(angle)]).reshape(2, 2, P, half).transpose(2, 0, 1, 3).reshape(P, -1)
    cos_T, sin_T = np.cos(angle).T, np.sin(angle).T
    rope_turned = np.concatenate([np.tile(cos_T, (2, 1)), np.concatenate([sin_T, -sin_T])], 1)
    i, j = np.arange(P)[:, None], np.arange(P)[None, :]
    low = np.float32(LOWEST)
    mask = np.concatenate([np.where(j > i, np.float32(0), low), np.where(j <= i, np.float32(0), low)], 1)

    arrays = {
        "x_in": a["L0_attn_hidden_states"].reshape(T, HID),
        "a_w": a_w, "a_wo": a_wo, "a_z": a["L0_attn_z"].T, "a_bq": a_bq,
        "f_w": f_w, "f_scale": f_scale, "down_s": np.broadcast_to(a["L0_ffn_down_s"], (P, HID)),
        "l_qkv": l_qkv, "l_wo": l_wo,
        "d_q": a["L1_ffn_weight_q"].T, "d_zp": np.repeat(a["L1_ffn_zp"].T, size, 0),
        "d_scale": np.repeat(a["L1_ffn_scale"].T, size, 0), "d_bias": np.broadcast_to(a["L1_ffn_bias"], (P, HID)),
        "rope": rope.astype(np.float32), "rope_turned": rope_turned.astype(np.float32),
        "mask": mask.astype(np.float32), "ident_in": np.eye(P, dtype=np.float32),
    }
    arrays = {name: np.ascontiguousarray(value) for name, value in arrays.items()}
    nc = bacc.Bacc("TRN2", target_bir_lowering=False, num_devices=1)
    args = {name: nc.dram_tensor(name, value.shape, mybir.dt.from_np(value.dtype), kind="ExternalInput").ap()
            for name, value in arrays.items()}
    result = nc.dram_tensor("result", (T, HID), F32, kind="ExternalOutput").ap()
    build(nc, out=result, **args)
    r = run(nc, [arrays], core_ids=[0])
    return r.results[0]["result"].reshape(4, 256, HID)
```
